# Optimizing a Trainium2 kernel written in Bass

```python
import numpy as np
import jax
import jax.numpy as jnp

def _softmax(x, axis=-1):
    return jax.nn.softmax(x, axis=axis)

def _gelu(x):
    return jax.nn.gelu(x, approximate=True)

def _silu(x):
    return jax.nn.silu(x)

def _sigmoid(x):
    return jax.nn.sigmoid(x)

def _layernorm(x, axis=-1, eps=1e-05):
    m = jnp.mean(x, axis=axis, keepdims=True)
    v = jnp.var(x, axis=axis, keepdims=True)
    return (x - m) / jnp.sqrt(v + eps)

def _scatter_add(tgt, idx, src, axis=0):
    return tgt.at[idx].add(src)

def _segment_sum(src, seg, n):
    return jax.ops.segment_sum(src, seg, n)
kernel_name = 'mk_audio_tower_d2_tok_audfeat512_r4_1e6d0c'

def setup_inputs(seed: int=0):
    np.random.seed(seed)
    _w = jnp.asarray

    def _rec_inputs():
        import jax
        import jax.numpy as jnp
        _rk = jax.random.key(seed)
        x = -7.10856e-05 + 0.999911 * jax.random.normal(jax.random.fold_in(_rk, 1), (8, 750, 128), jnp.float32)
        return x
    x = _rec_inputs()

    def _L0_tok_setup():
        import jax, jax.numpy as jnp
        import numpy as np
        EPS = 1e-05

        def conv1d(x, w, b, stride=1, padding=0):
            out = jax.lax.conv_general_dilated(x, w, window_strides=(stride,), padding=[(padding, padding)], dimension_numbers=('NCH', 'OIH', 'NCH'))
            return out + b[None, :, None]

        def layer_norm(x, g, b):
            mu = jnp.mean(x, axis=-1, keepdims=True)
            var = jnp.mean(jnp.square(x - mu), axis=-1, keepdims=True)
            return (x - mu) * jax.lax.rsqrt(var + EPS) * g + b
        key = jax.random.key(seed)
        ks = jax.random.split(key, 16)
        B, T, H = (64, 512, 128)
        Bn = H // 2
        s = 0.02
        return {'x': jax.random.normal(ks[0], (B, T, H), dtype=jnp.float32), 'w_compress': jax.random.normal(ks[1], (Bn, H, 1), dtype=jnp.float32) * s, 'b_compress': jnp.zeros((Bn,), dtype=jnp.float32), 'w_main': jax.random.normal(ks[2], (Bn, Bn, 3), dtype=jnp.float32) * s, 'b_main': jnp.zeros((Bn,), dtype=jnp.float32), 'w_expand': jax.random.normal(ks[3], (H, Bn, 1), dtype=jnp.float32) * s, 'b_expand': jnp.zeros((H,), dtype=jnp.float32), 'g_conv_norm': jnp.ones((H,), dtype=jnp.float32), 'b_conv_norm': jnp.zeros((H,), dtype=jnp.float32), 'w_ff1': jax.random.normal(ks[4], (Bn, H), dtype=jnp.float32) * s, 'b_ff1': jnp.zeros((Bn,), dtype=jnp.float32), 'w_ff2': jax.random.normal(ks[5], (H, Bn), dtype=jnp.float32) * s, 'b_ff2': jnp.zeros((H,), dtype=jnp.float32), 'g_ff_norm': jnp.ones((H,), dtype=jnp.float32), 'b_ff_norm': jnp.zeros((H,), dtype=jnp.float32)}
    _L0_tok_all = _L0_tok_setup()
    _L0_tok_in = {k: v for k, v in _L0_tok_all.items() if k in ('w_compress', 'b_compress', 'w_main', 'b_main', 'w_expand', 'b_expand', 'g_conv_norm', 'b_conv_norm', 'w_ff1', 'b_ff1', 'w_ff2', 'b_ff2', 'g_ff_norm', 'b_ff_norm')}
    del _L0_tok_all

    def _L0_attn_setup():
        import jax, jax.numpy as jnp
        import numpy as np
        N_HEADS = 8
        N_GROUPS = 4
        B, T, D = (16, 256, 128)
        GH = D // N_HEADS * N_GROUPS

        def _rope_tables(t, d):
            i = np.arange(d // 2, dtype=np.float64)
            theta = 10000.0 ** (-(2.0 * (i - 1.0))) / d
            ang = np.arange(t, dtype=np.float64)[:, None] * theta[None, :]
            return (jnp.asarray(np.cos(ang), jnp.float32), jnp.asarray(np.sin(ang), jnp.float32))

        def _apply_rope(x, cos, sin):
            xe, xo = (x[..., 0::2], x[..., 1::2])
            oe = xe * cos + xo * sin
            oo = -xe * sin + xo * cos
            return jnp.stack([oe, oo], axis=-1).reshape(x.shape)
        key = jax.random.key(seed)
        k1, k2, k3, k4 = jax.random.split(key, 4)
        x = jax.random.normal(k1, (B, T, D), dtype=jnp.float32)
        Wq = jax.random.normal(k2, (D, D), dtype=jnp.float32) * D ** (-0.5)
        Wk = jax.random.normal(k3, (D, GH), dtype=jnp.float32) * D ** (-0.5)
        Wv = jax.random.normal(k4, (D, GH), dtype=jnp.float32) * D ** (-0.5)
        return {'x': x, 'Wq': Wq, 'Wk': Wk, 'Wv': Wv}
    _L0_attn_all = _L0_attn_setup()
    _L0_attn_in = {k: v for k, v in _L0_attn_all.items() if k in ('Wq', 'Wk', 'Wv')}
    del _L0_attn_all

    def _L0_ffn_setup():
        import jax, jax.numpy as jnp
        import numpy as np
        NUM_EXPERTS = 8
        TOP_K = 2
        key = jax.random.key(seed)
        k0, k1, k2, k3, k4 = jax.random.split(key, 5)
        sl, bs, hs, ffn = (512, 2, 128, 512)
        T = sl * bs
        x = jax.random.normal(k0, (sl, bs, hs), jnp.float32)
        expert_weights = jax.random.uniform(k1, (T, TOP_K), jnp.float32)
        expert_indices = jax.random.randint(k2, (T, TOP_K), 0, NUM_EXPERTS)
        w1 = jax.random.normal(k3, (NUM_EXPERTS, hs, ffn), jnp.float32) * hs ** (-0.5)
        w2 = jax.random.normal(k4, (NUM_EXPERTS, ffn, hs), jnp.float32) * ffn ** (-0.5)
        return dict(x=x, expert_weights=expert_weights, expert_indices=expert_indices, w1=w1, w2=w2)
    _L0_ffn_all = _L0_ffn_setup()
    _L0_ffn_in = {k: v for k, v in _L0_ffn_all.items() if k in ('expert_weights', 'expert_indices', 'w1', 'w2')}
    del _L0_ffn_all

    def _L1_attn_setup():
        import jax, jax.numpy as jnp
        import numpy as np
        B, N, D_IN, D_HID, D_OUT = (8, 512, 128, 128, 128)
        key = jax.random.key(seed)
        k1, k2, k3, k4 = jax.random.split(key, 4)
        x = jax.random.normal(k1, (B, N, D_IN), dtype=jnp.float32)
        s_in = 1.0 / np.sqrt(D_IN)
        s_hid = 1.0 / np.sqrt(D_HID)
        Wq = jax.random.uniform(k2, (D_HID, D_IN), minval=-s_in, maxval=s_in, dtype=jnp.float32)
        Wk = jax.random.uniform(k3, (D_HID, D_IN), minval=-s_in, maxval=s_in, dtype=jnp.float32)
        Wv = jax.random.uniform(k4, (D_OUT, D_HID), minval=-s_hid, maxval=s_hid, dtype=jnp.float32)
        return {'x': x, 'Wq': Wq, 'Wk': Wk, 'Wv': Wv}
    _L1_attn_all = _L1_attn_setup()
    _L1_attn_in = {k: v for k, v in _L1_attn_all.items() if k in ('Wq', 'Wk', 'Wv')}
    del _L1_attn_all

    def _L1_ffn_setup():
        import jax, jax.numpy as jnp
        import numpy as np
        G = 4
        EPG = 4
        E = 16
        KG = 2
        K = 2
        GTP = 0.9
        TP = 0.9
        SCALE = 1.0 / float(np.sqrt(G))

        def _routing_weights(xf, Wr, br, Wgate, bgate):
            N = xf.shape[0]
            gp = jax.nn.softmax(xf @ Wr + br, axis=-1)
            order = jnp.argsort(-gp, axis=-1)
            sp_k = jnp.take_along_axis(gp, order, axis=-1)[:, :KG]
            idx_k = order[:, :KG]
            act = jnp.cumsum(sp_k, axis=-1) <= GTP
            act = act.at[:, 0].set(True)
            mp = sp_k * act
            rn = mp / (jnp.sum(mp, axis=-1, keepdims=True) + 1e-09)
            w_group = jnp.zeros((N, G), xf.dtype).at[jnp.arange(N)[:, None], idx_k].set(rn)
            ep = jax.nn.softmax(jnp.einsum('nd,gde->nge', xf, Wgate) + bgate, axis=-1)
            eorder = jnp.argsort(-ep, axis=-1)
            esp = jnp.take_along_axis(ep, eorder, axis=-1)[:, :, :K]
            eidx = eorder[:, :, :K]
            eact = jnp.cumsum(esp, axis=-1) <= TP
            eact = eact.at[:, :, 0].set(True)
            emp = esp * eact
            ern = emp / (jnp.sum(emp, axis=-1, keepdims=True) + 1e-09)
            w_exp = jnp.zeros((N, G, EPG), xf.dtype).at[jnp.arange(N)[:, None, None], jnp.arange(G)[None, :, None], eidx].set(ern)
            return (w_group[:, :, None] * w_exp * SCALE).reshape(N, E)
        key = jax.random.key(seed)
        ks = jax.random.split(key, 6)
        B, T, D, H = (2, 256, 128, 512)
        x = jax.random.normal(ks[0], (B, T, D), jnp.float32)
        Wr = jax.random.normal(ks[1], (D, G), jnp.float32) * 0.02
        br = jnp.zeros((G,), jnp.float32)
        Wgate = jax.random.normal(ks[2], (G, D, EPG), jnp.float32) * 0.02
        bgate = jnp.zeros((G, EPG), jnp.float32)
        W1 = jax.random.normal(ks[3], (E, D, H), jnp.float32) * 0.02
        W3 = jax.random.normal(ks[4], (E, D, H), jnp.float32) * 0.02
        W2 = jax.random.normal(ks[5], (E, H, D), jnp.float32) * 0.02
        return {'x': x, 'Wr': Wr, 'br': br, 'Wgate': Wgate, 'bgate': bgate, 'W1': W1, 'W3': W3, 'W2': W2}
    _L1_ffn_all = _L1_ffn_setup()
    _L1_ffn_in = {k: v for k, v in _L1_ffn_all.items() if k in ('Wr', 'br', 'Wgate', 'bgate', 'W1', 'W3', 'W2')}
    del _L1_ffn_all
    return {'x': x, 'L0_tok_w_compress': _L0_tok_in['w_compress'], 'L0_tok_b_compress': _L0_tok_in['b_compress'], 'L0_tok_w_main': _L0_tok_in['w_main'], 'L0_tok_b_main': _L0_tok_in['b_main'], 'L0_tok_w_expand': _L0_tok_in['w_expand'], 'L0_tok_b_expand': _L0_tok_in['b_expand'], 'L0_tok_g_conv_norm': _L0_tok_in['g_conv_norm'], 'L0_tok_b_conv_norm': _L0_tok_in['b_conv_norm'], 'L0_tok_w_ff1': _L0_tok_in['w_ff1'], 'L0_tok_b_ff1': _L0_tok_in['b_ff1'], 'L0_tok_w_ff2': _L0_tok_in['w_ff2'], 'L0_tok_b_ff2': _L0_tok_in['b_ff2'], 'L0_tok_g_ff_norm': _L0_tok_in['g_ff_norm'], 'L0_tok_b_ff_norm': _L0_tok_in['b_ff_norm'], 'L0_attn_Wq': _L0_attn_in['Wq'], 'L0_attn_Wk': _L0_attn_in['Wk'], 'L0_attn_Wv': _L0_attn_in['Wv'], 'L0_ffn_expert_weights': _L0_ffn_in['expert_weights'], 'L0_ffn_expert_indices': _L0_ffn_in['expert_indices'], 'L0_ffn_w1': _L0_ffn_in['w1'], 'L0_ffn_w2': _L0_ffn_in['w2'], 'L1_attn_Wq': _L1_attn_in['Wq'], 'L1_attn_Wk': _L1_attn_in['Wk'], 'L1_attn_Wv': _L1_attn_in['Wv'], 'L1_ffn_Wr': _L1_ffn_in['Wr'], 'L1_ffn_br': _L1_ffn_in['br'], 'L1_ffn_Wgate': _L1_ffn_in['Wgate'], 'L1_ffn_bgate': _L1_ffn_in['bgate'], 'L1_ffn_W1': _L1_ffn_in['W1'], 'L1_ffn_W3': _L1_ffn_in['W3'], 'L1_ffn_W2': _L1_ffn_in['W2']}

def reference(x, L0_tok_w_compress, L0_tok_b_compress, L0_tok_w_main, L0_tok_b_main, L0_tok_w_expand, L0_tok_b_expand, L0_tok_g_conv_norm, L0_tok_b_conv_norm, L0_tok_w_ff1, L0_tok_b_ff1, L0_tok_w_ff2, L0_tok_b_ff2, L0_tok_g_ff_norm, L0_tok_b_ff_norm, L0_attn_Wq, L0_attn_Wk, L0_attn_Wv, L0_ffn_expert_weights, L0_ffn_expert_indices, L0_ffn_w1, L0_ffn_w2, L1_attn_Wq, L1_attn_Wk, L1_attn_Wv, L1_ffn_Wr, L1_ffn_br, L1_ffn_Wgate, L1_ffn_bgate, L1_ffn_W1, L1_ffn_W3, L1_ffn_W2):
    import jax
    import jax.numpy as jnp

    def _L0_tok_ref(x, w_compress, b_compress, w_main, b_main, w_expand, b_expand, g_conv_norm, b_conv_norm, w_ff1, b_ff1, w_ff2, b_ff2, g_ff_norm, b_ff_norm):
        import jax, jax.numpy as jnp
        import numpy as np
        EPS = 1e-05

        def conv1d(x, w, b, stride=1, padding=0):
            out = jax.lax.conv_general_dilated(x, w, window_strides=(stride,), padding=[(padding, padding)], dimension_numbers=('NCH', 'OIH', 'NCH'))
            return out + b[None, :, None]

        def layer_norm(x, g, b):
            mu = jnp.mean(x, axis=-1, keepdims=True)
            var = jnp.mean(jnp.square(x - mu), axis=-1, keepdims=True)
            return (x - mu) * jax.lax.rsqrt(var + EPS) * g + b
        xt = jnp.transpose(x, (0, 2, 1))
        identity = xt
        h = jax.nn.silu(conv1d(xt, w_compress, b_compress))
        h = jax.nn.silu(conv1d(h, w_main, b_main, stride=1, padding=1))
        h = conv1d(h, w_expand, b_expand)
        h = jnp.transpose(h, (0, 2, 1))
        identity = jnp.transpose(identity, (0, 2, 1))
        y = layer_norm(h + identity, g_conv_norm, b_conv_norm)
        ff = jnp.einsum('bth,oh->bto', y, w_ff1) + b_ff1
        ff = jax.nn.gelu(ff, approximate=False)
        ff = jnp.einsum('bto,ho->bth', ff, w_ff2) + b_ff2
        y = layer_norm(ff + y, g_ff_norm, b_ff_norm)
        yt = jnp.transpose(y, (0, 2, 1))
        pooled = jax.lax.reduce_window(yt, -jnp.inf, jax.lax.max, (1, 1, 3), (1, 1, 1), 'VALID')
        return jnp.transpose(pooled, (0, 2, 1))

    def _L0_attn_ref(x, Wq, Wk, Wv):
        import jax, jax.numpy as jnp
        import numpy as np
        N_HEADS = 8
        N_GROUPS = 4
        B, T, D = (16, 256, 128)
        GH = D // N_HEADS * N_GROUPS

        def _rope_tables(t, d):
            i = np.arange(d // 2, dtype=np.float64)
            theta = 10000.0 ** (-(2.0 * (i - 1.0))) / d
            ang = np.arange(t, dtype=np.float64)[:, None] * theta[None, :]
            return (jnp.asarray(np.cos(ang), jnp.float32), jnp.asarray(np.sin(ang), jnp.float32))

        def _apply_rope(x, cos, sin):
            xe, xo = (x[..., 0::2], x[..., 1::2])
            oe = xe * cos + xo * sin
            oo = -xe * sin + xo * cos
            return jnp.stack([oe, oo], axis=-1).reshape(x.shape)
        b, t, c = x.shape
        n, ng = (N_HEADS, N_GROUPS)
        h = c // n
        npg = n // ng
        gh = h * ng
        cq, sq = _rope_tables(t, c)
        ck, sk = _rope_tables(t, gh)
        q = _apply_rope(x @ Wq, cq, sq)
        k = _apply_rope(x @ Wk, ck, sk)
        v = x @ Wv
        q = q.reshape(b, t, ng, npg, h)
        k = k.reshape(b, t, ng, h)
        v = v.reshape(b, t, ng, h)
        att = jnp.einsum('bigph,bjgh->bgpij', q, k) / h ** 0.5
        causal = jnp.tril(jnp.ones((t, t), dtype=bool))
        att = jnp.where(causal, att, -jnp.inf)
        att = jax.nn.softmax(att, axis=-1)
        out = jnp.einsum('bgpij,bjgh->bgpih', att, v)
        return jnp.transpose(out, (0, 2, 1, 3, 4)).reshape(b, t, c)

    def _L0_ffn_ref(x, expert_weights, expert_indices, w1, w2):
        import jax, jax.numpy as jnp
        import numpy as np
        NUM_EXPERTS = 8
        TOP_K = 2
        'Dropless MoE: sort assignments by expert, gather tokens, grouped MLP,\n            scatter-combine with top-k router weights (megablocks gather/scatter semantics).'
        in_shape = x.shape
        hs = in_shape[-1]
        x_flat = x.reshape(-1, hs)
        T = x_flat.shape[0]
        flat_ids = expert_indices.reshape(-1)
        order = jnp.argsort(flat_ids)
        bin_ids = flat_ids[order]
        token_ids = order // TOP_K
        xg = x_flat[token_ids]
        y = jnp.zeros_like(xg)
        for e in range(NUM_EXPERTS):
            h = jax.nn.gelu(xg @ w1[e], approximate=False)
            y = jnp.where((bin_ids == e)[:, None], h @ w2[e], y)
        w = expert_weights.reshape(-1)[order][:, None]
        out = jnp.zeros((T, hs), x.dtype).at[token_ids].add(w * y)
        return out.reshape(in_shape)

    def _L1_attn_ref(x, Wq, Wk, Wv):
        import jax, jax.numpy as jnp
        import numpy as np
        B, N, D_IN, D_HID, D_OUT = (8, 512, 128, 128, 128)
        q = jnp.einsum('bnd,hd->bnh', x, Wq)
        k = jnp.einsum('bnd,hd->bnh', x, Wk)
        v = jnp.einsum('bnd,od->bno', x, Wv)
        scores = jnp.einsum('bqh,bkh->bqk', q, k)
        attn = jax.nn.softmax(scores, axis=1)
        return jnp.einsum('bqk,bko->bqo', attn, v)

    def _L1_ffn_ref(x, Wr, br, Wgate, bgate, W1, W3, W2):
        import jax, jax.numpy as jnp
        import numpy as np
        G = 4
        EPG = 4
        E = 16
        KG = 2
        K = 2
        GTP = 0.9
        TP = 0.9
        SCALE = 1.0 / float(np.sqrt(G))

        def _routing_weights(xf, Wr, br, Wgate, bgate):
            N = xf.shape[0]
            gp = jax.nn.softmax(xf @ Wr + br, axis=-1)
            order = jnp.argsort(-gp, axis=-1)
            sp_k = jnp.take_along_axis(gp, order, axis=-1)[:, :KG]
            idx_k = order[:, :KG]
            act = jnp.cumsum(sp_k, axis=-1) <= GTP
            act = act.at[:, 0].set(True)
            mp = sp_k * act
            rn = mp / (jnp.sum(mp, axis=-1, keepdims=True) + 1e-09)
            w_group = jnp.zeros((N, G), xf.dtype).at[jnp.arange(N)[:, None], idx_k].set(rn)
            ep = jax.nn.softmax(jnp.einsum('nd,gde->nge', xf, Wgate) + bgate, axis=-1)
            eorder = jnp.argsort(-ep, axis=-1)
            esp = jnp.take_along_axis(ep, eorder, axis=-1)[:, :, :K]
            eidx = eorder[:, :, :K]
            eact = jnp.cumsum(esp, axis=-1) <= TP
            eact = eact.at[:, :, 0].set(True)
            emp = esp * eact
            ern = emp / (jnp.sum(emp, axis=-1, keepdims=True) + 1e-09)
            w_exp = jnp.zeros((N, G, EPG), xf.dtype).at[jnp.arange(N)[:, None, None], jnp.arange(G)[None, :, None], eidx].set(ern)
            return (w_group[:, :, None] * w_exp * SCALE).reshape(N, E)
        B, T, D = x.shape
        xf = x.reshape(-1, D)
        tw = _routing_weights(xf, Wr, br, Wgate, bgate)
        out = jnp.zeros_like(xf)
        for e in range(E):
            h = jax.nn.silu(xf @ W1[e]) * (xf @ W3[e])
            out = out + tw[:, e:e + 1] * (h @ W2[e])
        return out.reshape(B, T, D)
    h = _L0_tok_ref(x, L0_tok_w_compress, L0_tok_b_compress, L0_tok_w_main, L0_tok_b_main, L0_tok_w_expand, L0_tok_b_expand, L0_tok_g_conv_norm, L0_tok_b_conv_norm, L0_tok_w_ff1, L0_tok_b_ff1, L0_tok_w_ff2, L0_tok_b_ff2, L0_tok_g_ff_norm, L0_tok_b_ff_norm)
    h = h + _L0_attn_ref(_layernorm(h, axis=-1), L0_attn_Wq, L0_attn_Wk, L0_attn_Wv)
    h = h + _L0_ffn_ref(_layernorm(h, axis=-1), L0_ffn_expert_weights, L0_ffn_expert_indices, L0_ffn_w1, L0_ffn_w2)
    h = h + _L1_attn_ref(_layernorm(h, axis=-1), L1_attn_Wq, L1_attn_Wk, L1_attn_Wv)
    h = h + _L1_ffn_ref(_layernorm(h, axis=-1), L1_ffn_Wr, L1_ffn_br, L1_ffn_Wgate, L1_ffn_bgate, L1_ffn_W1, L1_ffn_W3, L1_ffn_W2)
    return h

_drawn_inputs = setup_inputs


def setup_inputs(seed=0):
    import zlib

    import numpy as np

    out = dict(_drawn_inputs(seed))
    spreads = {'L0_tok_b_compress': (0.0, 0.8),
     'L0_tok_b_main': (0.0, 0.267),
     'L0_tok_b_expand': (0.0, 0.1),
     'L0_tok_g_conv_norm': (1.0, 0.2),
     'L0_tok_b_conv_norm': (0.0, 0.1),
     'L0_tok_b_ff1': (0.0, 0.362),
     'L0_tok_b_ff2': (0.0, 0.1),
     'L0_tok_g_ff_norm': (1.0, 0.2),
     'L0_tok_b_ff_norm': (0.0, 0.1),
     'L1_ffn_br': (0.0, 0.8),
     'L1_ffn_bgate': (0.0, 0.8)}
    factors = {'L0_tok_w_compress': 8.0,
     'L0_tok_w_main': 8.0,
     'L1_ffn_Wr': 8.0,
     'L1_ffn_Wgate': 8.0,
     'L1_ffn_W1': 8.0,
     'L1_ffn_W3': 8.0,
     'L1_ffn_W2': 8.0}
    for name, (base, spread) in spreads.items():
        noise = np.random.default_rng([zlib.crc32(name.encode()), seed]).standard_normal(out[name].shape)
        drawn = base * np.exp(spread * noise) if base else spread * noise
        out[name] = jnp.asarray(drawn.astype(out[name].dtype))
    for name, factor in factors.items():
        out[name] = (out[name] * factor).astype(out[name].dtype)
    return out
```

```python
from contextlib import ExitStack

import numpy as np

import concourse.bass as bass
from concourse import mybir

F32 = mybir.dt.float32
I32 = mybir.dt.int32
BF16 = mybir.dt.bfloat16
ALU = mybir.AluOpType
ACT = mybir.ActivationFunctionType
AX = mybir.AxisListType

B, T_IN, D = 8, 750, 128
T = T_IN - 2
P = 128
NJ = -(-T // P)
TP = NJ * P
LAST = T - (NJ - 1) * P
LAST_IN = T_IN - (NJ - 1) * P
BN = 64
EPS = 1e-5
HEADS, GROUPS, HD = 8, 4, 16
ATT_SCALE = HD ** -0.5
MASKED = -1.0e30
E0, TOPK0, F0, N0 = 8, 2, 512, 1024
E1, G1, PG1, F1 = 16, 4, 4, 512
CHOICES = 4
BLOCKS = (CHOICES * B * TP + E1 * (P - 1)) // P
BLOCKS += BLOCKS % 2
THRESHOLD = 0.9


def batch_rows(dram, b):
    return dram[b][0:(NJ - 1) * P].rearrange("(j p) d -> p j d", p=P), dram[b][(NJ - 1) * P:]


def normalise(dve, consts, src, out, stats, moments, rstd, sems, turn):
    stats_done, moments_done, rstd_done, out_done = sems
    tiles = src.shape[1]
    for j in range(tiles):
        ins = dve.bn_stats(stats[:, j, :], src[:, j, :])
    ins.then_inc(stats_done, 1)
    dve.wait_ge(stats_done, turn)
    dve.memset(consts.carrier[:, 0:1], 0.0)
    for j in range(tiles):
        ins = dve.bn_aggr(moments[:, j, :], stats[:, j, :])
    ins.then_inc(moments_done, 1)
    dve.wait_ge(rstd_done, turn)
    for j in range(tiles):
        ins = dve.tensor_scalar(out[:, j, :], src[:, j, :], moments[:, j, 0:1], rstd[:, j:j + 1],
                                ALU.subtract, ALU.mult)
    ins.then_inc(out_done, 1)


def invert_deviation(pool, moments, rstd, consts, sems, turn):
    stats_done, moments_done, rstd_done, _ = sems
    tiles = moments.shape[1]
    pool.wait_ge(moments_done, 2 * turn - 1)
    pool.tensor_tensor(moments[:, :, 1], moments[:, :, 1], consts.eps[:, 0:tiles], ALU.add).then_inc(moments_done, 1)
    pool.wait_ge(moments_done, 2 * turn)
    pool.tensor_tensor(rstd[:, :], moments[:, :, 1], consts.minus_half[:, 0:tiles], ALU.pow).then_inc(rstd_done, 1)


def token_mixer(nc, x, w, hidden, ident, consts, psum):
    with ExitStack() as ctx:
        def sb(name, shape, n=2):
            return [ctx.enter_context(nc.sbuf_tensor(f"{name}{u}", shape, F32)) for u in range(n)]

        def sem(name):
            return ctx.enter_context(nc.semaphore(name))

        def two(name):
            return [sem(f"{name}{u}") for u in range(2)]

        x_in = sb("tm_x", [P, NJ, P])
        xT = sb("tm_xT", [P, TP])
        taps = sb("tm_taps", [P, T_IN + 2])
        mixed = sb("tm_mixed", [BN + 1, TP])
        y0 = sb("tm_y0", [P, NJ, P])
        yhat = sb("tm_yhat", [P, NJ, P])
        y1T = sb("tm_y1T", [P, TP])
        ff = sb("tm_ff", [BN + 1, TP])
        y2T = sb("tm_y2T", [P, TP])
        pool_a = sb("tm_pool_a", [P, TP])
        pooledT = sb("tm_pooledT", [P, TP])
        stats = sb("tm_stats", [P, NJ, 6])
        moments = sb("tm_moments", [P, NJ, 2])
        rstd = sb("tm_rstd", [P, NJ])
        wc = ctx.enter_context(nc.sbuf_tensor("tm_wc", [P, P], F32))
        wm01 = ctx.enter_context(nc.sbuf_tensor("tm_wm01", [P, BN], F32))
        wm2 = ctx.enter_context(nc.sbuf_tensor("tm_wm2", [BN, BN], F32))
        we = ctx.enter_context(nc.sbuf_tensor("tm_we", [BN + 1, P], F32))
        wf1 = ctx.enter_context(nc.sbuf_tensor("tm_wf1", [P, BN], F32))
        wf2 = ctx.enter_context(nc.sbuf_tensor("tm_wf2", [BN + 1, P], F32))
        vec = ctx.enter_context(nc.sbuf_tensor("tm_vec", [P, 7], F32))
        bc, bm, bf1, g_conv, b_conv, g_ff, b_ff = (vec[:, i:i + 1] for i in range(7))

        weights_in = sem("tm_weights_in")
        zeros_set = sem("tm_zeros_set")
        x_loaded = two("tm_x_loaded")
        xT_ps, xT_ready = sem("tm_xT_ps"), sem("tm_xT_ready")
        comp_ps, taps_ready = sem("tm_comp_ps"), sem("tm_taps_ready")
        mix_ps, mixed_ready = sem("tm_mix_ps"), sem("tm_mixed_ready")
        exp_ps, y0_ready = sem("tm_exp_ps"), sem("tm_y0_ready")
        norm1 = [sem(f"tm_norm1_{s}") for s in ("stats", "moments", "rstd", "out")]
        norm2 = [sem(f"tm_norm2_{s}") for s in ("stats", "moments", "rstd", "out")]
        y1T_ps, y1T_ready = sem("tm_y1T_ps"), sem("tm_y1T_ready")
        ff_ps, ff_ready = sem("tm_ff_ps"), sem("tm_ff_ready")
        out_ps = sem("tm_out_ps")
        y2T_ps, y2T_ready = sem("tm_y2T_ps"), sem("tm_y2T_ready")
        pool_half, pooled_ready = sem("tm_pool_half"), sem("tm_pooled_ready")
        h_ps, h_ready = sem("tm_h_ps"), sem("tm_h_ready")

        def banks(step, u):
            k = 4 * (step % 2) + 2 * u
            return psum[:, k:k + 2, :]

        def tiles_of(step, u):
            return banks(step, u).rearrange("p k n -> p (k n)")[:, 0:TP].rearrange("p (j n) -> p j n", n=P)

        HALF_IN = T_IN // 2

        with nc.Block() as block:
            @block.sync
            def _(sp):
                for dst, src in ((wc[:, 0:BN], w["wcT"]), (wc[:, BN:P], w["wcT"]),
                                 (wm01[0:BN, :], w["wmT"][0]), (wm01[BN:P, :], w["wmT"][1]), (wm2[:, :], w["wmT"][2]),
                                 (we[:, :], w["weT"]), (wf1[:, :], w["wf1T"]), (wf2[:, :], w["wf2T"]),
                                 (vec[0:BN, 0:1], w["bc"]), (vec[BN:P, 0:1], w["bc"]),
                                 (vec[0:BN, 1:2], w["bm"]), (vec[0:BN, 2:3], w["bf1"]),
                                 (vec[:, 3:7], w["norms"])):
                    sp.dma_start(dst, src).then_inc(weights_in, 16)
                sp.wait_ge(zeros_set, 1)
                for u in range(2):
                    whole, rest = batch_rows(x, u)
                    sp.dma_start(x_in[u][:, 0:NJ - 1, :], whole).then_inc(x_loaded[u], 16)
                    sp.dma_start(x_in[u][0:LAST_IN, NJ - 1, :], rest).then_inc(x_loaded[u], 16)
                with sp.Fori(1, B // 2) as i:
                    for u in range(2):
                        sp.wait_ge(y0_ready, 2 * i + u - 1)
                        whole, rest = batch_rows(x, 2 * i + u)
                        sp.dma_start(x_in[u][:, 0:NJ - 1, :], whole).then_inc(x_loaded[u], 16)
                        sp.dma_start(x_in[u][0:LAST_IN, NJ - 1, :], rest).then_inc(x_loaded[u], 16)

            @block.gpsimd
            def _(pool):
                with pool.Fori(0, B // 2) as i:
                    for norm in (norm1, norm2):
                        for u in range(2):
                            invert_deviation(pool, moments[u], rstd[u], consts, norm, 2 * i + u + 1)

            @block.tensor
            def _(pe):
                pe.wait_ge(weights_in, 16 * 13)
                pe.wait_ge(zeros_set, 2)
                with pe.Fori(0, B // 2) as i:
                    for u in range(2):
                        pe.wait_ge(x_loaded[u], 32 * i + 32)
                        pe.wait_ge(h_ready, 2 * i + u + 1)
                        for j in range(NJ):
                            ins = pe.transpose(tiles_of(0, u)[:, j, :], x_in[u][:, j, :], ident)
                        ins.then_inc(xT_ps, 1)
                    for u in range(2):
                        pe.wait_ge(xT_ready, 2 * i + u + 1)
                        for h in range(2):
                            ins = pe.matmul(banks(1, u)[:, h, 0:HALF_IN], wc[:, :], xT[u][:, h * HALF_IN:(h + 1) * HALF_IN],
                                            start=True, stop=True)
                        ins.then_inc(comp_ps, 1)
                    for u in range(2):
                        pe.wait_ge(taps_ready, 2 * (2 * i + u + 1))
                        for h in range(2):
                            pe.matmul(banks(2, u)[0:BN, h, 0:HALF_IN], wm01[:, :], taps[u][:, h * HALF_IN:(h + 1) * HALF_IN],
                                      start=True, stop=False)
                            ins = pe.matmul(banks(2, u)[0:BN, h, 0:HALF_IN], wm2[:, :],
                                            taps[u][0:BN, h * HALF_IN + 2:(h + 1) * HALF_IN + 2], start=False, stop=True)
                        ins.then_inc(mix_ps, 1)
                    for u in range(2):
                        pe.wait_ge(mixed_ready, 2 * i + u + 1)
                        for j in range(NJ):
                            ins = pe.matmul(tiles_of(3, u)[:, j, :], mixed[u][:, j * P:(j + 1) * P], we[:, :], start=True, stop=True)
                        ins.then_inc(exp_ps, 1)
                    for u in range(2):
                        pe.wait_ge(norm1[3], 2 * i + u + 1)
                        for j in range(NJ):
                            ins = pe.transpose(tiles_of(4, u)[:, j, :], yhat[u][:, j, :], ident)
                        ins.then_inc(y1T_ps, 1)
                    for u in range(2):
                        pe.wait_ge(y1T_ready, 2 * i + u + 1)
                        for h in range(2):
                            ins = pe.matmul(banks(5, u)[0:BN, h, 0:TP // 2], wf1[:, :], y1T[u][:, h * TP // 2:(h + 1) * TP // 2],
                                            start=True, stop=True)
                        ins.then_inc(ff_ps, 1)
                    for u in range(2):
                        pe.wait_ge(ff_ready, 2 * i + u + 1)
                        for j in range(NJ):
                            pe.matmul(tiles_of(6, u)[:, j, :], ff[u][:, j * P:(j + 1) * P], wf2[:, :], start=True, stop=False)
                            ins = pe.matmul(tiles_of(6, u)[:, j, :], y1T[u][:, j * P:(j + 1) * P], ident, start=False, stop=True)
                        ins.then_inc(out_ps, 1)
                    for u in range(2):
                        pe.wait_ge(norm2[3], 2 * i + u + 1)
                        for j in range(NJ):
                            ins = pe.transpose(tiles_of(7, u)[:, j, :], yhat[u][:, j, :], ident)
                        ins.then_inc(y2T_ps, 1)
                    for u in range(2):
                        pe.wait_ge(pooled_ready, 2 * i + u + 1)
                        for j in range(NJ):
                            ins = pe.transpose(tiles_of(8, u)[:, j, :], pooledT[u][:, j * P:(j + 1) * P], ident)
                        ins.then_inc(h_ps, 1)

            @block.scalar
            def _(act):
                act.wait_ge(weights_in, 16 * 13)
                act.wait_ge(zeros_set, 2)
                with act.Fori(0, B // 2) as i:
                    for u in range(2):
                        act.wait_ge(comp_ps, 2 * i + u + 1)
                        act.activation(taps[u][0:BN, 1:T_IN + 1].rearrange("p (h n) -> p h n", h=2),
                                       banks(1, u)[0:BN, :, 0:HALF_IN], ACT.Silu, bias=bc[0:BN]).then_inc(taps_ready, 1)
                        act.activation(taps[u][BN:P, 0:T_IN].rearrange("p (h n) -> p h n", h=2),
                                       banks(1, u)[BN:P, :, 0:HALF_IN], ACT.Silu, bias=bc[BN:P]).then_inc(taps_ready, 1)
                    for u in range(2):
                        act.wait_ge(mix_ps, 2 * i + u + 1)
                        act.activation(mixed[u][0:BN, 0:T_IN].rearrange("p (h n) -> p h n", h=2),
                                       banks(2, u)[0:BN, :, 0:HALF_IN], ACT.Silu, bias=bm[0:BN]).then_inc(mixed_ready, 1)
                    for u in range(2):
                        act.wait_ge(ff_ps, 2 * i + u + 1)
                        act.activation(ff[u][0:BN, :].rearrange("p (h n) -> p h n", h=2),
                                       banks(5, u)[0:BN, :, 0:TP // 2], ACT.Gelu, bias=bf1[0:BN]).then_inc(ff_ready, 1)
                    for u in range(2):
                        act.wait_ge(h_ps, 2 * i + u + 1)
                        act.activation(hidden[:, bass.ds((2 * i + u) * NJ, NJ), :], tiles_of(8, u), ACT.Copy).then_inc(h_ready, 1)

            @block.vector
            def _(dve):
                for u in range(2):
                    dve.memset(x_in[u][96:P, NJ - 1, :], 0.0)
                    dve.memset(taps[u][:, :], 0.0)
                    dve.memset(mixed[u][:, :], 0.0)
                    dve.memset(pooledT[u][:, :], 0.0)
                    dve.memset(ff[u][BN:BN + 1, :], 1.0)
                    dve.memset(pool_a[u][:, :], 0.0)
                dve.memset(y2T[0][:, :], 0.0).then_inc(zeros_set, 1)
                dve.memset(y2T[1][:, :], 0.0).then_inc(h_ready, 2)
                dve.wait_ge(zeros_set, 1)
                for u in range(2):
                    ins = dve.memset(mixed[u][BN:BN + 1, :], 1.0)
                ins.then_inc(zeros_set, 1)
                dve.wait_ge(weights_in, 16 * 13)
                with dve.Fori(0, B // 2) as i:
                    for u in range(2):
                        dve.wait_ge(xT_ps, 2 * i + u + 1)
                        dve.tensor_copy(xT[u][:, :].rearrange("p (j n) -> p j n", n=P), tiles_of(0, u)).then_inc(xT_ready, 1)
                    for u in range(2):
                        dve.wait_ge(exp_ps, 2 * i + u + 1)
                        dve.tensor_tensor(y0[u][:, :, :], tiles_of(3, u), x_in[u][:, :, :], ALU.add).then_inc(y0_ready, 1)
                        dve.wait_ge(y0_ready, 2 * i + u + 1)
                        normalise(dve, consts, y0[u], yhat[u], stats[u], moments[u], rstd[u], norm1, 2 * i + u + 1)
                    for u in range(2):
                        dve.wait_ge(y1T_ps, 2 * i + u + 1)
                        dve.tensor_scalar(y1T[u][:, :].rearrange("p (j n) -> p j n", n=P), tiles_of(4, u), g_conv, b_conv,
                                          ALU.mult, ALU.add).then_inc(y1T_ready, 1)
                    for u in range(2):
                        dve.wait_ge(out_ps, 2 * i + u + 1)
                        normalise(dve, consts, tiles_of(6, u), yhat[u], stats[u], moments[u], rstd[u], norm2, 2 * i + u + 1)
                    for u in range(2):
                        dve.wait_ge(y2T_ps, 2 * i + u + 1)
                        dve.tensor_scalar(y2T[u][:, :].rearrange("p (j n) -> p j n", n=P), tiles_of(7, u), g_ff, b_ff,
                                          ALU.mult, ALU.add).then_inc(y2T_ready, 1)
                    for u in range(2):
                        n = 2 * i + u + 1
                        dve.wait_ge(y2T_ready, n)
                        dve.tensor_tensor(pool_a[u][:, 0:T], y2T[u][:, 0:T], y2T[u][:, 1:T + 1], ALU.max).then_inc(pool_half, 1)
                        dve.wait_ge(pool_half, n)
                        dve.tensor_tensor(pooledT[u][:, 0:T], pool_a[u][:, 0:T], y2T[u][:, 2:T + 2], ALU.max).then_inc(pooled_ready, 1)



def rope_attention(nc, w, hidden, ident, consts, psum):
    UNITS = [(j, p, g) for j in range(NJ) for p in range(2) for g in range(GROUPS)]
    NU = len(UNITS)
    with ExitStack() as ctx:
        def sb(name, shape, n=1):
            t = [ctx.enter_context(nc.sbuf_tensor(f"{name}{u}", shape, F32)) for u in range(n)]
            return t if n > 1 else t[0]

        def sem(name):
            return ctx.enter_context(nc.semaphore(name))

        hn = sb("ra_hn", [P, NJ, P])
        hnT = sb("ra_hnT", [P, TP])
        stats, moments, rstd = sb("ra_stats", [P, NJ, 6]), sb("ra_moments", [P, NJ, 2]), sb("ra_rstd", [P, NJ])
        cos, sin = sb("ra_cos", [P, 3, TP]), sb("ra_sin", [P, 3, TP])
        wqk = sb("ra_wqk", [P, 3, 2, P])
        wv = sb("ra_wv", [P, GROUPS * HD])
        mask = sb("ra_mask", [P, TP])
        by_cos, by_sin = sb("ra_by_cos", [P, TP], 2), sb("ra_by_sin", [P, TP], 2)
        qk = sb("ra_qk", [P, 3, TP])
        v = sb("ra_v", [P, NJ, GROUPS * HD])
        scaled = sb("ra_scaled", [P, TP], 3)
        least = sb("ra_least", [P, 3])
        prob = sb("ra_prob", [P, TP], 2)
        probT = sb("ra_probT", [P, TP], 2)
        sums = sb("ra_sums", [P, NU])
        recip = sb("ra_recip", [P, NU])
        att = sb("ra_att", [P, NU, HD])
        rows = sb("ra_rows", [P, NJ, P], 2)

        consts_in = sem("ra_consts_in")
        norm = [sem(f"ra_norm_{s}") for s in ("stats", "moments", "rstd", "out")]
        hnT_ps, hnT_ready = sem("ra_hnT_ps"), sem("ra_hnT_ready")
        qk_ps, by_ready, qk_ready = sem("ra_qk_ps"), sem("ra_by_ready"), sem("ra_qk_ready")
        v_ps, v_ready = sem("ra_v_ps"), sem("ra_v_ready")
        score_ps, least_ready, prob_ready = sem("ra_score_ps"), sem("ra_least_ready"), sem("ra_prob_ready")
        probT_ps, probT_ready, pv_done = sem("ra_probT_ps"), sem("ra_probT_ready"), sem("ra_pv_done")
        recip_ready, att_ready, att_stored = sem("ra_recip_ready"), sem("ra_att_ready"), sem("ra_att_stored")
        rows_loaded, h_ready = [sem("ra_rows_loaded0"), sem("ra_rows_loaded1")], sem("ra_h_ready")
        by_head = nc.dram_tensor("att_by_head", (B, HEADS, T, HD), F32, kind="Internal").ap()
        by_row = by_head.rearrange("b h t c -> b (h t c)").rearrange("b (t d) -> b t d", d=D)

        flat = psum[:, :, :].rearrange("p k n -> p (k n)")

        def bank_pair(k):
            return flat[:, k * 512:k * 512 + TP]

        with nc.Block() as block:
            @block.sync
            def _(sp):
                for dst, src in ((cos[:, :, :], w["cos"]), (sin[:, :, :], w["sin"]), (wqk[:, :, :, :], w["wqk"]),
                                 (wv[:, :], w["wv0"]), (mask[:, :], w["mask"])):
                    sp.dma_start(dst, src).then_inc(consts_in, 16)
                with sp.Fori(0, B) as b:
                    sp.wait_ge(att_ready, b + 2)
                    for j in range(NJ):
                        rows = min(P, T - j * P)
                        sp.dma_start(by_head[b][:, j * P:j * P + rows, :].rearrange("h t c -> t h c"),
                                     att[0:rows, j * HEADS:(j + 1) * HEADS, :]).then_inc(att_stored, 16)
                sp.wait_ge(att_stored, 16 * NJ * (B + 1))

            @block.tensor
            def _(pe):
                pe.wait_ge(consts_in, 80)
                with pe.Fori(0, B) as b:
                    pe.wait_ge(norm[3], b + 1)
                    for j in range(NJ):
                        ins = pe.transpose(bank_pair(4)[:, j * P:(j + 1) * P], hn[:, j, :], ident)
                    ins.then_inc(hnT_ps, 1)
                    pe.wait_ge(hnT_ready, b + 1)
                    pe.wait_ge(att_ready, b + 1)
                    for s in range(3):
                        if s == 2:
                            pe.wait_ge(by_ready, 3 * b + 1)
                        for side in range(2):
                            for h in range(2):
                                k = 4 * (s % 2) + 2 * side + h
                                ins = pe.matmul(psum[:, k, 0:TP // 2], wqk[:, s, side, :], hnT[:, h * TP // 2:(h + 1) * TP // 2],
                                                start=True, stop=True)
                        ins.then_inc(qk_ps, 1)
                    pe.wait_ge(by_ready, 3 * b + 2)
                    for j in range(NJ):
                        ins = pe.matmul(psum[:, 4, j * BN:(j + 1) * BN], hnT[:, j * P:(j + 1) * P], wv[:, :], start=True, stop=True)
                    ins.then_inc(v_ps, 1)
                    pe.wait_ge(by_ready, 3 * b + 3)
                    pe.wait_ge(qk_ready, 3 * b + 3)
                    pe.wait_ge(v_ready, b + 1)

                    def scores(n):
                        j, p, g = UNITS[n]
                        if n >= 2:
                            pe.wait_ge(least_ready, NU * b + n - 1)
                        out = bank_pair(2 * (n % 2))
                        for lo in range(0, (j + 1) * P, 512):
                            hi = min(lo + 512, (j + 1) * P)
                            ins = pe.matmul(out[:, lo:hi], qk[32 * g:32 * g + 32, p, j * P:(j + 1) * P],
                                            qk[32 * g:32 * g + 32, 2, lo:hi], start=True, stop=True)
                        ins.then_inc(score_ps, 1)

                    def turn(n):
                        j = UNITS[n][0]
                        pe.wait_ge(prob_ready, NU * b + n + 1)
                        if n >= 1:
                            pe.wait_ge(probT_ready, NU * b + n)
                        for k in range(j + 1):
                            ins = pe.transpose(bank_pair(4)[:, k * P:(k + 1) * P], prob[n % 2][:, k * P:(k + 1) * P], ident)
                        ins.then_inc(probT_ps, 1)

                    def values(n):
                        j, p, g = UNITS[n]
                        col = j * P + (GROUPS * p + g) * HD
                        pe.wait_ge(probT_ready, NU * b + n + 1)
                        for k in range(j + 1):
                            ins = pe.matmul(bank_pair(6)[:, col:col + HD], probT[n % 2][:, k * P:(k + 1) * P],
                                            v[:, k, g * HD:(g + 1) * HD], start=(k == 0), stop=(k == j))
                        ins.then_inc(pv_done, 1)

                    scores(0)
                    scores(1)
                    for n in range(NU):
                        if n + 2 < NU:
                            scores(n + 2)
                        turn(n)
                        if n >= 1:
                            values(n - 1)
                    values(NU - 1)

            @block.scalar
            def _(act):
                with act.Fori(0, B) as b:
                    act.wait_ge(hnT_ps, b + 1)
                    act.activation(hnT[:, :], bank_pair(4), ACT.Copy).then_inc(hnT_ready, 1)
                    act.wait_ge(v_ps, b + 1)
                    act.activation(v[:, :, :].rearrange("p j n -> p (j n)"), psum[:, 4, 0:NJ * BN], ACT.Copy).then_inc(v_ready, 1)

                    def turned(n):
                        width = (UNITS[n][0] + 1) * P
                        act.wait_ge(probT_ps, NU * b + n + 1)
                        if n >= 2:
                            act.wait_ge(pv_done, NU * b + n - 1)
                        act.activation(probT[n % 2][:, 0:width], bank_pair(4)[:, 0:width], ACT.Copy).then_inc(probT_ready, 1)

                    for n in range(NU):
                        j, p, g = UNITS[n]
                        width = (j + 1) * P
                        act.wait_ge(least_ready, NU * b + n + 1)
                        if n >= 2:
                            act.wait_ge(probT_ps, NU * b + n - 1)
                        at = j * HEADS + GROUPS * p + g
                        act.activation(prob[n % 2][:, 0:width], scaled[n % 3][:, 0:width], ACT.Exp, bias=least[:, n % 3:n % 3 + 1],
                                       scale=-1.0, accum_out=sums[:, at:at + 1]).then_inc(prob_ready, 1)
                        if n >= 1 and (n - 1) % 2 == 1:
                            turned(n - 1)
                    turned(NU - 1)

            @block.vector
            def _(dve):
                dve.memset(recip[:, :], 0.0).then_inc(att_ready, 1)
                dve.memset(att[:, :, :], 0.0).then_inc(att_stored, 16 * NJ)
                dve.wait_ge(consts_in, 80)
                with dve.Fori(0, B) as b:
                    here = hidden[:, bass.ds(b * NJ, NJ), :]
                    normalise(dve, consts, here, hn, stats, moments, rstd, norm, b + 1)
                    for s in range(3):
                        k = 4 * (s % 2)
                        dve.wait_ge(qk_ps, 3 * b + s + 1)
                        if s == 2:
                            dve.wait_ge(qk_ready, 3 * b + 1)
                        for side, table, out in ((0, cos, by_cos), (1, sin, by_sin)):
                            src = psum[:, k + 2 * side:k + 2 * side + 2, 0:TP // 2]
                            ins = dve.tensor_tensor(out[s % 2][:, :].rearrange("p (h n) -> p h n", h=2), src,
                                                    table[:, s, :].rearrange("p (h n) -> p h n", h=2), ALU.mult)
                        ins.then_inc(by_ready, 1)

                    def turned(n):
                        width = (UNITS[n][0] + 1) * P
                        dve.wait_ge(probT_ps, NU * b + n + 1)
                        if n >= 2:
                            dve.wait_ge(pv_done, NU * b + n - 1)
                        dve.tensor_copy(probT[n % 2][:, 0:width], bank_pair(4)[:, 0:width]).then_inc(probT_ready, 1)

                    for n in range(NU):
                        j, p, g = UNITS[n]
                        width = (j + 1) * P
                        dve.wait_ge(score_ps, NU * b + n + 1)
                        if n >= 3:
                            dve.wait_ge(prob_ready, NU * b + n - 2)
                        dve.memset(consts.carrier[:, 1 + n % 4:2 + n % 4], 0.0)
                        dve.tensor_tensor_reduce(scaled[n % 3][:, 0:width], bank_pair(2 * (n % 2))[:, 0:width],
                                                 mask[:, TP - width:TP], -ATT_SCALE, -MASKED, ALU.add, ALU.min,
                                                 least[:, n % 3:n % 3 + 1]).then_inc(least_ready, 1)
                        if n >= 2 and n % 2 == 0:
                            turned(n - 2)
                    turned(NU - 2)
                    dve.wait_ge(prob_ready, NU * b + NU)
                    dve.reciprocal(recip[:, :], sums[:, :]).then_inc(recip_ready, 1)
                    dve.wait_ge(recip_ready, b + 1)
                    dve.wait_ge(pv_done, NU * b + NU)
                    dve.wait_ge(att_stored, 16 * NJ * (b + 1))
                    dve.tensor_tensor(att[:, :, :], bank_pair(6).rearrange("p (n c) -> p n c", c=HD),
                                      recip[:, :].rearrange("p (n o) -> p n o", o=1).broadcast_to([P, NU, HD]), ALU.mult).then_inc(att_ready, 1)

            @block.gpsimd
            def _(pool):
                with pool.Fori(0, B) as b:
                    invert_deviation(pool, moments, rstd, consts, norm, b + 1)
                    for s in range(3):
                        pool.wait_ge(by_ready, 3 * b + s + 1)
                        pool.tensor_tensor(qk[:, s, :], by_cos[s % 2][:, :], by_sin[s % 2][:, :], ALU.add).then_inc(qk_ready, 1)


        with nc.Block() as block:
            @block.sync
            def _(sp):
                for u in range(2):
                    whole, rest = batch_rows(by_row, u)
                    sp.dma_start(rows[u][:, 0:NJ - 1, :], whole).then_inc(rows_loaded[u], 16)
                    sp.dma_start(rows[u][0:LAST, NJ - 1, :], rest).then_inc(rows_loaded[u], 16)
                with sp.Fori(1, B // 2) as i:
                    for u in range(2):
                        sp.wait_ge(h_ready, 2 * (2 * i + u - 1))
                        whole, rest = batch_rows(by_row, 2 * i + u)
                        sp.dma_start(rows[u][:, 0:NJ - 1, :], whole).then_inc(rows_loaded[u], 16)
                        sp.dma_start(rows[u][0:LAST, NJ - 1, :], rest).then_inc(rows_loaded[u], 16)

            @block.vector
            def _(dve):
                with dve.Fori(0, B // 2) as i:
                    for u in range(2):
                        first = (2 * i + u) * NJ
                        dve.wait_ge(rows_loaded[u], 32 * i + 32)
                        dve.tensor_tensor(hidden[:, bass.ds(first, NJ - 1), :], hidden[:, bass.ds(first, NJ - 1), :],
                                          rows[u][:, 0:NJ - 1, :], ALU.add).then_inc(h_ready, 1)
                        dve.tensor_tensor(hidden[0:LAST, bass.ds(first + NJ - 1, 1), :], hidden[0:LAST, bass.ds(first + NJ - 1, 1), :],
                                          rows[u][0:LAST, NJ - 1:NJ, :], ALU.add).then_inc(h_ready, 1)


def routed_ffn(nc, w, hidden, ident, consts, psum):
    NT = NJ + -(-(N0 - T) // P)
    TC = 3
    VU, NC = NT // TC, F0 // P
    W = TC * P
    with ExitStack() as ctx:
        def sb(name, shape, n=1, dt=F32):
            t = [ctx.enter_context(nc.sbuf_tensor(f"{name}{u}", shape, dt)) for u in range(n)]
            return t if n > 1 else t[0]

        def sem(name):
            return ctx.enter_context(nc.semaphore(name))

        hn, hnT = sb("rf_hn", [P, NT, P]), sb("rf_hnT", [P, NT * P])
        stats, moments, rstd = sb("rf_stats", [P, NT, 6]), sb("rf_moments", [P, NT, 2]), sb("rf_rstd", [P, NT])
        weight, index = sb("rf_weight", [P, NT, TOPK0]), sb("rf_index", [P, NT, TOPK0], dt=I32)
        index_f = sb("rf_index_f", [P, NT, TOPK0])
        chosen = sb("rf_chosen", [P, E0, TOPK0, NT])
        gate = sb("rf_gate", [P, E0, NT])
        gate_now = sb("rf_gate_now", [P, NT], 2)
        w1, w2 = sb("rf_w1", [P, F0], 2), sb("rf_w2", [P, NC, P], 2)
        actT = sb("rf_actT", [P, NC, W], 2)

        norm = [sem(f"rf_norm_{s}") for s in ("stats", "moments", "rstd", "out")]
        w_loaded = [sem("rf_w_loaded0"), sem("rf_w_loaded1")]
        zeroed, routes_in, index_ready, chosen_ready, gate_ready = (
            sem(f"rf_{s}") for s in ("zeroed", "routes_in", "index_ready", "chosen_ready", "gate_ready"))
        hnT_ps, hnT_ready = sem("rf_hnT_ps"), sem("rf_hnT_ready")
        up_ps, act_ready, down_done, added = sem("rf_up_ps"), sem("rf_act_ready"), sem("rf_down_done"), sem("rf_added")
        copied = sem("rf_gate_copied")

        def spans():
            return ((0, (NJ - 1) * P, 0), ((NJ - 1) * P, LAST, NJ - 1),
                    (T, (N0 - T) // P * P, NJ), (T + (N0 - T) // P * P, (N0 - T) % P, NT - 1))

        with nc.Block() as block:
            @block.sync
            def _(sp):
                def load(u, e):
                    sp.dma_start(w1[u][:, :], w["w1"][e]).then_inc(w_loaded[u], 16)
                    sp.dma_start(w2[u][:, :, :], w["w2"][e].rearrange("(k p) d -> p k d", p=P)).then_inc(w_loaded[u], 16)

                sp.wait_ge(zeroed, 1)
                for first, n, tile in spans():
                    for dst, src in ((weight, w["ew0"]), (index, w["ei0"])):
                        if n % P == 0:
                            sp.dma_start(dst[:, tile:tile + n // P, :],
                                         src[first:first + n].rearrange("(j p) k -> p j k", p=P)).then_inc(routes_in, 16)
                        else:
                            sp.dma_start(dst[0:n, tile, :], src[first:first + n]).then_inc(routes_in, 16)
                for u in range(2):
                    load(u, u)
                with sp.Fori(1, E0 // 2) as i:
                    for u in range(2):
                        sp.wait_ge(down_done, VU * (2 * i + u - 1) + 2)
                        load(u, 2 * i + u)

            @block.gpsimd
            def _(pool):
                invert_deviation(pool, moments, rstd, consts, norm, 1)

            @block.vector
            def _(dve):
                dve.memset(weight[:, :, :], 0.0)
                dve.memset(index[:, :, :], 0).then_inc(zeroed, 1)
                dve.memset(index_f[:, :, :], 0.0).then_inc(act_ready, 3)
                dve.memset(gate_now[0][:, :], 0.0).then_inc(down_done, 2)
                dve.memset(gate_now[1][:, :], 0.0).then_inc(added, 2)
                normalise(dve, consts, hidden[:, 0:NT, :], hn, stats, moments, rstd, norm, 1)
                dve.wait_ge(hnT_ps, 1)
                dve.tensor_copy(hnT[:, :], psum[:, :, :].rearrange("p k n -> p (k n)")[:, 0:NT * P]).then_inc(hnT_ready, 1)
                dve.wait_ge(routes_in, 16 * 8)
                dve.tensor_copy(index_f[:, :, :], index[:, :, :]).then_inc(index_ready, 1)
                dve.wait_ge(index_ready, 1)
                for e in range(E0):
                    for k in range(TOPK0):
                        ins = dve.scalar_tensor_tensor(out=chosen[:, e, k, :], in0=index_f[:, :, k], scalar=float(e),
                                                       in1=weight[:, :, k], op0=ALU.is_equal, op1=ALU.mult)
                ins.then_inc(chosen_ready, 1)
                dve.wait_ge(chosen_ready, 1)
                dve.tensor_tensor(gate[:, :, :], chosen[:, :, 0, :], chosen[:, :, 1, :], ALU.add).then_inc(gate_ready, 1)
                dve.wait_ge(gate_ready, 1)
                with dve.Fori(0, E0 // 2) as i:
                    for u in range(2):
                        dve.wait_ge(added, VU * (2 * i + u) + 2)
                        dve.tensor_copy(gate_now[u][:, :].rearrange("p (o n) -> p o n", o=1),
                                        gate[:, bass.ds(2 * i + u, 1), :]).then_inc(copied, 1)
                        dve.wait_ge(copied, 2 * i + u + 1)
                        for c in range(VU):
                            v = VU * u + c
                            V = 2 * VU * i + v
                            dve.wait_ge(down_done, V + 3)
                            dve.wait_ge(added, V + 1)
                            for t in range(TC):
                                tile = TC * c + t
                                ins = dve.scalar_tensor_tensor(
                                    out=hidden[:, tile, :], in0=psum[:, 6 + v % 2, t * P:(t + 1) * P],
                                    scalar=gate_now[u][:, tile:tile + 1], in1=hidden[:, tile, :], op0=ALU.mult, op1=ALU.add)
                            ins.then_inc(added, 1)

            @block.scalar
            def _(act):
                with act.Fori(0, E0 // 2) as i:
                    for v in range(2 * VU):
                        act.wait_ge(down_done, 2 * VU * i + v + 1)
                        for half in range(2):
                            m = 2 * v + half
                            act.wait_ge(up_ps, 4 * VU * i + m + 1)
                            act.activation(actT[v % 2][:, 2 * half:2 * half + 2, :], psum[:, 2 * (m % 3):2 * (m % 3) + 2, 0:W],
                                           ACT.Gelu).then_inc(act_ready, 1)

            @block.tensor
            def _(pe):
                pe.wait_ge(norm[3], 1)
                flat = psum[:, :, :].rearrange("p k n -> p (k n)")
                for j in range(NT):
                    ins = pe.transpose(flat[:, j * P:(j + 1) * P], hn[:, j, :], ident)
                ins.then_inc(hnT_ps, 1)
                pe.wait_ge(hnT_ready, 1)
                pe.wait_ge(added, 2)
                pe.wait_ge(act_ready, 3)
                with pe.Fori(0, E0 // 2) as i:
                    def up(m):
                        u, c, half = m // (2 * VU), m // 2 % VU, m % 2
                        if m % (2 * VU) == 0:
                            pe.wait_ge(w_loaded[u], 32 * i + 32)
                        pe.wait_ge(act_ready, 4 * VU * i + m + 1)
                        for f in range(2):
                            lo = (2 * half + f) * P
                            ins = pe.matmul(psum[:, 2 * (m % 3) + f, 0:W], w1[u][:, lo:lo + P], hnT[:, c * W:(c + 1) * W],
                                            start=True, stop=True)
                        ins.then_inc(up_ps, 1)

                    def down(v):
                        u = v // VU
                        pe.wait_ge(act_ready, 4 * VU * i + 2 * v + 5)
                        pe.wait_ge(added, 2 * VU * i + v + 1)
                        for t in range(TC):
                            for f in range(NC):
                                ins = pe.matmul(psum[:, 6 + v % 2, t * P:(t + 1) * P], actT[v % 2][:, f, t * P:(t + 1) * P],
                                                w2[u][:, f, :], start=(f == 0), stop=(f == NC - 1))
                        ins.then_inc(down_done, 1)

                    up(0)
                    up(1)
                    for v in range(2 * VU):
                        if v + 1 < 2 * VU:
                            up(2 * v + 2)
                            up(2 * v + 3)
                        down(v)


def column_attention(nc, w, hidden, ident, consts, psum):
    HALF = T // 2
    with ExitStack() as ctx:
        def sb(name, shape, n=1, dt=F32):
            t = [ctx.enter_context(nc.sbuf_tensor(f"{name}{u}", shape, dt)) for u in range(n)]
            return t if n > 1 else t[0]

        def sem(name):
            return ctx.enter_context(nc.semaphore(name))

        hn, hnT = sb("ca_hn", [P, NJ, P]), sb("ca_hnT", [P, TP])
        stats, moments, rstd = sb("ca_stats", [P, NJ, 6]), sb("ca_moments", [P, NJ, 2]), sb("ca_rstd", [P, NJ])
        wq, wk, wv = sb("ca_wq", [P, P]), sb("ca_wk", [P, P]), sb("ca_wv", [P, P])
        qT, kT, v = sb("ca_qT", [P, TP]), sb("ca_kT", [P, TP]), sb("ca_v", [P, NJ, P])
        v_scaled = sb("ca_v_scaled", [P, NJ, P])
        prob = sb("ca_prob", [P, NJ, T])
        minus_max, sums, recip = sb("ca_minus_max", [P, NJ]), sb("ca_sums", [P, NJ]), sb("ca_recip", [P, NJ])

        weights_in = sem("ca_weights_in")
        norm = [sem(f"ca_norm_{s}") for s in ("stats", "moments", "rstd", "out")]
        hnT_ps, hnT_ready, proj_ps = sem("ca_hnT_ps"), sem("ca_hnT_ready"), sem("ca_proj_ps")
        q_ready, kv_ready = sem("ca_q_ready"), sem("ca_kv_ready")
        score_ps, max_ready, prob_ready = sem("ca_score_ps"), sem("ca_max_ready"), sem("ca_prob_ready")
        recip_ready, v_scaled_ready = sem("ca_recip_ready"), sem("ca_v_scaled_ready")
        out_ps, h_ready = sem("ca_out_ps"), sem("ca_h_ready")
        flat = psum[:, :, :].rearrange("p k n -> p (k n)")

        def pair(k):
            return flat[:, k * 512:k * 512 + TP]

        with nc.Block() as block:
            @block.sync
            def _(sp):
                for dst, src in ((wq, w["wqT"]), (wk, w["wkT"]), (wv, w["wvT"])):
                    sp.dma_start(dst[:, :], src).then_inc(weights_in, 16)

            @block.gpsimd
            def _(pool):
                with pool.Fori(0, B) as b:
                    invert_deviation(pool, moments, rstd, consts, norm, b + 1)

            @block.tensor
            def _(pe):
                pe.wait_ge(weights_in, 48)
                with pe.Fori(0, B) as b:
                    pe.wait_ge(norm[3], b + 1)
                    pe.wait_ge(h_ready, 2 * b + 2)
                    for j in range(NJ):
                        ins = pe.transpose(pair(6)[:, j * P:(j + 1) * P], hn[:, j, :], ident)
                    ins.then_inc(hnT_ps, 1)
                    pe.wait_ge(hnT_ready, b + 1)
                    for k, wt in ((0, wq), (2, wk)):
                        for h in range(2):
                            ins = pe.matmul(psum[:, k + h, 0:TP // 2], wt[:, :], hnT[:, h * TP // 2:(h + 1) * TP // 2],
                                            start=True, stop=True)
                        ins.then_inc(proj_ps, 1)
                    for j in range(NJ):
                        ins = pe.matmul(pair(4)[:, j * P:(j + 1) * P], hnT[:, j * P:(j + 1) * P], wv[:, :], start=True, stop=True)
                    ins.then_inc(proj_ps, 1)
                    pe.wait_ge(q_ready, b + 1)
                    for k in range(NJ):
                        if k == 0:
                            pe.wait_ge(kv_ready, 2 * b + 1)
                        if k == 2:
                            pe.wait_ge(kv_ready, 2 * b + 2)
                        if k >= 3:
                            pe.wait_ge(prob_ready, NJ * b + k - 2)
                        for h in range(2):
                            ins = pe.matmul(psum[:, 2 * (k % 3) + h, 0:HALF], kT[:, k * P:(k + 1) * P], qT[:, h * HALF:(h + 1) * HALF],
                                            start=True, stop=True)
                        ins.then_inc(score_ps, 1)
                    pe.wait_ge(v_scaled_ready, NJ * b + NJ)
                    for j in range(NJ):
                        rows = min(P, T - j * P)
                        for k in range(NJ):
                            ins = pe.matmul(pair(6)[0:rows, j * P:(j + 1) * P], prob[:, k, j * P:j * P + rows], v_scaled[:, k, :],
                                            start=(k == 0), stop=(k == NJ - 1))
                    ins.then_inc(out_ps, 1)

            @block.scalar
            def _(act):
                with act.Fori(0, B) as b:
                    act.wait_ge(hnT_ps, b + 1)
                    act.activation(hnT[:, :], pair(6), ACT.Copy).then_inc(hnT_ready, 1)
                    act.wait_ge(proj_ps, 3 * b + 1)
                    act.activation(qT[:, :].rearrange("p (h n) -> p h n", h=2), psum[:, 0:2, 0:TP // 2], ACT.Copy).then_inc(q_ready, 1)
                    for k in range(NJ):
                        act.wait_ge(max_ready, NJ * b + k + 1)
                        act.activation(prob[:, k, :].rearrange("p (h n) -> p h n", h=2), psum[:, 2 * (k % 3):2 * (k % 3) + 2, 0:HALF],
                                       ACT.Exp, bias=minus_max[:, k:k + 1], accum_out=sums[:, k:k + 1]).then_inc(prob_ready, 1)

            @block.vector
            def _(dve):
                dve.memset(minus_max[:, :], 0.0).then_inc(h_ready, 2)
                with dve.Fori(0, B) as b:
                    normalise(dve, consts, hidden[:, bass.ds(b * NJ, NJ), :], hn, stats, moments, rstd, norm, b + 1)
                    dve.wait_ge(proj_ps, 3 * b + 2)
                    dve.tensor_copy(kT[:, :].rearrange("p (h n) -> p h n", h=2), psum[:, 2:4, 0:TP // 2]).then_inc(kv_ready, 1)
                    dve.wait_ge(proj_ps, 3 * b + 3)
                    dve.tensor_copy(v[:, :, :].rearrange("p j n -> p (j n)"), pair(4)).then_inc(kv_ready, 1)

                    def scale_value(k):
                        dve.wait_ge(prob_ready, NJ * b + k + 1)
                        dve.reciprocal(recip[:, k:k + 1], sums[:, k:k + 1]).then_inc(recip_ready, 1)
                        dve.wait_ge(recip_ready, NJ * b + k + 1)
                        dve.wait_ge(kv_ready, 2 * b + 2)
                        dve.tensor_scalar(v_scaled[:, k, :], v[:, k, :], recip[:, k:k + 1], None, ALU.mult).then_inc(v_scaled_ready, 1)

                    for k in range(NJ):
                        dve.wait_ge(score_ps, NJ * b + k + 1)
                        dve.tensor_reduce(minus_max[:, k:k + 1], psum[:, 2 * (k % 3):2 * (k % 3) + 2, 0:HALF], AX.XY, ALU.max,
                                          negate=True).then_inc(max_ready, 1)
                        if k >= 1:
                            scale_value(k - 1)
                    scale_value(NJ - 1)
                    dve.wait_ge(out_ps, b + 1)
                    dve.tensor_tensor(hidden[:, bass.ds(b * NJ, NJ - 1), :], pair(6)[:, 0:(NJ - 1) * P].rearrange("p (j n) -> p j n", n=P),
                                      hidden[:, bass.ds(b * NJ, NJ - 1), :], ALU.add).then_inc(h_ready, 1)
                    dve.tensor_tensor(hidden[0:LAST, bass.ds(b * NJ + NJ - 1, 1), :],
                                      pair(6)[0:LAST, (NJ - 1) * P:TP].rearrange("p (j n) -> p j n", n=P),
                                      hidden[0:LAST, bass.ds(b * NJ + NJ - 1, 1), :], ALU.add).then_inc(h_ready, 1)


def route(nc, w, hidden, ident, consts, psum, hn_all, slot, weight, expert_of):
    NT, K = B * NJ, PG1
    SETS = 1 + G1
    N = NT * SETS
    with ExitStack() as ctx:
        def sb(name, shape, n=1, dt=F32):
            t = [ctx.enter_context(nc.sbuf_tensor(f"{name}{u}", shape, dt)) for u in range(n)]
            return t if n > 1 else t[0]

        def sem(name):
            return ctx.enter_context(nc.semaphore(name))

        stats, moments, rstd = sb("ro_stats", [P, NJ, 6]), sb("ro_moments", [P, NJ, 2]), sb("ro_rstd", [P, NJ])
        hn = sb("ro_hn", [P, NJ, P])
        hnT = sb("ro_hnT", [P, TP])
        wg, bias = sb("ro_wg", [P, SETS * K]), sb("ro_bias", [P, SETS * K])
        prob, first, second, rest = (sb(f"ro_{s}", [P, N, K]) for s in ("prob", "first", "second", "rest"))
        top, total, inv, next_, both, seen, w_first, w_second = (
            sb(f"ro_{s}", [P, N]) for s in ("top", "total", "inv", "next", "both", "seen", "w_first", "w_second"))

        one_hot = sb("ro_one_hot", [P, 4, NT, E1])
        sel, cum, scan = sb("ro_sel", [P, NT, E1]), sb("ro_cum", [P, NT, E1]), sb("ro_scan", [P, NT, E1], 2)
        within = sb("ro_within", [P, 2, NT, K])
        before, ones = sb("ro_before", [P, P]), sb("ro_ones", [P, P])
        count_i = sb("ro_count_i", [P, E1], dt=I32)
        padded, start, ends = sb("ro_padded", [P, E1]), sb("ro_start", [P, E1], 2), sb("ro_ends", [P, E1])
        slot_f = sb("ro_slot_f", [P, 4, NT])
        block_row, expert_f = sb("ro_block_row", [1, BLOCKS]), sb("ro_expert_f", [1, BLOCKS])

        weights_in = sem("ro_weights_in")
        sel_ready, rank_ps = sem("ro_sel_ready"), sem("ro_rank_ps")
        norm = [sem(f"ro_norm_{s}") for s in ("stats", "moments", "rstd", "out")]
        hnT_ps, hnT_ready, kept = sem("ro_hnT_ps"), sem("ro_hnT_ready"), sem("ro_hn_kept")
        logits_ps, logits_ready, exp_ready, chain = sem("ro_logits_ps"), sem("ro_logits_ready"), sem("ro_exp_ready"), sem("ro_chain")
        shifted = sem("ro_shifted")
        flat = psum[:, :, :].rearrange("p k n -> p (k n)")
        hnT_bank = flat[:, 0:TP]
        logits_bank = psum[:, 2, 0:NJ * SETS * K]

        def over(row):
            return row[:, :].rearrange("p (n o) -> p n o", o=1).broadcast_to([P, N, K])

        with nc.Block() as block:
            @block.sync
            def _(sp):
                sp.dma_start(wg[:, :], w["wgate"]).then_inc(weights_in, 16)
                sp.dma_start(bias[:, :], w["bgate"].broadcast_to([P, SETS * K])).then_inc(weights_in, 16)
                sp.dma_start(before[:, :], w["before"]).then_inc(weights_in, 16)
                sp.dma_start(block_row[:, :], w["block_row"]).then_inc(weights_in, 16)

            @block.gpsimd
            def _(pool):
                with pool.Fori(0, B) as b:
                    invert_deviation(pool, moments, rstd, consts, norm, b + 1)

            @block.tensor
            def _(pe):
                pe.wait_ge(weights_in, 64)
                with pe.Fori(0, B) as b:
                    pe.wait_ge(norm[3], b + 1)
                    for j in range(NJ):
                        ins = pe.transpose(hnT_bank[:, j * P:(j + 1) * P], hn[:, j, :], ident)
                    ins.then_inc(hnT_ps, 1)
                    pe.wait_ge(hnT_ready, b + 1)
                    pe.wait_ge(logits_ready, b + 1)
                    for j in range(NJ):
                        ins = pe.matmul(logits_bank[:, j * SETS * K:(j + 1) * SETS * K], hnT[:, j * P:(j + 1) * P], wg[:, :],
                                        start=True, stop=True)
                    ins.then_inc(logits_ps, 1)
                pe.wait_ge(sel_ready, 1)
                sel_cols = sel[:, :, :].rearrange("p t e -> p (t e)")
                for k, lhsT in ((0, before), (4, ones)):
                    for lo in range(0, NT * E1, 512):
                        hi = min(lo + 512, NT * E1)
                        ins = pe.matmul(psum[:, k + lo // 512, 0:hi - lo], lhsT[:, :], sel_cols[:, lo:hi], start=True, stop=True)
                ins.then_inc(rank_ps, 1)

            @block.scalar
            def _(act):
                with act.Fori(0, B) as b:
                    act.wait_ge(hnT_ps, b + 1)
                    act.activation(hnT[:, :], hnT_bank, ACT.Copy).then_inc(hnT_ready, 1)
                    act.activation(hn_all[:, bass.ds(b * NJ, NJ), :], hn[:, :, :], ACT.Copy).then_inc(kept, 1)
                act.wait_ge(shifted, 1)
                act.activation(prob[:, :, :], prob[:, :, :], ACT.Exp).then_inc(exp_ready, 1)

            @block.vector
            def _(dve):
                done = 0

                def link(ins):
                    nonlocal done
                    done += 1
                    ins.then_inc(chain, 1)
                    dve.wait_ge(chain, done)

                def choose(values, best, out):
                    link(dve.tensor_tensor(out[:, :, :], values[:, :, :], over(best), ALU.is_equal))
                    link(dve.tensor_tensor(seen[:, :], out[:, :, 0], out[:, :, 1], ALU.max))
                    link(dve.tensor_tensor(out[:, :, 1], out[:, :, 1], out[:, :, 0], ALU.is_gt))
                    link(dve.tensor_tensor(both[:, :], seen[:, :], out[:, :, 2], ALU.max))
                    link(dve.tensor_tensor(out[:, :, 2], out[:, :, 2], seen[:, :], ALU.is_gt))
                    link(dve.tensor_tensor(out[:, :, 3], out[:, :, 3], both[:, :], ALU.is_gt))

                dve.wait_ge(weights_in, 64)
                dve.memset(seen[:, :], 0.0).then_inc(logits_ready, 1)
                dve.memset(both[:, :], 0.0).then_inc(kept, 1)
                with dve.Fori(0, B) as b:
                    dve.wait_ge(kept, b + 1)
                    normalise(dve, consts, hidden[:, bass.ds(b * NJ, NJ), :], hn, stats, moments, rstd, norm, b + 1)
                    dve.wait_ge(logits_ps, b + 1)
                    dve.tensor_tensor(prob[:, bass.ds(b * NJ * SETS, NJ * SETS), :].rearrange("p (j s) k -> p j (s k)", s=SETS),
                                      logits_bank.rearrange("p (j n) -> p j n", j=NJ),
                                      bias[:, :].rearrange("p (o n) -> p o n", o=1).broadcast_to([P, NJ, SETS * K]),
                                      ALU.add).then_inc(logits_ready, 1)
                dve.wait_ge(logits_ready, B + 1)
                link(dve.tensor_reduce(top[:, :], prob[:, :, :], AX.X, ALU.max))
                dve.tensor_tensor(prob[:, :, :], prob[:, :, :], over(top), ALU.subtract).then_inc(shifted, 1)
                dve.wait_ge(exp_ready, 1)
                link(dve.tensor_reduce(total[:, :], prob[:, :, :], AX.X, ALU.add))
                link(dve.reciprocal(inv[:, :], total[:, :]))
                link(dve.tensor_tensor(prob[:, :, :], prob[:, :, :], over(inv), ALU.mult))
                link(dve.tensor_reduce(top[:, :], prob[:, :, :], AX.X, ALU.max))
                choose(prob, top, first)
                link(dve.scalar_tensor_tensor(out=rest[:, :, :], in0=first[:, :, :], scalar=-2.0, in1=prob[:, :, :],
                                              op0=ALU.mult, op1=ALU.add))
                link(dve.tensor_reduce(next_[:, :], rest[:, :, :], AX.X, ALU.max))
                choose(rest, next_, second)
                link(dve.tensor_tensor(total[:, :], top[:, :], next_[:, :], ALU.add))
                link(dve.scalar_tensor_tensor(out=next_[:, :], in0=total[:, :], scalar=THRESHOLD, in1=next_[:, :],
                                              op0=ALU.is_le, op1=ALU.mult))
                link(dve.tensor_tensor(total[:, :], top[:, :], next_[:, :], ALU.add))
                link(dve.tensor_scalar(total[:, :], total[:, :], 1e-9, None, ALU.add))
                link(dve.reciprocal(inv[:, :], total[:, :]))
                link(dve.tensor_tensor(w_first[:, :], top[:, :], inv[:, :], ALU.mult))
                link(dve.tensor_tensor(w_second[:, :], next_[:, :], inv[:, :], ALU.mult))
                picks = [x[:, :, :].rearrange("p (t s) k -> p t s k", s=SETS) for x in (first, second)]
                shares = [x[:, :].rearrange("p (t s) -> p t s", s=SETS) for x in (w_first, w_second)]
                for a in range(2):
                    for c in range(2):
                        link(dve.tensor_tensor(within[:, c, :, :], picks[a][:, :, 0, :], shares[c][:, :, 1:], ALU.mult))
                        link(dve.tensor_reduce(slot_f[:, 2 * a + c, :], within[:, c, :, :], AX.X, ALU.add))
                        link(dve.scalar_tensor_tensor(out=weight[:, 2 * a + c, :], in0=slot_f[:, 2 * a + c, :], scalar=G1 ** -0.5,
                                                      in1=shares[a][:, :, 0], op0=ALU.mult, op1=ALU.mult))
                        for g in range(G1):
                            ins = dve.tensor_tensor(one_hot[:, 2 * a + c, :, g * K:(g + 1) * K], picks[c][:, :, 1 + g, :],
                                                    picks[a][:, :, 0, g:g + 1].broadcast_to([P, NT, K]), ALU.mult)
                        link(ins)
                link(dve.tensor_tensor(sel[:, :, :], one_hot[:, 0, :, :], one_hot[:, 1, :, :], ALU.add))
                link(dve.tensor_tensor(sel[:, :, :], sel[:, :, :], one_hot[:, 2, :, :], ALU.add))
                link(dve.memset(ones[:, :], 1.0))
                dve.tensor_tensor(sel[:, :, :], sel[:, :, :], one_hot[:, 3, :, :], ALU.add).then_inc(sel_ready, 1)
                dve.wait_ge(rank_ps, 1)
                in_tile = flat[:, 0:NT * E1].rearrange("p (t e) -> p t e", e=E1)
                of_tile = flat[:, 2048:2048 + NT * E1].rearrange("p (t e) -> p t e", e=E1)
                link(dve.tensor_copy(scan[0][:, :, :], of_tile))
                step, at = 1, 0
                while step < NT:
                    link(dve.tensor_copy(scan[1 - at][:, 0:step, :], scan[at][:, 0:step, :]))
                    link(dve.tensor_tensor(scan[1 - at][:, step:, :], scan[at][:, step:, :], scan[at][:, 0:NT - step, :], ALU.add))
                    step, at = 2 * step, 1 - at
                total_of = scan[at][:, NT - 1, :]
                link(dve.tensor_tensor(cum[:, :, :], scan[at][:, :, :], of_tile, ALU.subtract))
                link(dve.tensor_tensor(cum[:, :, :], cum[:, :, :], in_tile, ALU.add))
                link(dve.tensor_scalar(padded[:, :], total_of, float(P - 1), None, ALU.add))
                link(dve.tensor_copy(count_i[:, :], padded[:, :]))
                link(dve.tensor_scalar(count_i[:, :], count_i[:, :], -P, None, ALU.bitwise_and))
                link(dve.tensor_copy(padded[:, :], count_i[:, :]))
                link(dve.tensor_copy(start[0][:, :], padded[:, :]))
                step, at = 1, 0
                while step < E1:
                    link(dve.tensor_copy(start[1 - at][:, 0:step], start[at][:, 0:step]))
                    link(dve.tensor_tensor(start[1 - at][:, step:], start[at][:, step:], start[at][:, 0:E1 - step], ALU.add))
                    step, at = 2 * step, 1 - at
                link(dve.tensor_copy(ends[:, :], start[at][:, :]))
                link(dve.tensor_tensor(start[at][:, :], ends[:, :], padded[:, :], ALU.subtract))
                link(dve.tensor_tensor(cum[:, :, :], cum[:, :, :],
                                       start[at][:, :].rearrange("p (o e) -> p o e", o=1).broadcast_to([P, NT, E1]), ALU.add))
                for r in range(4):
                    link(dve.tensor_tensor(one_hot[:, r, :, :], one_hot[:, r, :, :], cum[:, :, :], ALU.mult))
                    link(dve.tensor_reduce(slot_f[:, r, :], one_hot[:, r, :, :], AX.X, ALU.add))
                link(dve.tensor_copy(slot[:, :, :], slot_f[:, :, :]))
                link(dve.memset(expert_f[:, :], 0.0))
                for e in range(E1 - 1):
                    link(dve.scalar_tensor_tensor(out=expert_f[:, :], in0=block_row[:, :], scalar=ends[0:1, e:e + 1],
                                                  in1=expert_f[:, :], op0=ALU.is_ge, op1=ALU.add))
                link(dve.tensor_copy(expert_of[:, :], expert_f[:, :]))


def grouped_ffn(nc, w, hidden, ident, consts, psum):
    NT, NC = B * NJ, F1 // P
    ZB = 16
    assert BLOCKS % ZB == 0
    with ExitStack() as ctx:
        def sb(name, shape, n=1, dt=F32, stack=ctx):
            t = [stack.enter_context(nc.sbuf_tensor(f"{name}{u}", shape, dt)) for u in range(n)]
            return t if n > 1 else t[0]

        def sem(name):
            return ctx.enter_context(nc.semaphore(name))

        slot, weight = sb("gf_slot", [P, CHOICES, NT], dt=I32), sb("gf_weight", [P, CHOICES, NT])
        expert_of = sb("gf_expert_of", [1, BLOCKS], dt=I32)
        w1, w3 = sb("gf_w1", [P, E1, F1]), sb("gf_w3", [P, E1, F1])
        x_rows = nc.dram_tensor("x_by_slot", (BLOCKS * P, D), F32, kind="Internal").ap()
        y_rows = nc.dram_tensor("y_by_slot", (BLOCKS * P, D), F32, kind="Internal").ap()
        w13_loaded = sem("gf_w13_loaded")

        with ExitStack() as inner:
            hn_all = sb("gf_hn_all", [P, NT, P], stack=inner)
            zeros = sb("gf_zeros", [P, ZB * P], stack=inner)
            zero_set, rows_zeroed, scattered = sem("gf_zero_set"), sem("gf_rows_zeroed"), sem("gf_scattered")
            with nc.Block() as block:
                @block.vector
                def _(dve):
                    dve.memset(zeros[:, :], 0.0).then_inc(zero_set, 1)

                @block.sync
                def _(sp):
                    sp.wait_ge(zero_set, 1)
                    for n in range(BLOCKS // ZB):
                        sp.dma_start(x_rows[n * ZB * P:(n + 1) * ZB * P, :].rearrange("(p k) d -> p (k d)", p=P),
                                     zeros[:, :]).then_inc(rows_zeroed, 16)
                    for e in range(E1):
                        sp.dma_start(w1[:, e, :], w["W1"][e]).then_inc(w13_loaded, 16)
                        sp.dma_start(w3[:, e, :], w["W3"][e]).then_inc(w13_loaded, 16)

            route(nc, w, hidden, ident, consts, psum, hn_all, slot, weight, expert_of)

            with nc.Block() as block:
                @block.gpsimd
                def _(pool):
                    pool.wait_ge(rows_zeroed, 16 * (BLOCKS // ZB))
                    for tile in range(NT):
                        for r in range(CHOICES):
                            pool.indirect_dma_start(
                                x_rows, bass.IndirectOffsetOnAxis(slot[:, r, tile:tile + 1], 0),
                                hn_all[:, tile, :], None).then_inc(scattered, 16)
                    pool.wait_ge(scattered, 16 * CHOICES * NT)

        expert_blocks(nc, w, ident, psum, expert_of, w1, w3, w13_loaded, x_rows, y_rows)

        with ExitStack() as inner:
            GB = 4
            rows = sb("gf_rows", [P, CHOICES, P], GB, stack=inner)
            gathered, added, chain = [sem(f"gf_gathered{u}") for u in range(GB)], sem("gf_added"), sem("gf_chain")
            with nc.Block() as block:
                @block.gpsimd
                def _(pool):
                    for tile in range(NT):
                        if tile >= GB:
                            pool.wait_ge(added, tile - GB + 1)
                        for r in range(CHOICES):
                            pool.indirect_dma_start(
                                rows[tile % GB][:, r, :], None, y_rows,
                                bass.IndirectOffsetOnAxis(slot[:, r, tile:tile + 1], 0)).then_inc(gathered[tile % GB], 16)

                @block.vector
                def _(dve):
                    for tile in range(NT):
                        dve.wait_ge(gathered[tile % GB], 16 * CHOICES * (tile // GB + 1))
                        for r in range(CHOICES):
                            ins = dve.scalar_tensor_tensor(out=hidden[:, tile, :], in0=rows[tile % GB][:, r, :],
                                                           scalar=weight[:, r, tile:tile + 1], in1=hidden[:, tile, :],
                                                           op0=ALU.mult, op1=ALU.add)
                            if r < CHOICES - 1:
                                ins.then_inc(chain, 1)
                                dve.wait_ge(chain, tile * (CHOICES - 1) + r + 1)
                        ins.then_inc(added, 1)


def expert_blocks(nc, w, ident, psum, expert_of, w1, w3, w13_loaded, x_rows, y_rows):
    NC, LASTB = F1 // P, BLOCKS - 1
    with ExitStack() as ctx:
        def sb(name, shape, n=1, dt=F32):
            t = [ctx.enter_context(nc.sbuf_tensor(f"{name}{u}", shape, dt)) for u in range(n)]
            return t if n > 1 else t[0]

        def sem(name):
            return ctx.enter_context(nc.semaphore(name))

        w2 = sb("eb_w2", [P, E1 * NC, P])
        x_in, xT = sb("eb_x", [P, P], 2), sb("eb_xT", [P, P], 2)
        silu, product, productT = sb("eb_silu", [P, F1], 2), sb("eb_product", [P, F1], 2), sb("eb_productT", [P, F1], 2)
        y = sb("eb_y", [P, P], 2)
        w2_loaded = sem("eb_w2_loaded")
        x_loaded, y_stored = [sem(f"eb_x_loaded{u}") for u in range(2)], [sem(f"eb_y_stored{u}") for u in range(2)]
        xT_ps, xT_ready, up_ps, silu_ready, product_ready, productT_ps, productT_ready, y_ps, y_ready = (
            sem(f"eb_{s}") for s in ("xT_ps", "xT_ready", "up_ps", "silu_ready", "product_ready", "productT_ps",
                                     "productT_ready", "y_ps", "y_ready"))
        x_blocks = x_rows.rearrange("(n p) d -> n p d", p=P)
        y_blocks = y_rows.rearrange("(n p) d -> n p d", p=P)

        def steps(eng, step):
            for n in (0, 1):
                step(n, n, 0)
            with eng.Fori(1, BLOCKS // 2 - 1) as pair:
                for u in range(2):
                    step(2 * pair + u, u, pair)
            for n in range(BLOCKS - 2, BLOCKS + 2):
                step(n, n % 2, n // 2)

        def has(n, shift):
            return not isinstance(n, int) or 0 <= n + shift <= LASTB

        with nc.Block() as block:
            @block.sync
            def _(sp):
                for e in range(E1):
                    sp.dma_start(w2[:, e * NC:(e + 1) * NC, :], w["W2"][e].rearrange("(k p) d -> p k d", p=P)).then_inc(w2_loaded, 16)
                for u in range(2):
                    sp.dma_start(x_in[u][:, :], x_blocks[u]).then_inc(x_loaded[u], 16)

                def step(n, u, pair):
                    if has(n, 2):
                        sp.wait_ge(xT_ps, n + 1)
                        sp.dma_start(x_in[u][:, :], x_blocks[n + 2]).then_inc(x_loaded[u], 16)
                    if has(n, -2):
                        sp.wait_ge(y_ready, n)
                        sp.dma_start(y_blocks[n - 2], y[u][:, :]).then_inc(y_stored[u], 16)

                steps(sp, step)
                for u in range(2):
                    sp.wait_ge(y_stored[u], 16 * (BLOCKS // 2 + 1))

            @block.tensor
            def _(pe):
                def turn_input(n, u):
                    ins = pe.transpose(psum[:, 6, 0:P], x_in[u][:, :], ident)
                    ins.then_inc(xT_ps, 1)

                def expert(n):
                    where = slice(n, n + 1) if isinstance(n, int) else bass.ds(n, 1)
                    return pe.value_load(expert_of[0:1, where], min_val=0, max_val=E1 - 1)

                def step(n, u, pair):
                    if has(n, 1):
                        pe.wait_ge(x_loaded[1 - u], 16 * (pair + u + 1))
                        pe.wait_ge(xT_ready, n + 1)
                        turn_input(n + 1, 1 - u)
                    if has(n, 0):
                        pe.wait_ge(xT_ready, n + 1)
                        e = expert(n)
                        for k, wt in ((u, w1), (2 + u, w3)):
                            ins = pe.matmul(psum[:, k, :], xT[u][:, :], wt[:, bass.ds(e, 1), :], start=True, stop=True)
                        ins.then_inc(up_ps, 1)
                    if has(n, -1):
                        pe.wait_ge(product_ready, n)
                        for f in range(NC):
                            ins = pe.transpose(psum[:, 4 + (1 - u), f * P:(f + 1) * P], product[1 - u][:, f * P:(f + 1) * P], ident)
                        ins.then_inc(productT_ps, 1)
                    if has(n, -2):
                        pe.wait_ge(productT_ready, n - 1)
                        pe.wait_ge(y_ready, n - 1)
                        e = expert(n - 2)
                        for f in range(NC):
                            ins = pe.matmul(psum[:, 7, 0:P], productT[u][:, f * P:(f + 1) * P],
                                            w2[:, bass.ds(e * NC + f, 1), :], start=(f == 0), stop=(f == NC - 1))
                        ins.then_inc(y_ps, 1)

                pe.wait_ge(w13_loaded, 32 * E1)
                pe.wait_ge(x_loaded[0], 16)
                turn_input(0, 0)
                pe.wait_ge(w2_loaded, 16 * E1)
                steps(pe, step)

            @block.scalar
            def _(act):
                def step(n, u, pair):
                    if has(n, 0):
                        act.wait_ge(up_ps, n + 1)
                        act.activation(silu[u][:, :], psum[:, u, :], ACT.Silu).then_inc(silu_ready, 1)
                    if has(n, -1):
                        act.wait_ge(productT_ps, n)
                        act.activation(productT[1 - u][:, :], psum[:, 4 + (1 - u), :], ACT.Copy).then_inc(productT_ready, 1)

                steps(act, step)

            @block.vector
            def _(dve):
                dve.memset(y[0][:, :], 0.0).then_inc(y_stored[0], 16)
                dve.memset(y[1][:, :], 0.0).then_inc(y_stored[1], 16)
                dve.memset(xT[0][:, 0:1], 0.0).then_inc(y_ready, 1)
                dve.wait_ge(y_ready, 1)
                dve.wait_ge(xT_ps, 1)
                dve.tensor_copy(xT[0][:, :], psum[:, 6, 0:P]).then_inc(xT_ready, 1)

                def step(n, u, pair):
                    if has(n, 1):
                        dve.wait_ge(xT_ps, n + 2)
                        dve.tensor_copy(xT[1 - u][:, :], psum[:, 6, 0:P]).then_inc(xT_ready, 1)
                    if has(n, 0):
                        dve.wait_ge(silu_ready, n + 1)
                        dve.tensor_tensor(product[u][:, :], silu[u][:, :], psum[:, 2 + u, :], ALU.mult).then_inc(product_ready, 1)
                    if has(n, -2):
                        dve.wait_ge(y_ps, n - 1)
                        dve.wait_ge(y_stored[u], 16 * pair)
                        dve.tensor_copy(y[u][:, :], psum[:, 7, 0:P]).then_inc(y_ready, 1)

                steps(dve, step)


def store(nc, hidden, out):
    with nc.semaphore("st_stored") as stored, nc.Block() as block:
        @block.sync
        def _(sp):
            for b in range(B):
                whole, rest = batch_rows(out, b)
                sp.dma_start(whole, hidden[:, b * NJ:(b + 1) * NJ - 1, :]).then_inc(stored, 16)
                sp.dma_start(rest, hidden[0:LAST, (b + 1) * NJ - 1, :]).then_inc(stored, 16)
            sp.wait_ge(stored, 32 * B)


class Consts:
    pass


def audio_tower(nc, a, out):
    with ExitStack() as ctx:
        hidden = ctx.enter_context(nc.sbuf_tensor("hidden", [P, B * NJ, P], F32))
        ident_sb = ctx.enter_context(nc.sbuf_tensor("ident", [P, P], F32))
        psum = ctx.enter_context(nc.psum_tensor("psum", [P, 8, 512], F32))
        consts = Consts()
        consts.minus_half = ctx.enter_context(nc.sbuf_tensor("minus_half", [P, 16], F32))
        consts.eps = ctx.enter_context(nc.sbuf_tensor("eps", [P, 16], F32))
        consts.carrier = ctx.enter_context(nc.sbuf_tensor("wait_carrier", [P, 8], F32))
        consts.loaded = ctx.enter_context(nc.semaphore("ident_loaded"))
        ident = ident_sb[:, :]
        with nc.Block() as block:
            @block.sync
            def _(sp):
                sp.dma_start(ident, a["ident"]).then_inc(consts.loaded, 16)
                sp.wait_ge(consts.loaded, 16)

            @block.gpsimd
            def _(pool):
                pool.memset(consts.minus_half[:, :], -0.5)
                pool.memset(consts.eps[:, :], EPS)
        token_mixer(nc, a["x"], a, hidden, ident, consts, psum)
        rope_attention(nc, a, hidden, ident, consts, psum)
        routed_ffn(nc, a, hidden, ident, consts, psum)
        column_attention(nc, a, hidden, ident, consts, psum)
        grouped_ffn(nc, a, hidden, ident, consts, psum)
        store(nc, hidden, out)


def rope_tables():
    cos, sin = np.zeros((P, 3, TP), np.float32), np.zeros((P, 3, TP), np.float32)
    for s in range(3):
        width = D if s < 2 else GROUPS * HD
        i = np.arange(width // 2, dtype=np.float64)
        theta = 10000.0 ** (-(2.0 * (i - 1.0))) / width
        angle = np.arange(T, dtype=np.float64)[:, None] * theta[None, :]
        for g in range(GROUPS):
            for h in range(HD):
                c = (2 * g + s) * HD + h if s < 2 else g * HD + h
                cos[32 * g + h, s, 0:T] = np.cos(angle[:, c // 2]).astype(np.float32)
                sin[32 * g + h, s, 0:T] = np.sin(angle[:, c // 2]).astype(np.float32) * (1 if c % 2 == 0 else -1)
    return cos, sin


def kernel(**inputs):
    import concourse.bacc as bacc
    from concourse.bass_utils import run_bass_kernel_spmd

    g = {k: np.asarray(v) for k, v in inputs.items()}
    t0 = "L0_tok_"
    wqk = np.zeros((P, 3, 2, P), g["L0_attn_Wq"].dtype)
    for s in range(3):
        for grp in range(GROUPS):
            for h in range(HD):
                weight = g["L0_attn_Wq"] if s < 2 else g["L0_attn_Wk"]
                c = (2 * grp + s) * HD + h if s < 2 else grp * HD + h
                wqk[:, s, 0, 32 * grp + h] = weight[:, c]
                wqk[:, s, 1, 32 * grp + h] = weight[:, c ^ 1]
    cos, sin = rope_tables()
    mask = np.zeros((P, TP), np.float32)
    mask[:, TP - P:] = np.where(np.arange(P)[None, :] > np.arange(P)[:, None], MASKED, 0.0)
    arrays = {
        "x": g["x"],
        "ident": np.eye(P, dtype=np.float32),
        "wcT": g[t0 + "w_compress"][:, :, 0].T, "bc": g[t0 + "b_compress"][:, None],
        "wmT": g[t0 + "w_main"].transpose(2, 1, 0), "bm": g[t0 + "b_main"][:, None],
        "weT": np.concatenate([g[t0 + "w_expand"][:, :, 0].T, g[t0 + "b_expand"][None, :]]),
        "wf1T": g[t0 + "w_ff1"].T, "bf1": g[t0 + "b_ff1"][:, None],
        "wf2T": np.concatenate([g[t0 + "w_ff2"].T, g[t0 + "b_ff2"][None, :]]),
        "norms": np.stack([g[t0 + "g_conv_norm"], g[t0 + "b_conv_norm"], g[t0 + "g_ff_norm"], g[t0 + "b_ff_norm"]], axis=1),
        "wqk": wqk, "wv0": g["L0_attn_Wv"], "cos": cos, "sin": sin, "mask": mask,
        "ew0": g["L0_ffn_expert_weights"], "ei0": g["L0_ffn_expert_indices"],
        "w1": g["L0_ffn_w1"], "w2": g["L0_ffn_w2"],
        "wqT": g["L1_attn_Wq"].T, "wkT": g["L1_attn_Wk"].T, "wvT": g["L1_attn_Wv"].T,
        "wgate": np.concatenate([g["L1_ffn_Wr"], g["L1_ffn_Wgate"].transpose(1, 0, 2).reshape(D, E1)], axis=1),
        "bgate": np.concatenate([g["L1_ffn_br"], g["L1_ffn_bgate"].reshape(E1)])[None, :],
        "before": np.triu(np.ones((P, P), np.float32), 1), "block_row": np.arange(BLOCKS, dtype=np.float32)[None, :] * P,
        "W1": g["L1_ffn_W1"], "W3": g["L1_ffn_W3"], "W2": g["L1_ffn_W2"],
    }
    arrays = {k: np.ascontiguousarray(v) for k, v in arrays.items()}
    nc = bacc.Bacc("TRN2", target_bir_lowering=False, num_devices=1)
    aps = {k: nc.dram_tensor(f"in_{k}", v.shape, mybir.dt.from_np(v.dtype), kind="ExternalInput").ap()
           for k, v in arrays.items()}
    out = nc.dram_tensor("out", (B, T, D), F32, kind="ExternalOutput").ap()
    audio_tower(nc, aps, out)
    r = run_bass_kernel_spmd(nc, [{f"in_{k}": v for k, v in arrays.items()}], core_ids=[0])
    return r.results[0]["out"]
```

```python
from contextlib import ExitStack

import numpy as np

import concourse.bass as bass
from concourse import mybir

F32 = mybir.dt.float32
I32 = mybir.dt.int32
BF16 = mybir.dt.bfloat16
ALU = mybir.AluOpType
ACT = mybir.ActivationFunctionType
AX = mybir.AxisListType

B, T_IN, D = 8, 750, 128
T = T_IN - 2
P = 128
NJ = -(-T // P)
TP = NJ * P
LAST = T - (NJ - 1) * P
LAST_IN = T_IN - (NJ - 1) * P
BN = 64
EPS = 1e-5
HEADS, GROUPS, HD = 8, 4, 16
ATT_SCALE = HD ** -0.5
MASKED = -1.0e30
E0, TOPK0, F0, N0 = 8, 2, 512, 1024
E1, G1, PG1, F1 = 16, 4, 4, 512
CHOICES = 4
BLOCKS = (CHOICES * B * TP + E1 * (P - 1)) // P
BLOCKS += BLOCKS % 2
THRESHOLD = 0.9


def batch_rows(dram, b):
    return dram[b][0:(NJ - 1) * P].rearrange("(j p) d -> p j d", p=P), dram[b][(NJ - 1) * P:]


def normalise(dve, consts, src, out, stats, moments, rstd, sems, turn):
    stats_done, moments_done, rstd_done, out_done = sems
    tiles = src.shape[1]
    for j in range(tiles):
        ins = dve.bn_stats(stats[:, j, :], src[:, j, :])
    ins.then_inc(stats_done, 1)
    dve.wait_ge(stats_done, turn)
    dve.memset(consts.carrier[:, 0:1], 0.0)
    for j in range(tiles):
        ins = dve.bn_aggr(moments[:, j, :], stats[:, j, :])
    ins.then_inc(moments_done, 1)
    dve.wait_ge(rstd_done, turn)
    for j in range(tiles):
        ins = dve.tensor_scalar(out[:, j, :], src[:, j, :], moments[:, j, 0:1], rstd[:, j:j + 1],
                                ALU.subtract, ALU.mult)
    ins.then_inc(out_done, 1)


def invert_deviation(pool, moments, rstd, consts, sems, turn):
    stats_done, moments_done, rstd_done, _ = sems
    tiles = moments.shape[1]
    pool.wait_ge(moments_done, 2 * turn - 1)
    pool.tensor_tensor(moments[:, :, 1], moments[:, :, 1], consts.eps[:, 0:tiles], ALU.add).then_inc(moments_done, 1)
    pool.wait_ge(moments_done, 2 * turn)
    pool.tensor_tensor(rstd[:, :], moments[:, :, 1], consts.minus_half[:, 0:tiles], ALU.pow).then_inc(rstd_done, 1)


def all_moments(dve, consts, hidden, stats, moments, sems):
    stats_done, moments_done = sems[0], sems[1]
    with dve.Fori(0, B) as b:
        for j in range(NJ):
            ins = dve.bn_stats(stats[:, bass.ds(b * NJ + j, 1), :].rearrange("p o n -> p (o n)"),
                               hidden[:, bass.ds(b * NJ + j, 1), :].rearrange("p o n -> p (o n)"))
        ins.then_inc(stats_done, 1)
    dve.wait_ge(stats_done, B)
    dve.memset(consts.carrier[:, 0:1], 0.0)
    for tile in range(B * NJ):
        ins = dve.bn_aggr(moments[:, tile, :], stats[:, tile, :])
    ins.then_inc(moments_done, 1)


def all_deviations(pool, moments, rstd, consts, sems):
    moments_done, rstd_done = sems[1], sems[2]
    tiles = B * NJ
    pool.wait_ge(moments_done, 1)
    pool.tensor_tensor(moments[:, :, 1], moments[:, :, 1], consts.eps[:, 0:1].broadcast_to([P, tiles]), ALU.add).then_inc(moments_done, 1)
    pool.wait_ge(moments_done, 2)
    pool.tensor_tensor(rstd[:, :], moments[:, :, 1], consts.minus_half[:, 0:1].broadcast_to([P, tiles]), ALU.pow).then_inc(rstd_done, 1)


def apply_moments(dve, hidden, out, moments, rstd, batch, out_done):
    for j in range(NJ):
        tile = bass.ds(batch * NJ + j, 1)
        ins = dve.tensor_scalar(out[:, j, :], hidden[:, tile, :].rearrange("p o n -> p (o n)"),
                                moments[:, tile, 0:1].rearrange("p o n -> p (o n)"), rstd[:, tile], ALU.subtract, ALU.mult)
    ins.then_inc(out_done, 1)


def token_mixer(nc, x, w, hidden, ident, consts, psum):
    with ExitStack() as ctx:
        def sb(name, shape, n=2):
            return [ctx.enter_context(nc.sbuf_tensor(f"{name}{u}", shape, F32)) for u in range(n)]

        def sem(name):
            return ctx.enter_context(nc.semaphore(name))

        def two(name):
            return [sem(f"{name}{u}") for u in range(2)]

        x_in = sb("tm_x", [P, NJ, P])
        xT = sb("tm_xT", [P, TP])
        taps = sb("tm_taps", [P, T_IN + 2])
        mixed = sb("tm_mixed", [BN + 1, TP])
        y0 = sb("tm_y0", [P, NJ, P])
        yhat = sb("tm_yhat", [P, NJ, P])
        y1T = sb("tm_y1T", [P, TP])
        ff = sb("tm_ff", [BN + 1, TP])
        y2T = sb("tm_y2T", [P, TP])
        pool_a = sb("tm_pool_a", [P, TP])
        pooledT = sb("tm_pooledT", [P, TP])
        stats = sb("tm_stats", [P, NJ, 6])
        moments = sb("tm_moments", [P, NJ, 2])
        rstd = sb("tm_rstd", [P, NJ])
        wc = ctx.enter_context(nc.sbuf_tensor("tm_wc", [P, P], F32))
        wm01 = ctx.enter_context(nc.sbuf_tensor("tm_wm01", [P, BN], F32))
        wm2 = ctx.enter_context(nc.sbuf_tensor("tm_wm2", [BN, BN], F32))
        we = ctx.enter_context(nc.sbuf_tensor("tm_we", [BN + 1, P], F32))
        wf1 = ctx.enter_context(nc.sbuf_tensor("tm_wf1", [P, BN], F32))
        wf2 = ctx.enter_context(nc.sbuf_tensor("tm_wf2", [BN + 1, P], F32))
        vec = ctx.enter_context(nc.sbuf_tensor("tm_vec", [P, 7], F32))
        bc, bm, bf1, g_conv, b_conv, g_ff, b_ff = (vec[:, i:i + 1] for i in range(7))

        weights_in = sem("tm_weights_in")
        zeros_set = sem("tm_zeros_set")
        x_loaded = two("tm_x_loaded")
        xT_ps, xT_ready = sem("tm_xT_ps"), sem("tm_xT_ready")
        comp_ps, taps_ready = sem("tm_comp_ps"), sem("tm_taps_ready")
        mix_ps, mixed_ready = sem("tm_mix_ps"), sem("tm_mixed_ready")
        exp_ps, y0_ready = sem("tm_exp_ps"), sem("tm_y0_ready")
        norm1 = [sem(f"tm_norm1_{s}") for s in ("stats", "moments", "rstd", "out")]
        norm2 = [sem(f"tm_norm2_{s}") for s in ("stats", "moments", "rstd", "out")]
        y1T_ps, y1T_ready = sem("tm_y1T_ps"), sem("tm_y1T_ready")
        ff_ps, ff_ready = sem("tm_ff_ps"), sem("tm_ff_ready")
        out_ps = sem("tm_out_ps")
        y2T_ps, y2T_ready = sem("tm_y2T_ps"), sem("tm_y2T_ready")
        pool_half, pooled_ready = sem("tm_pool_half"), sem("tm_pooled_ready")
        h_ps, h_ready = sem("tm_h_ps"), sem("tm_h_ready")

        def banks(step, u):
            k = 4 * (step % 2) + 2 * u
            return psum[:, k:k + 2, :]

        def tiles_of(step, u):
            return banks(step, u).rearrange("p k n -> p (k n)")[:, 0:TP].rearrange("p (j n) -> p j n", n=P)

        HALF_IN = T_IN // 2

        with nc.Block() as block:
            @block.sync
            def _(sp):
                for dst, src in ((wc[:, 0:BN], w["wcT"]), (wc[:, BN:P], w["wcT"]),
                                 (wm01[0:BN, :], w["wmT"][0]), (wm01[BN:P, :], w["wmT"][1]), (wm2[:, :], w["wmT"][2]),
                                 (we[:, :], w["weT"]), (wf1[:, :], w["wf1T"]), (wf2[:, :], w["wf2T"]),
                                 (vec[0:BN, 0:1], w["bc"]), (vec[BN:P, 0:1], w["bc"]),
                                 (vec[0:BN, 1:2], w["bm"]), (vec[0:BN, 2:3], w["bf1"]),
                                 (vec[:, 3:7], w["norms"])):
                    sp.dma_start(dst, src).then_inc(weights_in, 16)
                sp.wait_ge(zeros_set, 1)
                for u in range(2):
                    whole, rest = batch_rows(x, u)
                    sp.dma_start(x_in[u][:, 0:NJ - 1, :], whole).then_inc(x_loaded[u], 16)
                    sp.dma_start(x_in[u][0:LAST_IN, NJ - 1, :], rest).then_inc(x_loaded[u], 16)
                with sp.Fori(1, B // 2) as i:
                    for u in range(2):
                        sp.wait_ge(y0_ready, 2 * i + u - 1)
                        whole, rest = batch_rows(x, 2 * i + u)
                        sp.dma_start(x_in[u][:, 0:NJ - 1, :], whole).then_inc(x_loaded[u], 16)
                        sp.dma_start(x_in[u][0:LAST_IN, NJ - 1, :], rest).then_inc(x_loaded[u], 16)

            @block.gpsimd
            def _(pool):
                with pool.Fori(0, B // 2) as i:
                    for norm in (norm1, norm2):
                        for u in range(2):
                            invert_deviation(pool, moments[u], rstd[u], consts, norm, 2 * i + u + 1)

            @block.tensor
            def _(pe):
                pe.wait_ge(weights_in, 16 * 13)
                pe.wait_ge(zeros_set, 2)
                with pe.Fori(0, B // 2) as i:
                    for u in range(2):
                        pe.wait_ge(x_loaded[u], 32 * i + 32)
                        pe.wait_ge(h_ready, 2 * i + u + 1)
                        for j in range(NJ):
                            ins = pe.transpose(tiles_of(0, u)[:, j, :], x_in[u][:, j, :], ident)
                        ins.then_inc(xT_ps, 1)
                    for u in range(2):
                        pe.wait_ge(xT_ready, 2 * i + u + 1)
                        for h in range(2):
                            ins = pe.matmul(banks(1, u)[:, h, 0:HALF_IN], wc[:, :], xT[u][:, h * HALF_IN:(h + 1) * HALF_IN],
                                            start=True, stop=True)
                        ins.then_inc(comp_ps, 1)
                    for u in range(2):
                        pe.wait_ge(taps_ready, 2 * (2 * i + u + 1))
                        for h in range(2):
                            pe.matmul(banks(2, u)[0:BN, h, 0:HALF_IN], wm01[:, :], taps[u][:, h * HALF_IN:(h + 1) * HALF_IN],
                                      start=True, stop=False)
                            ins = pe.matmul(banks(2, u)[0:BN, h, 0:HALF_IN], wm2[:, :],
                                            taps[u][0:BN, h * HALF_IN + 2:(h + 1) * HALF_IN + 2], start=False, stop=True)
                        ins.then_inc(mix_ps, 1)
                    for u in range(2):
                        pe.wait_ge(mixed_ready, 2 * i + u + 1)
                        for j in range(NJ):
                            ins = pe.matmul(tiles_of(3, u)[:, j, :], mixed[u][:, j * P:(j + 1) * P], we[:, :], start=True, stop=True)
                        ins.then_inc(exp_ps, 1)
                    for u in range(2):
                        pe.wait_ge(norm1[3], 2 * i + u + 1)
                        for j in range(NJ):
                            ins = pe.transpose(tiles_of(4, u)[:, j, :], yhat[u][:, j, :], ident)
                        ins.then_inc(y1T_ps, 1)
                    for u in range(2):
                        pe.wait_ge(y1T_ready, 2 * i + u + 1)
                        for h in range(2):
                            ins = pe.matmul(banks(5, u)[0:BN, h, 0:TP // 2], wf1[:, :], y1T[u][:, h * TP // 2:(h + 1) * TP // 2],
                                            start=True, stop=True)
                        ins.then_inc(ff_ps, 1)
                    for u in range(2):
                        pe.wait_ge(ff_ready, 2 * i + u + 1)
                        for j in range(NJ):
                            pe.matmul(tiles_of(6, u)[:, j, :], ff[u][:, j * P:(j + 1) * P], wf2[:, :], start=True, stop=False)
                            ins = pe.matmul(tiles_of(6, u)[:, j, :], y1T[u][:, j * P:(j + 1) * P], ident, start=False, stop=True)
                        ins.then_inc(out_ps, 1)
                    for u in range(2):
                        pe.wait_ge(norm2[3], 2 * i + u + 1)
                        for j in range(NJ):
                            ins = pe.transpose(tiles_of(7, u)[:, j, :], yhat[u][:, j, :], ident)
                        ins.then_inc(y2T_ps, 1)
                    for u in range(2):
                        pe.wait_ge(pooled_ready, 2 * i + u + 1)
                        for j in range(NJ):
                            ins = pe.transpose(tiles_of(8, u)[:, j, :], pooledT[u][:, j * P:(j + 1) * P], ident)
                        ins.then_inc(h_ps, 1)

            @block.scalar
            def _(act):
                act.wait_ge(weights_in, 16 * 13)
                act.wait_ge(zeros_set, 2)
                with act.Fori(0, B // 2) as i:
                    for u in range(2):
                        act.wait_ge(comp_ps, 2 * i + u + 1)
                        act.activation(taps[u][0:BN, 1:T_IN + 1].rearrange("p (h n) -> p h n", h=2),
                                       banks(1, u)[0:BN, :, 0:HALF_IN], ACT.Silu, bias=bc[0:BN]).then_inc(taps_ready, 1)
                        act.activation(taps[u][BN:P, 0:T_IN].rearrange("p (h n) -> p h n", h=2),
                                       banks(1, u)[BN:P, :, 0:HALF_IN], ACT.Silu, bias=bc[BN:P]).then_inc(taps_ready, 1)
                    for u in range(2):
                        act.wait_ge(mix_ps, 2 * i + u + 1)
                        act.activation(mixed[u][0:BN, 0:T_IN].rearrange("p (h n) -> p h n", h=2),
                                       banks(2, u)[0:BN, :, 0:HALF_IN], ACT.Silu, bias=bm[0:BN]).then_inc(mixed_ready, 1)
                    for u in range(2):
                        act.wait_ge(ff_ps, 2 * i + u + 1)
                        act.activation(ff[u][0:BN, :].rearrange("p (h n) -> p h n", h=2),
                                       banks(5, u)[0:BN, :, 0:TP // 2], ACT.Gelu, bias=bf1[0:BN]).then_inc(ff_ready, 1)
                    for u in range(2):
                        act.wait_ge(h_ps, 2 * i + u + 1)
                        act.activation(hidden[:, bass.ds((2 * i + u) * NJ, NJ), :], tiles_of(8, u), ACT.Copy).then_inc(h_ready, 1)

            @block.vector
            def _(dve):
                for u in range(2):
                    dve.memset(x_in[u][96:P, NJ - 1, :], 0.0)
                    dve.memset(taps[u][:, :], 0.0)
                    dve.memset(mixed[u][:, :], 0.0)
                    dve.memset(pooledT[u][:, :], 0.0)
                    dve.memset(ff[u][BN:BN + 1, :], 1.0)
                    dve.memset(pool_a[u][:, :], 0.0)
                dve.memset(y2T[0][:, :], 0.0).then_inc(zeros_set, 1)
                dve.memset(y2T[1][:, :], 0.0).then_inc(h_ready, 2)
                dve.wait_ge(zeros_set, 1)
                for u in range(2):
                    ins = dve.memset(mixed[u][BN:BN + 1, :], 1.0)
                ins.then_inc(zeros_set, 1)
                dve.wait_ge(weights_in, 16 * 13)
                with dve.Fori(0, B // 2) as i:
                    for u in range(2):
                        dve.wait_ge(xT_ps, 2 * i + u + 1)
                        dve.tensor_copy(xT[u][:, :].rearrange("p (j n) -> p j n", n=P), tiles_of(0, u)).then_inc(xT_ready, 1)
                    for u in range(2):
                        dve.wait_ge(exp_ps, 2 * i + u + 1)
                        dve.tensor_tensor(y0[u][:, :, :], tiles_of(3, u), x_in[u][:, :, :], ALU.add).then_inc(y0_ready, 1)
                        dve.wait_ge(y0_ready, 2 * i + u + 1)
                        normalise(dve, consts, y0[u], yhat[u], stats[u], moments[u], rstd[u], norm1, 2 * i + u + 1)
                    for u in range(2):
                        dve.wait_ge(y1T_ps, 2 * i + u + 1)
                        dve.tensor_scalar(y1T[u][:, :].rearrange("p (j n) -> p j n", n=P), tiles_of(4, u), g_conv, b_conv,
                                          ALU.mult, ALU.add).then_inc(y1T_ready, 1)
                    for u in range(2):
                        dve.wait_ge(out_ps, 2 * i + u + 1)
                        normalise(dve, consts, tiles_of(6, u), yhat[u], stats[u], moments[u], rstd[u], norm2, 2 * i + u + 1)
                    for u in range(2):
                        dve.wait_ge(y2T_ps, 2 * i + u + 1)
                        dve.tensor_scalar(y2T[u][:, :].rearrange("p (j n) -> p j n", n=P), tiles_of(7, u), g_ff, b_ff,
                                          ALU.mult, ALU.add).then_inc(y2T_ready, 1)
                    for u in range(2):
                        n = 2 * i + u + 1
                        dve.wait_ge(y2T_ready, n)
                        dve.tensor_tensor(pool_a[u][:, 0:T], y2T[u][:, 0:T], y2T[u][:, 1:T + 1], ALU.max).then_inc(pool_half, 1)
                        dve.wait_ge(pool_half, n)
                        dve.tensor_tensor(pooledT[u][:, 0:T], pool_a[u][:, 0:T], y2T[u][:, 2:T + 2], ALU.max).then_inc(pooled_ready, 1)



def rope_attention(nc, w, hidden, ident, consts, psum):
    UNITS = [(j, g, p) for j in range(NJ) for g in range(GROUPS) for p in range(2)]
    NU, PAIRS = len(UNITS), len(UNITS) // 2
    PREP = 8
    AFTER_UNIT = (22, 26, 28, 31, 34, 37, 40, 43)
    STATS_AT, APPLY_AT = 10, 16
    SLOTS, AT_SLOT = [], []
    for n in range(NU):
        AT_SLOT.append(len(SLOTS))
        SLOTS.append(("unit", n))
        SLOTS += [("prepare", x) for x in range(PREP) if AFTER_UNIT[x] == n]
    NS = len(SLOTS)
    with ExitStack() as ctx:
        def sb(name, shape, n=1):
            t = [ctx.enter_context(nc.sbuf_tensor(f"{name}{u}", shape, F32)) for u in range(n)]
            return t if n > 1 else t[0]

        def sem(name):
            return ctx.enter_context(nc.semaphore(name))

        hn = sb("ra_hn", [P, NJ, P])
        hnT = sb("ra_hnT", [P, TP])
        stats, moments, rstd = sb("ra_stats", [P, NJ, 6]), sb("ra_moments", [P, NJ, 2]), sb("ra_rstd", [P, NJ])
        cos, sin = sb("ra_cos", [P, 3, TP]), sb("ra_sin", [P, 3, TP])
        wqk = sb("ra_wqk", [P, 3, 2, P])
        wv = sb("ra_wv", [P, P])
        mask = sb("ra_mask", [P, TP])
        by_cos, by_sin = sb("ra_by_cos", [P, 3, TP]), sb("ra_by_sin", [P, 3, TP])
        v_next = sb("ra_v_next", [P, NJ, P])
        qk = sb("ra_qk", [P, 3, TP])
        v = sb("ra_v", [P, NJ, P])
        scaled = sb("ra_scaled", [P, TP], 3)
        least = sb("ra_least", [P, 3])
        prob = sb("ra_prob", [P, TP], 2)
        probT = sb("ra_probT", [P, NJ, 2, P], 2)
        sums = sb("ra_sums", [P, NU])
        recip = sb("ra_recip", [P, NU])
        outT = sb("ra_outT", [P, 2 * P], 2)
        att = sb("ra_att", [P, NU, HD])
        rows = sb("ra_rows", [P, NJ, P], 2)

        consts_in = sem("ra_consts_in")
        norm = [sem(f"ra_norm_{s}") for s in ("stats", "moments", "rstd", "out")]
        slot_ps, slot_read = sem("ra_slot_ps"), sem("ra_slot_read")
        k_q0_ready, q1_ready, v_ready = sem("ra_k_q0_ready"), sem("ra_q1_ready"), sem("ra_v_ready")
        prob_ready, probT_ps = sem("ra_prob_ready"), sem("ra_probT_ps")
        probT_ready = [sem("ra_probT_ready_by_vector"), sem("ra_probT_ready_by_scalar")]
        pv_done = sem("ra_pv_done")
        outT_ready, out_ps = sem("ra_outT_ready"), sem("ra_out_ps")
        recip_ready, att_ready, att_stored = sem("ra_recip_ready"), sem("ra_att_ready"), sem("ra_att_stored")
        rows_loaded, h_ready = [sem("ra_rows_loaded0"), sem("ra_rows_loaded1")], sem("ra_h_ready")
        by_head = nc.dram_tensor("att_by_head", (B, HEADS, T, HD), F32, kind="Internal").ap()
        by_row = by_head.rearrange("b h t c -> b (h t c)").rearrange("b (t d) -> b t d", d=D)

        flat = psum[:, :, :].rearrange("p k n -> p (k n)")
        HALF = TP // 2

        def bank_pair(k):
            return flat[:, k * 512:k * 512 + TP]

        def slots_before(b):
            return PREP + NS * b

        def turned_bank(n):
            return bank_pair(5 if UNITS[n][0] < 4 and n % 2 else 4)

        def slots_of(prepares):
            return [s for s in SLOTS if prepares or s[0] == "unit"]

        def slot_of(n, prepares):
            return AT_SLOT[n] if prepares else n

        with nc.Block() as block:
            @block.sync
            def _(sp):
                for dst, src in ((cos[:, :, :], w["cos"]), (sin[:, :, :], w["sin"]), (wqk[:, :, :, :], w["wqk"]),
                                 (wv[:, :], w["wv0"]), (mask[:, :], w["mask"])):
                    sp.dma_start(dst, src).then_inc(consts_in, 16)
                with sp.Fori(0, B) as b:
                    for j in range(NJ):
                        sp.wait_ge(att_ready, NJ * b + j + 3)
                        rows = min(P, T - j * P)
                        sp.dma_start(by_head[b][:, j * P:j * P + rows, :].rearrange("h t c -> t h c"),
                                     att[0:rows, j * HEADS:(j + 1) * HEADS, :]).then_inc(att_stored, 16)
                sp.wait_ge(att_stored, 16 * NJ * (B + 1))

            @block.tensor
            def _(pe):
                def prepare(x, slot, batch):
                    k = 2 * (slot % 2)
                    if x == 0:
                        pe.wait_ge(norm[3], batch + 1)
                        for j in range(NJ):
                            ins = pe.transpose(bank_pair(k)[:, j * P:(j + 1) * P], hn[:, j, :], ident)
                    elif x == 1:
                        for j in range(NJ):
                            ins = pe.matmul(bank_pair(k)[:, j * P:(j + 1) * P], hnT[:, j * P:(j + 1) * P], wv[:, :], start=True, stop=True)
                    else:
                        s, h = (x - 2) // 2, x % 2
                        for side in range(2):
                            ins = pe.matmul(psum[:, k + side, 0:HALF], wqk[:, s, side, :], hnT[:, h * HALF:(h + 1) * HALF],
                                            start=True, stop=True)
                    ins.then_inc(slot_ps, 1)

                def attend(b, prepares):
                    base, slots = slots_before(b), slots_of(prepares)

                    def fill(slot):
                        kind, n = slots[slot]
                        pe.wait_ge(slot_read, base + slot - 1)
                        if kind == "prepare":
                            if n == 1:
                                pe.wait_ge(slot_read, base + slots.index(("prepare", 0)) + 1)
                            prepare(n, slot, b + 1)
                            return
                        j, g, p = UNITS[n]
                        for lo in range(0, (j + 1) * P, 512):
                            hi = min(lo + 512, (j + 1) * P)
                            ins = pe.matmul(bank_pair(2 * (slot % 2))[:, lo:hi], qk[32 * g:32 * g + 32, p, j * P:(j + 1) * P],
                                            qk[32 * g:32 * g + 32, 2, lo:hi], start=True, stop=True)
                        ins.then_inc(slot_ps, 1)

                    def turn(n):
                        j = UNITS[n][0]
                        pe.wait_ge(prob_ready, NU * b + n + 1)
                        if n >= 2 and (j < 4 or n == 4 * HEADS):
                            pe.wait_ge(probT_ready[n % 2], PAIRS * b + n // 2)
                        if j >= 4:
                            pe.wait_ge(probT_ready[(n - 1) % 2], PAIRS * b + (n - 1) // 2 + 1)
                        for k in range(j + 1):
                            ins = pe.transpose(turned_bank(n)[:, k * P:(k + 1) * P], prob[n % 2][:, k * P:(k + 1) * P], ident)
                        ins.then_inc(probT_ps, 1)

                    def values(m):
                        j, g, _ = UNITS[2 * m]
                        pe.wait_ge(probT_ready[0], PAIRS * b + m + 1)
                        pe.wait_ge(probT_ready[1], PAIRS * b + m + 1)
                        if g == 0:
                            pe.wait_ge(att_ready, NJ * b + j + 1)
                        for k in range(j + 1):
                            ins = pe.matmul(psum[32 * g:32 * g + 32, 6 + j % 2, 0:2 * P],
                                            v[:, k, 32 * g:32 * g + 32], probT[m % 2][:, k, :, :].rearrange("q p n -> q (p n)"),
                                            start=(k == 0), stop=(k == j))
                        ins.then_inc(pv_done, 1)

                    def turn_back(j):
                        pe.wait_ge(outT_ready, NJ * b + j + 1)
                        for p in range(2):
                            ins = pe.transpose(psum[:, 6 + j % 2, (2 + p) * P:(3 + p) * P], outT[j % 2][:, p * P:(p + 1) * P], ident)
                        ins.then_inc(out_ps, 1)

                    pe.wait_ge(k_q0_ready, 2 * b + 2)
                    filled = 0
                    for n in range(-2, NU):
                        last = slot_of(min(n + 2, NU - 1), prepares) + 1
                        for slot in range(filled, last):
                            if slot == 1:
                                pe.wait_ge(q1_ready, b + 1)
                            fill(slot)
                        filled = last
                        if n >= 0:
                            turn(n)
                        if n == 2:
                            pe.wait_ge(v_ready, b + 1)
                        if n >= 2 and n % 2 == 0:
                            values(n // 2 - 1)
                        if n >= 12 and n % 8 == 4:
                            turn_back(n // 8 - 1)
                    values(PAIRS - 1)
                    turn_back(NJ - 1)

                pe.wait_ge(consts_in, 80)
                for x in range(PREP):
                    if x >= 2 or x == 1:
                        pe.wait_ge(slot_read, max(x - 1, 1))
                    prepare(x, x, 0)
                with pe.Fori(0, B - 1) as b:
                    attend(b, True)
                attend(B - 1, False)

            @block.scalar
            def _(act):
                def attend(b, prepares):
                    act.wait_ge(slot_read, slots_before(b))
                    act.activation(v[:, :, :], v_next[:, :, :], ACT.Copy).then_inc(v_ready, 1)

                    def turned(n):
                        width = UNITS[n][0] + 1
                        act.wait_ge(probT_ps, NU * b + n + 1)
                        if n >= 4:
                            act.wait_ge(pv_done, PAIRS * b + n // 2 - 1)
                        act.activation(probT[n // 2 % 2][:, 0:width, n % 2, :],
                                       turned_bank(n)[:, 0:width * P].rearrange("q (k n) -> q k n", n=P), ACT.Copy).then_inc(probT_ready[1], 1)

                    def out_of_tile(j):
                        act.wait_ge(pv_done, PAIRS * b + GROUPS * (j + 1))
                        act.activation(outT[j % 2][:, :], psum[:, 6 + j % 2, 0:2 * P], ACT.Copy).then_inc(outT_ready, 1)

                    for n in range(NU):
                        j, g, p = UNITS[n]
                        width = (j + 1) * P
                        act.wait_ge(slot_read, slots_before(b) + slot_of(n, prepares) + 1)
                        if n >= 2:
                            act.wait_ge(probT_ps, NU * b + n - 1)
                        at = j * HEADS + GROUPS * p + g
                        act.activation(prob[n % 2][:, 0:width], scaled[n % 3][:, 0:width], ACT.Exp, bias=least[:, n % 3:n % 3 + 1],
                                       scale=-1.0, accum_out=sums[:, at:at + 1]).then_inc(prob_ready, 1)
                        if n >= 2 and n % 2 == 0:
                            turned(n - 1)
                        if n >= 10 and n % 8 == 2:
                            out_of_tile(n // 8 - 1)
                    turned(NU - 1)
                    out_of_tile(NJ - 1)

                with act.Fori(0, B - 1) as b:
                    attend(b, True)
                attend(B - 1, False)

            @block.vector
            def _(dve):
                def statistics(batch):
                    for j in range(NJ):
                        ins = dve.bn_stats(stats[:, j, :], hidden[:, bass.ds(batch * NJ + j, 1), :].rearrange("p o n -> p (o n)"))
                    ins.then_inc(norm[0], 1)
                    dve.wait_ge(norm[0], batch + 1)
                    dve.memset(consts.carrier[:, 0:1], 0.0)
                    for j in range(NJ):
                        ins = dve.bn_aggr(moments[:, j, :], stats[:, j, :])
                    ins.then_inc(norm[1], 1)

                def apply(batch):
                    dve.wait_ge(norm[2], batch + 1)
                    for j in range(NJ):
                        ins = dve.tensor_scalar(hn[:, j, :], hidden[:, bass.ds(batch * NJ + j, 1), :].rearrange("p o n -> p (o n)"),
                                                moments[:, j, 0:1], rstd[:, j:j + 1], ALU.subtract, ALU.mult)
                    ins.then_inc(norm[3], 1)

                def stage(x, slot, batch, first=False):
                    k = 2 * (slot % 2)
                    if x == 0:
                        ins = dve.tensor_copy(hnT[:, :], bank_pair(k))
                    elif x == 1:
                        if not first:
                            dve.wait_ge(v_ready, batch)
                        ins = dve.tensor_copy(v_next[:, :, :].rearrange("p j n -> p (j n)"), bank_pair(k))
                    else:
                        s, h = (x - 2) // 2, x % 2
                        if x == 4 and not first:
                            dve.wait_ge(q1_ready, batch)
                        for side, table, out in ((0, cos, by_cos), (1, sin, by_sin)):
                            ins = dve.tensor_tensor(out[:, s, h * HALF:(h + 1) * HALF], psum[:, k + side, 0:HALF],
                                                    table[:, s, h * HALF:(h + 1) * HALF], ALU.mult)
                    ins.then_inc(slot_read, 1)

                def attend(b, prepares):
                    base = slots_before(b)

                    def turned(n):
                        width = UNITS[n][0] + 1
                        dve.wait_ge(probT_ps, NU * b + n + 1)
                        if n >= 4:
                            dve.wait_ge(pv_done, PAIRS * b + n // 2 - 1)
                        dve.tensor_copy(probT[n // 2 % 2][:, 0:width, n % 2, :],
                                        turned_bank(n)[:, 0:width * P].rearrange("q (k n) -> q k n", n=P)).then_inc(probT_ready[0], 1)

                    def normalised_output(j):
                        dve.wait_ge(prob_ready, NU * b + HEADS * (j + 1))
                        here = slice(j * HEADS, (j + 1) * HEADS)
                        dve.reciprocal(recip[:, here], sums[:, here]).then_inc(recip_ready, 1)
                        if j == 0:
                            dve.wait_ge(att_stored, 16 * NJ * (b + 1))
                        dve.wait_ge(out_ps, NJ * b + j + 1)
                        dve.wait_ge(recip_ready, NJ * b + j + 1)
                        dve.tensor_tensor(att[:, here, :],
                                          psum[:, 6 + j % 2, 2 * P:4 * P].rearrange("q (n c) -> q n c", c=32)[:, :, 0:HD],
                                          recip[:, here].rearrange("p (n o) -> p n o", o=1).broadcast_to([P, HEADS, HD]),
                                          ALU.mult).then_inc(att_ready, 1)

                    dve.wait_ge(slot_read, base)
                    dve.tensor_tensor(qk[:, 2, :], by_cos[:, 2, :], by_sin[:, 2, :], ALU.add).then_inc(k_q0_ready, 1)
                    dve.tensor_tensor(qk[:, 0, :], by_cos[:, 0, :], by_sin[:, 0, :], ALU.add).then_inc(k_q0_ready, 1)
                    for slot, (kind, n) in enumerate(slots_of(prepares)):
                        if kind == "prepare":
                            dve.wait_ge(slot_ps, base + slot + 1)
                            stage(n, slot, b + 1)
                            continue
                        j, g, p = UNITS[n]
                        width = (j + 1) * P
                        dve.wait_ge(slot_ps, base + slot + 1)
                        if n >= 3:
                            dve.wait_ge(prob_ready, NU * b + n - 2)
                        dve.memset(consts.carrier[:, 1 + n % 4:2 + n % 4], 0.0)
                        dve.tensor_tensor_reduce(scaled[n % 3][:, 0:width], bank_pair(2 * (slot % 2))[:, 0:width],
                                                 mask[:, TP - width:TP], -ATT_SCALE, -MASKED, ALU.add, ALU.min,
                                                 least[:, n % 3:n % 3 + 1]).then_inc(slot_read, 1)
                        if n >= 2 and n % 2 == 0:
                            turned(n - 2)
                        if n >= 14 and n % 8 == 6:
                            normalised_output(n // 8 - 1)
                        if prepares and n == STATS_AT:
                            statistics(b + 1)
                        if prepares and n == APPLY_AT:
                            apply(b + 1)
                    turned(NU - 2)
                    normalised_output(NJ - 1)

                dve.memset(recip[:, :], 0.0).then_inc(att_ready, 2)
                dve.memset(att[:, :, :], 0.0).then_inc(att_stored, 16 * NJ)
                dve.wait_ge(consts_in, 80)
                statistics(0)
                apply(0)
                for x in range(PREP):
                    dve.wait_ge(slot_ps, x + 1)
                    stage(x, x, 0, first=True)
                with dve.Fori(0, B - 1) as b:
                    attend(b, True)
                attend(B - 1, False)

            @block.gpsimd
            def _(pool):
                invert_deviation(pool, moments, rstd, consts, norm, 1)
                with pool.Fori(0, B - 1) as b:
                    pool.wait_ge(slot_read, slots_before(b))
                    pool.tensor_tensor(qk[:, 1, :], by_cos[:, 1, :], by_sin[:, 1, :], ALU.add).then_inc(q1_ready, 1)
                    invert_deviation(pool, moments, rstd, consts, norm, b + 2)
                pool.wait_ge(slot_read, slots_before(B - 1))
                pool.tensor_tensor(qk[:, 1, :], by_cos[:, 1, :], by_sin[:, 1, :], ALU.add).then_inc(q1_ready, 1)


        with nc.Block() as block:
            @block.sync
            def _(sp):
                for u in range(2):
                    whole, rest = batch_rows(by_row, u)
                    sp.dma_start(rows[u][:, 0:NJ - 1, :], whole).then_inc(rows_loaded[u], 16)
                    sp.dma_start(rows[u][0:LAST, NJ - 1, :], rest).then_inc(rows_loaded[u], 16)
                with sp.Fori(1, B // 2) as i:
                    for u in range(2):
                        sp.wait_ge(h_ready, 2 * (2 * i + u - 1))
                        whole, rest = batch_rows(by_row, 2 * i + u)
                        sp.dma_start(rows[u][:, 0:NJ - 1, :], whole).then_inc(rows_loaded[u], 16)
                        sp.dma_start(rows[u][0:LAST, NJ - 1, :], rest).then_inc(rows_loaded[u], 16)

            @block.vector
            def _(dve):
                with dve.Fori(0, B // 2) as i:
                    for u in range(2):
                        first = (2 * i + u) * NJ
                        dve.wait_ge(rows_loaded[u], 32 * i + 32)
                        dve.tensor_tensor(hidden[:, bass.ds(first, NJ - 1), :], hidden[:, bass.ds(first, NJ - 1), :],
                                          rows[u][:, 0:NJ - 1, :], ALU.add).then_inc(h_ready, 1)
                        dve.tensor_tensor(hidden[0:LAST, bass.ds(first + NJ - 1, 1), :], hidden[0:LAST, bass.ds(first + NJ - 1, 1), :],
                                          rows[u][0:LAST, NJ - 1:NJ, :], ALU.add).then_inc(h_ready, 1)


def routed_ffn(nc, w, hidden, ident, consts, psum):
    NT = NJ + -(-(N0 - T) // P)
    TC = 3
    VU, NC = NT // TC, F0 // P
    W = TC * P
    with ExitStack() as ctx:
        def sb(name, shape, n=1, dt=F32):
            t = [ctx.enter_context(nc.sbuf_tensor(f"{name}{u}", shape, dt)) for u in range(n)]
            return t if n > 1 else t[0]

        def sem(name):
            return ctx.enter_context(nc.semaphore(name))

        hn, hnT = sb("rf_hn", [P, NT, P]), sb("rf_hnT", [P, NT * P])
        stats, moments, rstd = sb("rf_stats", [P, NT, 6]), sb("rf_moments", [P, NT, 2]), sb("rf_rstd", [P, NT])
        weight, index = sb("rf_weight", [P, NT, TOPK0]), sb("rf_index", [P, NT, TOPK0], dt=I32)
        index_f = sb("rf_index_f", [P, NT, TOPK0])
        chosen = sb("rf_chosen", [P, E0, TOPK0, NT])
        gate = sb("rf_gate", [P, E0, NT])
        gate_now = sb("rf_gate_now", [P, NT], 2)
        w1, w2 = sb("rf_w1", [P, F0], 2), sb("rf_w2", [P, NC, P], 2)
        actT = sb("rf_actT", [P, NC, W], 2)

        norm = [sem(f"rf_norm_{s}") for s in ("stats", "moments", "rstd", "out")]
        w_loaded = [sem("rf_w_loaded0"), sem("rf_w_loaded1")]
        zeroed, routes_in, index_ready, chosen_ready, gate_ready = (
            sem(f"rf_{s}") for s in ("zeroed", "routes_in", "index_ready", "chosen_ready", "gate_ready"))
        hnT_ps, hnT_ready = sem("rf_hnT_ps"), sem("rf_hnT_ready")
        up_ps, act_ready, down_done, added = sem("rf_up_ps"), sem("rf_act_ready"), sem("rf_down_done"), sem("rf_added")
        copied = sem("rf_gate_copied")

        def spans():
            return ((0, (NJ - 1) * P, 0), ((NJ - 1) * P, LAST, NJ - 1),
                    (T, (N0 - T) // P * P, NJ), (T + (N0 - T) // P * P, (N0 - T) % P, NT - 1))

        with nc.Block() as block:
            @block.sync
            def _(sp):
                def load(u, e):
                    sp.dma_start(w1[u][:, :], w["w1"][e]).then_inc(w_loaded[u], 16)
                    sp.dma_start(w2[u][:, :, :], w["w2"][e].rearrange("(k p) d -> p k d", p=P)).then_inc(w_loaded[u], 16)

                sp.wait_ge(zeroed, 1)
                for first, n, tile in spans():
                    for dst, src in ((weight, w["ew0"]), (index, w["ei0"])):
                        if n % P == 0:
                            sp.dma_start(dst[:, tile:tile + n // P, :],
                                         src[first:first + n].rearrange("(j p) k -> p j k", p=P)).then_inc(routes_in, 16)
                        else:
                            sp.dma_start(dst[0:n, tile, :], src[first:first + n]).then_inc(routes_in, 16)
                for u in range(2):
                    load(u, u)
                with sp.Fori(1, E0 // 2) as i:
                    for u in range(2):
                        sp.wait_ge(down_done, VU * (2 * i + u - 1) + 2)
                        load(u, 2 * i + u)

            @block.gpsimd
            def _(pool):
                invert_deviation(pool, moments, rstd, consts, norm, 1)

            @block.vector
            def _(dve):
                dve.memset(weight[:, :, :], 0.0)
                dve.memset(index[:, :, :], 0).then_inc(zeroed, 1)
                dve.memset(index_f[:, :, :], 0.0).then_inc(act_ready, 3)
                dve.memset(gate_now[0][:, :], 0.0).then_inc(down_done, 2)
                dve.memset(gate_now[1][:, :], 0.0).then_inc(added, 2)
                normalise(dve, consts, hidden[:, 0:NT, :], hn, stats, moments, rstd, norm, 1)
                dve.wait_ge(hnT_ps, 1)
                dve.tensor_copy(hnT[:, :], psum[:, :, :].rearrange("p k n -> p (k n)")[:, 0:NT * P]).then_inc(hnT_ready, 1)
                dve.wait_ge(routes_in, 16 * 8)
                dve.tensor_copy(index_f[:, :, :], index[:, :, :]).then_inc(index_ready, 1)
                dve.wait_ge(index_ready, 1)
                for e in range(E0):
                    for k in range(TOPK0):
                        ins = dve.scalar_tensor_tensor(out=chosen[:, e, k, :], in0=index_f[:, :, k], scalar=float(e),
                                                       in1=weight[:, :, k], op0=ALU.is_equal, op1=ALU.mult)
                ins.then_inc(chosen_ready, 1)
                dve.wait_ge(chosen_ready, 1)
                dve.tensor_tensor(gate[:, :, :], chosen[:, :, 0, :], chosen[:, :, 1, :], ALU.add).then_inc(gate_ready, 1)
                dve.wait_ge(gate_ready, 1)
                with dve.Fori(0, E0 // 2) as i:
                    for u in range(2):
                        dve.wait_ge(added, VU * (2 * i + u) + 2)
                        dve.tensor_copy(gate_now[u][:, :].rearrange("p (o n) -> p o n", o=1),
                                        gate[:, bass.ds(2 * i + u, 1), :]).then_inc(copied, 1)
                        dve.wait_ge(copied, 2 * i + u + 1)
                        for c in range(VU):
                            v = VU * u + c
                            V = 2 * VU * i + v
                            dve.wait_ge(down_done, V + 3)
                            dve.wait_ge(added, V + 1)
                            for t in range(TC):
                                tile = TC * c + t
                                ins = dve.scalar_tensor_tensor(
                                    out=hidden[:, tile, :], in0=psum[:, 6 + v % 2, t * P:(t + 1) * P],
                                    scalar=gate_now[u][:, tile:tile + 1], in1=hidden[:, tile, :], op0=ALU.mult, op1=ALU.add)
                            ins.then_inc(added, 1)

            @block.scalar
            def _(act):
                with act.Fori(0, E0 // 2) as i:
                    for v in range(2 * VU):
                        act.wait_ge(down_done, 2 * VU * i + v + 1)
                        for half in range(2):
                            m = 2 * v + half
                            act.wait_ge(up_ps, 4 * VU * i + m + 1)
                            act.activation(actT[v % 2][:, 2 * half:2 * half + 2, :], psum[:, 2 * (m % 3):2 * (m % 3) + 2, 0:W],
                                           ACT.Gelu).then_inc(act_ready, 1)

            @block.tensor
            def _(pe):
                pe.wait_ge(norm[3], 1)
                flat = psum[:, :, :].rearrange("p k n -> p (k n)")
                for j in range(NT):
                    ins = pe.transpose(flat[:, j * P:(j + 1) * P], hn[:, j, :], ident)
                ins.then_inc(hnT_ps, 1)
                pe.wait_ge(hnT_ready, 1)
                pe.wait_ge(added, 2)
                pe.wait_ge(act_ready, 3)
                with pe.Fori(0, E0 // 2) as i:
                    def up(m):
                        u, c, half = m // (2 * VU), m // 2 % VU, m % 2
                        if m % (2 * VU) == 0:
                            pe.wait_ge(w_loaded[u], 32 * i + 32)
                        pe.wait_ge(act_ready, 4 * VU * i + m + 1)
                        for f in range(2):
                            lo = (2 * half + f) * P
                            ins = pe.matmul(psum[:, 2 * (m % 3) + f, 0:W], w1[u][:, lo:lo + P], hnT[:, c * W:(c + 1) * W],
                                            start=True, stop=True)
                        ins.then_inc(up_ps, 1)

                    def down(v):
                        u = v // VU
                        pe.wait_ge(act_ready, 4 * VU * i + 2 * v + 5)
                        pe.wait_ge(added, 2 * VU * i + v + 1)
                        for t in range(TC):
                            for f in range(NC):
                                ins = pe.matmul(psum[:, 6 + v % 2, t * P:(t + 1) * P], actT[v % 2][:, f, t * P:(t + 1) * P],
                                                w2[u][:, f, :], start=(f == 0), stop=(f == NC - 1))
                        ins.then_inc(down_done, 1)

                    up(0)
                    up(1)
                    for v in range(2 * VU):
                        if v + 1 < 2 * VU:
                            up(2 * v + 2)
                            up(2 * v + 3)
                        down(v)


def column_attention(nc, w, hidden, ident, consts, psum):
    HALF = T // 2
    with ExitStack() as ctx:
        def sb(name, shape, n=1, dt=F32):
            t = [ctx.enter_context(nc.sbuf_tensor(f"{name}{u}", shape, dt)) for u in range(n)]
            return t if n > 1 else t[0]

        def sem(name):
            return ctx.enter_context(nc.semaphore(name))

        hn, hnT = sb("ca_hn", [P, NJ, P]), sb("ca_hnT", [P, TP])
        stats, moments, rstd = sb("ca_stats", [P, B * NJ, 6]), sb("ca_moments", [P, B * NJ, 2]), sb("ca_rstd", [P, B * NJ])
        wq, wk, wv = sb("ca_wq", [P, P]), sb("ca_wk", [P, P]), sb("ca_wv", [P, P])
        qT, kT, v = sb("ca_qT", [P, TP]), sb("ca_kT", [P, TP]), sb("ca_v", [P, NJ, P])
        v_scaled = sb("ca_v_scaled", [P, NJ, P])
        prob = sb("ca_prob", [P, NJ, T])
        minus_max, sums, recip = sb("ca_minus_max", [P, NJ]), sb("ca_sums", [P, NJ]), sb("ca_recip", [P, NJ])

        weights_in = sem("ca_weights_in")
        norm = [sem(f"ca_norm_{s}") for s in ("stats", "moments", "rstd", "out")]
        hnT_ps, hnT_ready, proj_ps = sem("ca_hnT_ps"), sem("ca_hnT_ready"), sem("ca_proj_ps")
        q_ready, k_ready, v_ready = sem("ca_q_ready"), sem("ca_k_ready"), sem("ca_v_ready")
        score_ps, max_ready, prob_ready = sem("ca_score_ps"), sem("ca_max_ready"), sem("ca_prob_ready")
        recip_ready, v_scaled_ready = sem("ca_recip_ready"), sem("ca_v_scaled_ready")
        out_ps, h_ready = sem("ca_out_ps"), sem("ca_h_ready")
        flat = psum[:, :, :].rearrange("p k n -> p (k n)")

        def pair(k):
            return flat[:, 2 * k * 512:2 * k * 512 + TP]

        def halves(k, n):
            return psum[:, 2 * k:2 * k + 2, 0:n]

        with nc.Block() as block:
            @block.sync
            def _(sp):
                for dst, src in ((wq, w["wqT"]), (wk, w["wkT"]), (wv, w["wvT"])):
                    sp.dma_start(dst[:, :], src).then_inc(weights_in, 16)

            @block.gpsimd
            def _(pool):
                all_deviations(pool, moments, rstd, consts, norm)

            @block.tensor
            def _(pe):
                def prepare(batch, free):
                    pe.wait_ge(norm[3], batch + 1)
                    free(0)
                    for j in range(NJ):
                        ins = pe.transpose(pair(0)[:, j * P:(j + 1) * P], hn[:, j, :], ident)
                    ins.then_inc(hnT_ps, 1)
                    pe.wait_ge(hnT_ready, batch + 1)
                    for r, wt in ((1, wq), (2, wk)):
                        free(r)
                        for h in range(2):
                            ins = pe.matmul(psum[:, 2 * r + h, 0:TP // 2], wt[:, :], hnT[:, h * TP // 2:(h + 1) * TP // 2],
                                            start=True, stop=True)
                        ins.then_inc(proj_ps, 1)
                    for j in range(NJ):
                        ins = pe.matmul(pair(0)[:, j * P:(j + 1) * P], hnT[:, j * P:(j + 1) * P], wv[:, :], start=True, stop=True)
                    ins.then_inc(proj_ps, 1)

                def attend(b, prepares):
                    pe.wait_ge(q_ready, b + 1)
                    pe.wait_ge(k_ready, b + 1)
                    pe.wait_ge(v_ready, b + 1)
                    for k in range(NJ):
                        if k >= 3:
                            pe.wait_ge(prob_ready, NJ * b + k - 2)
                        for h in range(2):
                            ins = pe.matmul(psum[:, 2 * (k % 3) + h, 0:HALF], kT[:, k * P:(k + 1) * P], qT[:, h * HALF:(h + 1) * HALF],
                                            start=True, stop=True)
                        ins.then_inc(score_ps, 1)
                    if prepares:
                        prepare(b + 1, lambda r: pe.wait_ge(prob_ready, NJ * b + NJ - 2 + r))
                    pe.wait_ge(v_scaled_ready, NJ * b + NJ)
                    pe.wait_ge(h_ready, 2 * b + 2)
                    for j in range(NJ):
                        rows = min(P, T - j * P)
                        for k in range(NJ):
                            ins = pe.matmul(pair(3)[0:rows, j * P:(j + 1) * P], prob[:, k, j * P:j * P + rows], v_scaled[:, k, :],
                                            start=(k == 0), stop=(k == NJ - 1))
                    ins.then_inc(out_ps, 1)

                pe.wait_ge(weights_in, 48)
                prepare(0, lambda r: None)
                with pe.Fori(0, B - 1) as b:
                    attend(b, True)
                attend(B - 1, False)

            @block.scalar
            def _(act):
                def prepare(batch):
                    act.wait_ge(hnT_ps, batch + 1)
                    act.activation(hnT[:, :], pair(0), ACT.Copy).then_inc(hnT_ready, 1)
                    act.wait_ge(proj_ps, 3 * batch + 1)
                    act.activation(qT[:, :].rearrange("p (h n) -> p h n", h=2), halves(1, TP // 2), ACT.Copy).then_inc(q_ready, 1)

                def attend(b, prepares):
                    act.wait_ge(out_ps, b + 1)
                    for k in range(NJ):
                        act.wait_ge(max_ready, NJ * b + k + 1)
                        act.activation(prob[:, k, :].rearrange("p (h n) -> p h n", h=2), halves(k % 3, HALF),
                                       ACT.Exp, bias=minus_max[:, k:k + 1], accum_out=sums[:, k:k + 1]).then_inc(prob_ready, 1)
                    if prepares:
                        prepare(b + 1)

                prepare(0)
                with act.Fori(0, B - 1) as b:
                    attend(b, True)
                attend(B - 1, False)

            @block.vector
            def _(dve):
                def prepare(batch, first=False):
                    dve.wait_ge(proj_ps, 3 * batch + 2)
                    dve.tensor_copy(kT[:, :].rearrange("p (h n) -> p h n", h=2), halves(2, TP // 2)).then_inc(k_ready, 1)
                    dve.wait_ge(proj_ps, 3 * batch + 3)
                    if not first:
                        dve.wait_ge(v_scaled_ready, NJ * batch)
                    dve.tensor_copy(v[:, :, :].rearrange("p j n -> p (j n)"), pair(0)).then_inc(v_ready, 1)

                def attend(b, prepares):
                    def scale_value(k):
                        dve.wait_ge(prob_ready, NJ * b + k + 1)
                        dve.reciprocal(recip[:, k:k + 1], sums[:, k:k + 1]).then_inc(recip_ready, 1)
                        dve.wait_ge(recip_ready, NJ * b + k + 1)
                        dve.wait_ge(v_ready, b + 1)
                        dve.tensor_scalar(v_scaled[:, k, :], v[:, k, :], recip[:, k:k + 1], None, ALU.mult).then_inc(v_scaled_ready, 1)

                    for k in range(NJ):
                        dve.wait_ge(score_ps, NJ * b + k + 1)
                        dve.tensor_reduce(minus_max[:, k:k + 1], halves(k % 3, HALF), AX.XY, ALU.max,
                                          negate=True).then_inc(max_ready, 1)
                        if k >= 1:
                            scale_value(k - 1)
                        if k == 2 and prepares:
                            apply_moments(dve, hidden, hn, moments, rstd, b + 1, norm[3])
                    scale_value(NJ - 1)
                    if prepares:
                        prepare(b + 1)
                    dve.wait_ge(out_ps, b + 2)
                    dve.tensor_tensor(hidden[:, bass.ds(b * NJ, NJ - 1), :], pair(3)[:, 0:(NJ - 1) * P].rearrange("p (j n) -> p j n", n=P),
                                      hidden[:, bass.ds(b * NJ, NJ - 1), :], ALU.add).then_inc(h_ready, 1)
                    dve.tensor_tensor(hidden[0:LAST, bass.ds(b * NJ + NJ - 1, 1), :],
                                      pair(3)[0:LAST, (NJ - 1) * P:TP].rearrange("p (j n) -> p j n", n=P),
                                      hidden[0:LAST, bass.ds(b * NJ + NJ - 1, 1), :], ALU.add).then_inc(h_ready, 1)

                dve.memset(minus_max[:, :], 0.0).then_inc(h_ready, 2)
                dve.memset(recip[:, :], 0.0).then_inc(out_ps, 1)
                all_moments(dve, consts, hidden, stats, moments, norm)
                dve.wait_ge(norm[2], 1)
                apply_moments(dve, hidden, hn, moments, rstd, 0, norm[3])
                prepare(0, first=True)
                with dve.Fori(0, B - 1) as b:
                    attend(b, True)
                attend(B - 1, False)


def route(nc, w, hidden, ident, consts, psum, hn_all, slot, weight, expert_of, prepare_blocks):
    NT, K = B * NJ, PG1
    SETS = 1 + G1
    N = NT * SETS
    with ExitStack() as ctx:
        def sb(name, shape, n=1, dt=F32):
            t = [ctx.enter_context(nc.sbuf_tensor(f"{name}{u}", shape, dt)) for u in range(n)]
            return t if n > 1 else t[0]

        def sem(name):
            return ctx.enter_context(nc.semaphore(name))

        stats, moments, rstd = sb("ro_stats", [P, NT, 6]), sb("ro_moments", [P, NT, 2]), sb("ro_rstd", [P, NT])
        hn = sb("ro_hn", [P, NJ, P], 2)
        hnT = sb("ro_hnT", [P, TP], 2)
        wg, bias = sb("ro_wg", [P, SETS * K]), sb("ro_bias", [P, SETS * K])
        prob, first, second, rest = (sb(f"ro_{s}", [P, N, K]) for s in ("prob", "first", "second", "rest"))
        top, total, inv, next_, both, seen, w_first, w_second = (
            sb(f"ro_{s}", [P, N]) for s in ("top", "total", "inv", "next", "both", "seen", "w_first", "w_second"))

        one_hot = sb("ro_one_hot", [P, 4, NT, E1])
        sel, cum, scan = sb("ro_sel", [P, NT, E1]), sb("ro_cum", [P, NT, E1]), sb("ro_scan", [P, NT, E1], 2)
        within = sb("ro_within", [P, 2, NT, K])
        before, ones = sb("ro_before", [P, P]), sb("ro_ones", [P, P])
        count_i = sb("ro_count_i", [P, E1], dt=I32)
        padded, start, ends = sb("ro_padded", [P, E1]), sb("ro_start", [P, E1], 2), sb("ro_ends", [P, E1])
        slot_f = sb("ro_slot_f", [P, 4, NT])
        block_row, expert_f = sb("ro_block_row", [1, BLOCKS]), sb("ro_expert_f", [1, BLOCKS])

        weights_in = sem("ro_weights_in")
        sel_ready, rank_ps = sem("ro_sel_ready"), sem("ro_rank_ps")
        norm = [sem(f"ro_norm_{s}") for s in ("stats", "moments", "rstd", "out")]
        hnT_ps, hnT_ready, kept = sem("ro_hnT_ps"), sem("ro_hnT_ready"), sem("ro_hn_kept")
        logits_ps, logits_ready, exp_ready, chain = sem("ro_logits_ps"), sem("ro_logits_ready"), sem("ro_exp_ready"), sem("ro_chain")
        shifted = sem("ro_shifted")
        flat = psum[:, :, :].rearrange("p k n -> p (k n)")
        hnT_bank = [flat[:, k * 512:k * 512 + TP] for k in (0, 4)]
        logits_bank = [psum[:, k, 0:NJ * SETS * K] for k in (2, 6)]

        def over(row):
            return row[:, :].rearrange("p (n o) -> p n o", o=1).broadcast_to([P, N, K])

        with nc.Block() as block:
            @block.sync
            def _(sp):
                sp.dma_start(wg[:, :], w["wgate"]).then_inc(weights_in, 16)
                sp.dma_start(bias[:, :], w["bgate"].broadcast_to([P, SETS * K])).then_inc(weights_in, 16)
                sp.dma_start(before[:, :], w["before"]).then_inc(weights_in, 16)
                sp.dma_start(block_row[:, :], w["block_row"]).then_inc(weights_in, 16)
                prepare_blocks(sp)

            @block.gpsimd
            def _(pool):
                all_deviations(pool, moments, rstd, consts, norm)

            @block.tensor
            def _(pe):
                pe.wait_ge(weights_in, 64)
                with pe.Fori(0, B // 2) as i:
                    for u in range(2):
                        pe.wait_ge(norm[3], 2 * i + u + 1)
                        for j in range(NJ):
                            ins = pe.transpose(hnT_bank[u][:, j * P:(j + 1) * P], hn[u][:, j, :], ident)
                        ins.then_inc(hnT_ps, 1)
                    for u in range(2):
                        pe.wait_ge(hnT_ready, 2 * i + u + 1)
                        pe.wait_ge(logits_ready, 2 * i + u + 1)
                        for j in range(NJ):
                            ins = pe.matmul(logits_bank[u][:, j * SETS * K:(j + 1) * SETS * K], hnT[u][:, j * P:(j + 1) * P], wg[:, :],
                                            start=True, stop=True)
                        ins.then_inc(logits_ps, 1)
                pe.wait_ge(sel_ready, 1)
                sel_cols = sel[:, :, :].rearrange("p t e -> p (t e)")
                for k, lhsT in ((0, before), (4, ones)):
                    for lo in range(0, NT * E1, 512):
                        hi = min(lo + 512, NT * E1)
                        ins = pe.matmul(psum[:, k + lo // 512, 0:hi - lo], lhsT[:, :], sel_cols[:, lo:hi], start=True, stop=True)
                ins.then_inc(rank_ps, 1)

            @block.scalar
            def _(act):
                with act.Fori(0, B // 2) as i:
                    for u in range(2):
                        act.wait_ge(hnT_ps, 2 * i + u + 1)
                        act.activation(hnT[u][:, :], hnT_bank[u], ACT.Copy).then_inc(hnT_ready, 1)
                    for u in range(2):
                        act.activation(hn_all[:, bass.ds((2 * i + u) * NJ, NJ), :], hn[u][:, :, :], ACT.Copy).then_inc(kept, 1)
                act.wait_ge(shifted, 1)
                act.activation(prob[:, :, :], prob[:, :, :], ACT.Exp).then_inc(exp_ready, 1)

            @block.vector
            def _(dve):
                done = 0

                def link(ins):
                    nonlocal done
                    done += 1
                    ins.then_inc(chain, 1)
                    dve.wait_ge(chain, done)

                def choose(values, best, out):
                    link(dve.tensor_tensor(out[:, :, :], values[:, :, :], over(best), ALU.is_equal))
                    link(dve.tensor_tensor(seen[:, :], out[:, :, 0], out[:, :, 1], ALU.max))
                    link(dve.tensor_tensor(out[:, :, 1], out[:, :, 1], out[:, :, 0], ALU.is_gt))
                    link(dve.tensor_tensor(both[:, :], seen[:, :], out[:, :, 2], ALU.max))
                    link(dve.tensor_tensor(out[:, :, 2], out[:, :, 2], seen[:, :], ALU.is_gt))
                    link(dve.tensor_tensor(out[:, :, 3], out[:, :, 3], both[:, :], ALU.is_gt))

                dve.wait_ge(weights_in, 64)
                dve.memset(seen[:, :], 0.0).then_inc(logits_ready, 2)
                dve.memset(both[:, :], 0.0).then_inc(kept, 2)
                all_moments(dve, consts, hidden, stats, moments, norm)
                dve.wait_ge(norm[2], 1)
                with dve.Fori(0, B // 2) as i:
                    for u in range(2):
                        dve.wait_ge(kept, 2 * i + u + 1)
                        apply_moments(dve, hidden, hn[u], moments, rstd, 2 * i + u, norm[3])
                    for u in range(2):
                        dve.wait_ge(logits_ps, 2 * i + u + 1)
                        dve.tensor_tensor(prob[:, bass.ds((2 * i + u) * NJ * SETS, NJ * SETS), :].rearrange("p (j s) k -> p j (s k)", s=SETS),
                                          logits_bank[u].rearrange("p (j n) -> p j n", j=NJ),
                                          bias[:, :].rearrange("p (o n) -> p o n", o=1).broadcast_to([P, NJ, SETS * K]),
                                          ALU.add).then_inc(logits_ready, 1)
                dve.wait_ge(logits_ready, B + 2)
                link(dve.tensor_reduce(top[:, :], prob[:, :, :], AX.X, ALU.max))
                dve.tensor_tensor(prob[:, :, :], prob[:, :, :], over(top), ALU.subtract).then_inc(shifted, 1)
                dve.wait_ge(exp_ready, 1)
                link(dve.tensor_reduce(total[:, :], prob[:, :, :], AX.X, ALU.add))
                link(dve.reciprocal(inv[:, :], total[:, :]))
                link(dve.tensor_tensor(prob[:, :, :], prob[:, :, :], over(inv), ALU.mult))
                link(dve.tensor_reduce(top[:, :], prob[:, :, :], AX.X, ALU.max))
                choose(prob, top, first)
                link(dve.scalar_tensor_tensor(out=rest[:, :, :], in0=first[:, :, :], scalar=-2.0, in1=prob[:, :, :],
                                              op0=ALU.mult, op1=ALU.add))
                link(dve.tensor_reduce(next_[:, :], rest[:, :, :], AX.X, ALU.max))
                choose(rest, next_, second)
                link(dve.tensor_tensor(total[:, :], top[:, :], next_[:, :], ALU.add))
                link(dve.scalar_tensor_tensor(out=next_[:, :], in0=total[:, :], scalar=THRESHOLD, in1=next_[:, :],
                                              op0=ALU.is_le, op1=ALU.mult))
                link(dve.tensor_tensor(total[:, :], top[:, :], next_[:, :], ALU.add))
                link(dve.tensor_scalar(total[:, :], total[:, :], 1e-9, None, ALU.add))
                link(dve.reciprocal(inv[:, :], total[:, :]))
                link(dve.tensor_tensor(w_first[:, :], top[:, :], inv[:, :], ALU.mult))
                link(dve.tensor_tensor(w_second[:, :], next_[:, :], inv[:, :], ALU.mult))
                picks = [x[:, :, :].rearrange("p (t s) k -> p t s k", s=SETS) for x in (first, second)]
                shares = [x[:, :].rearrange("p (t s) -> p t s", s=SETS) for x in (w_first, w_second)]
                for a in range(2):
                    for c in range(2):
                        link(dve.tensor_tensor(within[:, c, :, :], picks[a][:, :, 0, :], shares[c][:, :, 1:], ALU.mult))
                        link(dve.tensor_reduce(slot_f[:, 2 * a + c, :], within[:, c, :, :], AX.X, ALU.add))
                        link(dve.scalar_tensor_tensor(out=weight[:, 2 * a + c, :], in0=slot_f[:, 2 * a + c, :], scalar=G1 ** -0.5,
                                                      in1=shares[a][:, :, 0], op0=ALU.mult, op1=ALU.mult))
                        for g in range(G1):
                            ins = dve.tensor_tensor(one_hot[:, 2 * a + c, :, g * K:(g + 1) * K], picks[c][:, :, 1 + g, :],
                                                    picks[a][:, :, 0, g:g + 1].broadcast_to([P, NT, K]), ALU.mult)
                        link(ins)
                link(dve.tensor_tensor(sel[:, :, :], one_hot[:, 0, :, :], one_hot[:, 1, :, :], ALU.add))
                link(dve.tensor_tensor(sel[:, :, :], sel[:, :, :], one_hot[:, 2, :, :], ALU.add))
                link(dve.memset(ones[:, :], 1.0))
                dve.tensor_tensor(sel[:, :, :], sel[:, :, :], one_hot[:, 3, :, :], ALU.add).then_inc(sel_ready, 1)
                dve.wait_ge(rank_ps, 1)
                in_tile = flat[:, 0:NT * E1].rearrange("p (t e) -> p t e", e=E1)
                of_tile = flat[:, 2048:2048 + NT * E1].rearrange("p (t e) -> p t e", e=E1)
                link(dve.tensor_copy(scan[0][:, :, :], of_tile))
                step, at = 1, 0
                while step < NT:
                    link(dve.tensor_copy(scan[1 - at][:, 0:step, :], scan[at][:, 0:step, :]))
                    link(dve.tensor_tensor(scan[1 - at][:, step:, :], scan[at][:, step:, :], scan[at][:, 0:NT - step, :], ALU.add))
                    step, at = 2 * step, 1 - at
                total_of = scan[at][:, NT - 1, :]
                link(dve.tensor_tensor(cum[:, :, :], scan[at][:, :, :], of_tile, ALU.subtract))
                link(dve.tensor_tensor(cum[:, :, :], cum[:, :, :], in_tile, ALU.add))
                link(dve.tensor_scalar(padded[:, :], total_of, float(P - 1), None, ALU.add))
                link(dve.tensor_copy(count_i[:, :], padded[:, :]))
                link(dve.tensor_scalar(count_i[:, :], count_i[:, :], -P, None, ALU.bitwise_and))
                link(dve.tensor_copy(padded[:, :], count_i[:, :]))
                link(dve.tensor_copy(start[0][:, :], padded[:, :]))
                step, at = 1, 0
                while step < E1:
                    link(dve.tensor_copy(start[1 - at][:, 0:step], start[at][:, 0:step]))
                    link(dve.tensor_tensor(start[1 - at][:, step:], start[at][:, step:], start[at][:, 0:E1 - step], ALU.add))
                    step, at = 2 * step, 1 - at
                link(dve.tensor_copy(ends[:, :], start[at][:, :]))
                link(dve.tensor_tensor(start[at][:, :], ends[:, :], padded[:, :], ALU.subtract))
                link(dve.tensor_tensor(cum[:, :, :], cum[:, :, :],
                                       start[at][:, :].rearrange("p (o e) -> p o e", o=1).broadcast_to([P, NT, E1]), ALU.add))
                for r in range(4):
                    link(dve.tensor_tensor(one_hot[:, r, :, :], one_hot[:, r, :, :], cum[:, :, :], ALU.mult))
                    link(dve.tensor_reduce(slot_f[:, r, :], one_hot[:, r, :, :], AX.X, ALU.add))
                link(dve.tensor_copy(slot[:, :, :], slot_f[:, :, :]))
                link(dve.memset(expert_f[:, :], 0.0))
                for e in range(E1 - 1):
                    link(dve.scalar_tensor_tensor(out=expert_f[:, :], in0=block_row[:, :], scalar=ends[0:1, e:e + 1],
                                                  in1=expert_f[:, :], op0=ALU.is_ge, op1=ALU.add))
                link(dve.tensor_copy(expert_of[:, :], expert_f[:, :]))


def grouped_ffn(nc, w, hidden, ident, consts, psum):
    NT, NC = B * NJ, F1 // P
    ZB = 16
    assert BLOCKS % ZB == 0
    with ExitStack() as ctx:
        def sb(name, shape, n=1, dt=F32, stack=ctx):
            t = [stack.enter_context(nc.sbuf_tensor(f"{name}{u}", shape, dt)) for u in range(n)]
            return t if n > 1 else t[0]

        def sem(name):
            return ctx.enter_context(nc.semaphore(name))

        slot, weight = sb("gf_slot", [P, CHOICES, NT], dt=I32), sb("gf_weight", [P, CHOICES, NT])
        expert_of = sb("gf_expert_of", [1, BLOCKS], dt=I32)
        w1, w3 = sb("gf_w1", [P, E1, F1]), sb("gf_w3", [P, E1, F1])
        x_rows = nc.dram_tensor("x_by_slot", (BLOCKS * P, D), F32, kind="Internal").ap()
        y_rows = nc.dram_tensor("y_by_slot", (BLOCKS * P, D), F32, kind="Internal").ap()
        w13_loaded = sem("gf_w13_loaded")

        with ExitStack() as inner:
            hn_all = sb("gf_hn_all", [P, NT, P], stack=inner)
            zeros = sb("gf_zeros", [P, ZB * P], stack=inner)
            zero_set, rows_zeroed, scattered = sem("gf_zero_set"), sem("gf_rows_zeroed"), sem("gf_scattered")
            with nc.Block() as block:
                @block.vector
                def _(dve):
                    dve.memset(zeros[:, :], 0.0).then_inc(zero_set, 1)

            def prepare_blocks(sp):
                sp.wait_ge(zero_set, 1)
                for n in range(BLOCKS // ZB):
                    sp.dma_start(x_rows[n * ZB * P:(n + 1) * ZB * P, :].rearrange("(p k) d -> p (k d)", p=P),
                                 zeros[:, :]).then_inc(rows_zeroed, 16)
                sp.dma_start(w1[:, :, :], w["W1"].rearrange("e p f -> p e f")).then_inc(w13_loaded, 16)
                sp.dma_start(w3[:, :, :], w["W3"].rearrange("e p f -> p e f")).then_inc(w13_loaded, 16)

            route(nc, w, hidden, ident, consts, psum, hn_all, slot, weight, expert_of, prepare_blocks)

            with nc.Block() as block:
                @block.gpsimd
                def _(pool):
                    pool.wait_ge(rows_zeroed, 16 * (BLOCKS // ZB))
                    for tile in range(NT):
                        for r in range(CHOICES):
                            pool.indirect_dma_start(
                                x_rows, bass.IndirectOffsetOnAxis(slot[:, r, tile:tile + 1], 0),
                                hn_all[:, tile, :], None).then_inc(scattered, 16)
                    pool.wait_ge(scattered, 16 * CHOICES * NT)

        expert_blocks(nc, w, ident, psum, expert_of, w1, w3, w13_loaded, x_rows, y_rows)

        with ExitStack() as inner:
            GB = 4
            rows = sb("gf_rows", [P, CHOICES, P], GB, stack=inner)
            gathered, added, chain = [sem(f"gf_gathered{u}") for u in range(GB)], sem("gf_added"), sem("gf_chain")
            with nc.Block() as block:
                @block.gpsimd
                def _(pool):
                    for tile in range(NT):
                        if tile >= GB:
                            pool.wait_ge(added, tile - GB + 1)
                        for r in range(CHOICES):
                            pool.indirect_dma_start(
                                rows[tile % GB][:, r, :], None, y_rows,
                                bass.IndirectOffsetOnAxis(slot[:, r, tile:tile + 1], 0)).then_inc(gathered[tile % GB], 16)

                @block.vector
                def _(dve):
                    for tile in range(NT):
                        dve.wait_ge(gathered[tile % GB], 16 * CHOICES * (tile // GB + 1))
                        for r in range(CHOICES):
                            ins = dve.scalar_tensor_tensor(out=hidden[:, tile, :], in0=rows[tile % GB][:, r, :],
                                                           scalar=weight[:, r, tile:tile + 1], in1=hidden[:, tile, :],
                                                           op0=ALU.mult, op1=ALU.add)
                            if r < CHOICES - 1:
                                ins.then_inc(chain, 1)
                                dve.wait_ge(chain, tile * (CHOICES - 1) + r + 1)
                        ins.then_inc(added, 1)


def expert_blocks(nc, w, ident, psum, expert_of, w1, w3, w13_loaded, x_rows, y_rows):
    NC, LASTB = F1 // P, BLOCKS - 1
    UNROLL = 8
    assert BLOCKS % UNROLL == 0
    with ExitStack() as ctx:
        def sb(name, shape, n=1, dt=F32):
            t = [ctx.enter_context(nc.sbuf_tensor(f"{name}{u}", shape, dt)) for u in range(n)]
            return t if n > 1 else t[0]

        def sem(name):
            return ctx.enter_context(nc.semaphore(name))

        w2 = sb("eb_w2", [P, E1 * NC, P])
        x_in, xT = sb("eb_x", [P, P], 4), sb("eb_xT", [P, P], 2)
        silu, product, productT = sb("eb_silu", [P, F1], 2), sb("eb_product", [P, F1], 2), sb("eb_productT", [P, F1], 2)
        y = sb("eb_y", [P, P], 4)
        w2_loaded = sem("eb_w2_loaded")
        x_loaded, y_stored = [sem(f"eb_x_loaded{u}") for u in range(4)], [sem(f"eb_y_stored{u}") for u in range(4)]
        xT_ps, xT_ready, up_ps, silu_ready, product_ready, productT_ps, productT_ready, y_ps, y_ready = (
            sem(f"eb_{s}") for s in ("xT_ps", "xT_ready", "up_ps", "silu_ready", "product_ready", "productT_ps",
                                     "productT_ready", "y_ps", "y_ready"))
        x_blocks = x_rows.rearrange("(n p) d -> n p d", p=P)
        y_blocks = y_rows.rearrange("(n p) d -> n p d", p=P)

        def steps(eng, step):
            for n in range(UNROLL):
                step(n, n % 2, 0, n)
            with eng.Fori(1, BLOCKS // UNROLL - 1) as i:
                for m in range(UNROLL):
                    step(UNROLL * i + m, m % 2, i, m)
            for n in range(BLOCKS - UNROLL, BLOCKS + 2):
                step(n, n % 2, BLOCKS // UNROLL - 1, n - (BLOCKS - UNROLL))

        def has(n, shift):
            return not isinstance(n, int) or 0 <= n + shift <= LASTB

        with nc.Block() as block:
            @block.sync
            def _(sp):
                for e in range(E1):
                    sp.dma_start(w2[:, e * NC:(e + 1) * NC, :], w["W2"][e].rearrange("(k p) d -> p k d", p=P)).then_inc(w2_loaded, 16)
                for u in range(4):
                    sp.dma_start(x_in[u][:, :], x_blocks[u]).then_inc(x_loaded[u], 16)

                def step(n, u, i, m):
                    if has(n, 4):
                        sp.wait_ge(xT_ps, n + 1)
                        sp.dma_start(x_in[m % 4][:, :], x_blocks[n + 4]).then_inc(x_loaded[m % 4], 16)
                    if has(n, -2):
                        sp.wait_ge(y_ready, n)
                        sp.dma_start(y_blocks[n - 2], y[(m - 2) % 4][:, :]).then_inc(y_stored[(m - 2) % 4], 16)

                steps(sp, step)
                for stored in y_stored:
                    sp.wait_ge(stored, 16 * (BLOCKS // 4 + 1))

            @block.tensor
            def _(pe):
                def turn_input(u):
                    ins = pe.transpose(psum[:, 6, 0:P], x_in[u][:, :], ident)
                    ins.then_inc(xT_ps, 1)

                def expert(n):
                    where = slice(n, n + 1) if isinstance(n, int) else bass.ds(n, 1)
                    return pe.value_load(expert_of[0:1, where], min_val=0, max_val=E1 - 1)

                expert_at = {}

                def step(n, u, i, m):
                    if m == 0:
                        for back in range(3):
                            if has(n, -back):
                                expert_at[-back] = expert(n - back)
                    if has(n, 1):
                        pe.wait_ge(x_loaded[(m + 1) % 4], 16 * (UNROLL // 4 * i + (m + 1) // 4 + 1))
                        pe.wait_ge(xT_ready, n + 1)
                        turn_input((m + 1) % 4)
                    if has(n, 0):
                        e = expert_at[m]
                        pe.wait_ge(xT_ready, n + 1)
                        for k, wt in ((u, w1), (2 + u, w3)):
                            ins = pe.matmul(psum[:, k, :], xT[u][:, :], wt[:, bass.ds(e, 1), :], start=True, stop=True)
                        ins.then_inc(up_ps, 1)
                    if has(n, 1) and m + 1 < UNROLL:
                        expert_at[m + 1] = expert(n + 1)
                    if has(n, -1):
                        pe.wait_ge(product_ready, n)
                        for f in range(NC):
                            ins = pe.transpose(psum[:, 4 + (1 - u), f * P:(f + 1) * P], product[1 - u][:, f * P:(f + 1) * P], ident)
                        ins.then_inc(productT_ps, 1)
                    if has(n, -2):
                        e = expert_at[m - 2]
                        pe.wait_ge(productT_ready, n - 1)
                        pe.wait_ge(y_ready, n - 1)
                        for f in range(NC):
                            ins = pe.matmul(psum[:, 7, 0:P], productT[u][:, f * P:(f + 1) * P],
                                            w2[:, bass.ds(e * NC + f, 1), :], start=(f == 0), stop=(f == NC - 1))
                        ins.then_inc(y_ps, 1)

                pe.wait_ge(w13_loaded, 32)
                pe.wait_ge(x_loaded[0], 16)
                turn_input(0)
                pe.wait_ge(w2_loaded, 16 * E1)
                steps(pe, step)

            @block.scalar
            def _(act):
                def step(n, u, i, m):
                    if has(n, 0):
                        act.wait_ge(up_ps, n + 1)
                        act.activation(silu[u][:, :], psum[:, u, :], ACT.Silu).then_inc(silu_ready, 1)
                    if has(n, -1):
                        act.wait_ge(productT_ps, n)
                        act.activation(productT[1 - u][:, :], psum[:, 4 + (1 - u), :], ACT.Copy).then_inc(productT_ready, 1)

                steps(act, step)

            @block.vector
            def _(dve):
                for buffer, stored in zip(y, y_stored):
                    dve.memset(buffer[:, :], 0.0).then_inc(stored, 16)
                dve.memset(xT[0][:, 0:1], 0.0).then_inc(y_ready, 1)
                dve.wait_ge(y_ready, 1)
                dve.wait_ge(xT_ps, 1)
                dve.tensor_copy(xT[0][:, :], psum[:, 6, 0:P]).then_inc(xT_ready, 1)

                def step(n, u, i, m):
                    if has(n, 1):
                        dve.wait_ge(xT_ps, n + 2)
                        dve.tensor_copy(xT[1 - u][:, :], psum[:, 6, 0:P]).then_inc(xT_ready, 1)
                    if has(n, 0):
                        dve.wait_ge(silu_ready, n + 1)
                        dve.tensor_tensor(product[u][:, :], silu[u][:, :], psum[:, 2 + u, :], ALU.mult).then_inc(product_ready, 1)
                    if has(n, -2):
                        dve.wait_ge(y_ps, n - 1)
                        dve.wait_ge(y_stored[(m - 2) % 4], 16 * (UNROLL // 4 * i + (m - 2) // 4 + 1))
                        dve.tensor_copy(y[(m - 2) % 4][:, :], psum[:, 7, 0:P]).then_inc(y_ready, 1)

                steps(dve, step)


def store(nc, hidden, out):
    with nc.semaphore("st_stored") as stored, nc.Block() as block:
        @block.sync
        def _(sp):
            for b in range(B):
                whole, rest = batch_rows(out, b)
                sp.dma_start(whole, hidden[:, b * NJ:(b + 1) * NJ - 1, :]).then_inc(stored, 16)
                sp.dma_start(rest, hidden[0:LAST, (b + 1) * NJ - 1, :]).then_inc(stored, 16)
            sp.wait_ge(stored, 32 * B)


class Consts:
    pass


def audio_tower(nc, a, out):
    with ExitStack() as ctx:
        hidden = ctx.enter_context(nc.sbuf_tensor("hidden", [P, B * NJ, P], F32))
        ident_sb = ctx.enter_context(nc.sbuf_tensor("ident", [P, P], F32))
        psum = ctx.enter_context(nc.psum_tensor("psum", [P, 8, 512], F32))
        consts = Consts()
        consts.minus_half = ctx.enter_context(nc.sbuf_tensor("minus_half", [P, 16], F32))
        consts.eps = ctx.enter_context(nc.sbuf_tensor("eps", [P, 16], F32))
        consts.carrier = ctx.enter_context(nc.sbuf_tensor("wait_carrier", [P, 8], F32))
        consts.loaded = ctx.enter_context(nc.semaphore("ident_loaded"))
        ident = ident_sb[:, :]
        with nc.Block() as block:
            @block.sync
            def _(sp):
                sp.dma_start(ident, a["ident"]).then_inc(consts.loaded, 16)
                sp.wait_ge(consts.loaded, 16)

            @block.gpsimd
            def _(pool):
                pool.memset(consts.minus_half[:, :], -0.5)
                pool.memset(consts.eps[:, :], EPS)
        token_mixer(nc, a["x"], a, hidden, ident, consts, psum)
        rope_attention(nc, a, hidden, ident, consts, psum)
        routed_ffn(nc, a, hidden, ident, consts, psum)
        column_attention(nc, a, hidden, ident, consts, psum)
        grouped_ffn(nc, a, hidden, ident, consts, psum)
        store(nc, hidden, out)


def rope_tables():
    cos, sin = np.zeros((P, 3, TP), np.float32), np.zeros((P, 3, TP), np.float32)
    for s in range(3):
        width = D if s < 2 else GROUPS * HD
        i = np.arange(width // 2, dtype=np.float64)
        theta = 10000.0 ** (-(2.0 * (i - 1.0))) / width
        angle = np.arange(T, dtype=np.float64)[:, None] * theta[None, :]
        for g in range(GROUPS):
            for h in range(HD):
                c = (2 * g + s) * HD + h if s < 2 else g * HD + h
                cos[32 * g + h, s, 0:T] = np.cos(angle[:, c // 2]).astype(np.float32)
                sin[32 * g + h, s, 0:T] = np.sin(angle[:, c // 2]).astype(np.float32) * (1 if c % 2 == 0 else -1)
    return cos, sin


def kernel(**inputs):
    import concourse.bacc as bacc
    from concourse.bass_utils import run_bass_kernel_spmd

    g = {k: np.asarray(v) for k, v in inputs.items()}
    t0 = "L0_tok_"
    wqk = np.zeros((P, 3, 2, P), g["L0_attn_Wq"].dtype)
    for s in range(3):
        for grp in range(GROUPS):
            for h in range(HD):
                weight = g["L0_attn_Wq"] if s < 2 else g["L0_attn_Wk"]
                c = (2 * grp + s) * HD + h if s < 2 else grp * HD + h
                wqk[:, s, 0, 32 * grp + h] = weight[:, c]
                wqk[:, s, 1, 32 * grp + h] = weight[:, c ^ 1]
    wv = np.zeros((P, P), g["L0_attn_Wv"].dtype)
    for grp in range(GROUPS):
        wv[:, 32 * grp:32 * grp + HD] = g["L0_attn_Wv"][:, grp * HD:(grp + 1) * HD]
    cos, sin = rope_tables()
    mask = np.zeros((P, TP), np.float32)
    mask[:, TP - P:] = np.where(np.arange(P)[None, :] > np.arange(P)[:, None], MASKED, 0.0)
    arrays = {
        "x": g["x"],
        "ident": np.eye(P, dtype=np.float32),
        "wcT": g[t0 + "w_compress"][:, :, 0].T, "bc": g[t0 + "b_compress"][:, None],
        "wmT": g[t0 + "w_main"].transpose(2, 1, 0), "bm": g[t0 + "b_main"][:, None],
        "weT": np.concatenate([g[t0 + "w_expand"][:, :, 0].T, g[t0 + "b_expand"][None, :]]),
        "wf1T": g[t0 + "w_ff1"].T, "bf1": g[t0 + "b_ff1"][:, None],
        "wf2T": np.concatenate([g[t0 + "w_ff2"].T, g[t0 + "b_ff2"][None, :]]),
        "norms": np.stack([g[t0 + "g_conv_norm"], g[t0 + "b_conv_norm"], g[t0 + "g_ff_norm"], g[t0 + "b_ff_norm"]], axis=1),
        "wqk": wqk, "wv0": wv, "cos": cos, "sin": sin, "mask": mask,
        "ew0": g["L0_ffn_expert_weights"], "ei0": g["L0_ffn_expert_indices"],
        "w1": g["L0_ffn_w1"], "w2": g["L0_ffn_w2"],
        "wqT": g["L1_attn_Wq"].T, "wkT": g["L1_attn_Wk"].T, "wvT": g["L1_attn_Wv"].T,
        "wgate": np.concatenate([g["L1_ffn_Wr"], g["L1_ffn_Wgate"].transpose(1, 0, 2).reshape(D, E1)], axis=1),
        "bgate": np.concatenate([g["L1_ffn_br"], g["L1_ffn_bgate"].reshape(E1)])[None, :],
        "before": np.triu(np.ones((P, P), np.float32), 1), "block_row": np.arange(BLOCKS, dtype=np.float32)[None, :] * P,
        "W1": g["L1_ffn_W1"], "W3": g["L1_ffn_W3"], "W2": g["L1_ffn_W2"],
    }
    arrays = {k: np.ascontiguousarray(v) for k, v in arrays.items()}
    nc = bacc.Bacc("TRN2", target_bir_lowering=False, num_devices=1)
    aps = {k: nc.dram_tensor(f"in_{k}", v.shape, mybir.dt.from_np(v.dtype), kind="ExternalInput").ap()
           for k, v in arrays.items()}
    out = nc.dram_tensor("out", (B, T, D), F32, kind="ExternalOutput").ap()
    audio_tower(nc, aps, out)
    r = run_bass_kernel_spmd(nc, [{f"in_{k}": v for k, v in arrays.items()}], core_ids=[0])
    return r.results[0]["out"]
```

```python
from contextlib import ExitStack

import numpy as np

import concourse.bass as bass
from concourse import mybir

F32 = mybir.dt.float32
I32 = mybir.dt.int32
BF16 = mybir.dt.bfloat16
ALU = mybir.AluOpType
ACT = mybir.ActivationFunctionType
AX = mybir.AxisListType

B, T_IN, D = 8, 750, 128
T = T_IN - 2
P = 128
NJ = -(-T // P)
TP = NJ * P
LAST = T - (NJ - 1) * P
LAST_IN = T_IN - (NJ - 1) * P
BN = 64
EPS = 1e-5
HEADS, GROUPS, HD = 8, 4, 16
ATT_SCALE = HD ** -0.5
MASKED = -1.0e30
E0, TOPK0, F0, N0 = 8, 2, 512, 1024
E1, G1, PG1, F1 = 16, 4, 4, 512
CHOICES, LISTS, UNROLL = 4, 2, 8
PER_LIST = CHOICES // LISTS
LIST_BLOCKS = (PER_LIST * B * TP + E1 * (P - 1)) // P
LIST_BLOCKS += -LIST_BLOCKS % UNROLL
BLOCKS = LISTS * LIST_BLOCKS
THRESHOLD = 0.9


def batch_rows(dram, b):
    return dram[b][0:(NJ - 1) * P].rearrange("(j p) d -> p j d", p=P), dram[b][(NJ - 1) * P:]


def normalise(dve, consts, src, out, stats, moments, rstd, sems, turn):
    find_moments(dve, consts.carrier[:, 0:1], src, stats, moments, sems, turn)
    scale_tokens(dve, src, out, moments, rstd, sems, turn)


def find_moments(dve, carrier, src, stats, moments, sems, turn):
    stats_done, moments_done, _, _ = sems
    tiles = src.shape[1]
    for j in range(tiles):
        ins = dve.bn_stats(stats[:, j, :], src[:, j, :])
    ins.then_inc(stats_done, 1)
    dve.wait_ge(stats_done, turn)
    dve.memset(carrier, 0.0)
    for j in range(tiles):
        ins = dve.bn_aggr(moments[:, j, :], stats[:, j, :])
    ins.then_inc(moments_done, 1)


def scale_tokens(dve, src, out, moments, rstd, sems, turn):
    _, _, rstd_done, out_done = sems
    tiles = src.shape[1]
    dve.wait_ge(rstd_done, turn)
    for j in range(tiles):
        ins = dve.tensor_scalar(out[:, j, :], src[:, j, :], moments[:, j, 0:1], rstd[:, j:j + 1],
                                ALU.subtract, ALU.mult)
    ins.then_inc(out_done, 1)


def invert_deviation(pool, moments, rstd, consts, sems, turn):
    stats_done, moments_done, rstd_done, _ = sems
    tiles = moments.shape[1]
    pool.wait_ge(moments_done, 2 * turn - 1)
    pool.tensor_tensor(moments[:, :, 1], moments[:, :, 1], consts.eps[:, 0:tiles], ALU.add).then_inc(moments_done, 1)
    pool.wait_ge(moments_done, 2 * turn)
    pool.tensor_tensor(rstd[:, :], moments[:, :, 1], consts.minus_half[:, 0:tiles], ALU.pow).then_inc(rstd_done, 1)


def token_mixer(nc, x, w, hidden, ident, consts, psum):
    with ExitStack() as ctx:
        def sb(name, shape, n=2):
            return [ctx.enter_context(nc.sbuf_tensor(f"{name}{u}", shape, F32)) for u in range(n)]

        def sem(name):
            return ctx.enter_context(nc.semaphore(name))

        def two(name):
            return [sem(f"{name}{u}") for u in range(2)]

        x_in = sb("tm_x", [P, NJ, P])
        xT = sb("tm_xT", [P, TP])
        taps = sb("tm_taps", [P, T_IN + 2])
        mixed = sb("tm_mixed", [BN + 1, TP])
        y0 = sb("tm_y0", [P, NJ, P])
        yhat = sb("tm_yhat", [P, NJ, P])
        y1T = sb("tm_y1T", [P, TP])
        ff = sb("tm_ff", [BN + 1, TP])
        y2T = sb("tm_y2T", [P, TP])
        pool_a = sb("tm_pool_a", [P, TP])
        pooledT = sb("tm_pooledT", [P, TP])
        stats = sb("tm_stats", [P, NJ, 6])
        moments = sb("tm_moments", [P, NJ, 2])
        rstd = sb("tm_rstd", [P, NJ])
        wc = ctx.enter_context(nc.sbuf_tensor("tm_wc", [P, P], F32))
        wm01 = ctx.enter_context(nc.sbuf_tensor("tm_wm01", [P, BN], F32))
        wm2 = ctx.enter_context(nc.sbuf_tensor("tm_wm2", [BN, BN], F32))
        we = ctx.enter_context(nc.sbuf_tensor("tm_we", [BN + 1, P], F32))
        wf1 = ctx.enter_context(nc.sbuf_tensor("tm_wf1", [P, BN], F32))
        wf2 = ctx.enter_context(nc.sbuf_tensor("tm_wf2", [BN + 1, P], F32))
        vec = ctx.enter_context(nc.sbuf_tensor("tm_vec", [P, 7], F32))
        bc, bm, bf1, g_conv, b_conv, g_ff, b_ff = (vec[:, i:i + 1] for i in range(7))

        weights_in = sem("tm_weights_in")
        zeros_set = sem("tm_zeros_set")
        x_loaded = two("tm_x_loaded")
        xT_ps, xT_ready = sem("tm_xT_ps"), sem("tm_xT_ready")
        comp_ps, taps_ready = sem("tm_comp_ps"), sem("tm_taps_ready")
        mix_ps, mixed_ready = sem("tm_mix_ps"), sem("tm_mixed_ready")
        exp_ps, y0_ready = sem("tm_exp_ps"), sem("tm_y0_ready")
        norm1, norm2 = ([[sem(f"tm_norm{k}_{s}{u}") for s in ("stats", "moments", "rstd", "out")] for u in range(2)]
                        for k in (1, 2))
        y1T_ps, y1T_ready = sem("tm_y1T_ps"), sem("tm_y1T_ready")
        ff_ps, ff_ready = sem("tm_ff_ps"), sem("tm_ff_ready")
        out_ps = sem("tm_out_ps")
        y2T_ps, y2T_ready = sem("tm_y2T_ps"), sem("tm_y2T_ready")
        pool_half, pooled_ready = sem("tm_pool_half"), sem("tm_pooled_ready")
        h_ps, h_ready = sem("tm_h_ps"), sem("tm_h_ready")

        def banks(step, u):
            k = 4 * (step % 2) + 2 * u
            return psum[:, k:k + 2, :]

        def tiles_of(step, u):
            return banks(step, u).rearrange("p k n -> p (k n)")[:, 0:TP].rearrange("p (j n) -> p j n", n=P)

        HALF_IN = T_IN // 2

        with nc.Block() as block:
            @block.sync
            def _(sp):
                for dst, src in ((wc[:, 0:BN], w["wcT"]), (wc[:, BN:P], w["wcT"]),
                                 (wm01[0:BN, :], w["wmT"][0]), (wm01[BN:P, :], w["wmT"][1]), (wm2[:, :], w["wmT"][2]),
                                 (we[:, :], w["weT"]), (wf1[:, :], w["wf1T"]), (wf2[:, :], w["wf2T"]),
                                 (vec[0:BN, 0:1], w["bc"]), (vec[BN:P, 0:1], w["bc"]),
                                 (vec[0:BN, 1:2], w["bm"]), (vec[0:BN, 2:3], w["bf1"]),
                                 (vec[:, 3:7], w["norms"])):
                    sp.dma_start(dst, src).then_inc(weights_in, 16)
                sp.wait_ge(zeros_set, 1)
                for u in range(2):
                    whole, rest = batch_rows(x, u)
                    sp.dma_start(x_in[u][:, 0:NJ - 1, :], whole).then_inc(x_loaded[u], 16)
                    sp.dma_start(x_in[u][0:LAST_IN, NJ - 1, :], rest).then_inc(x_loaded[u], 16)
                with sp.Fori(1, B // 2) as i:
                    for u in range(2):
                        sp.wait_ge(y0_ready, 2 * i + u - 1)
                        whole, rest = batch_rows(x, 2 * i + u)
                        sp.dma_start(x_in[u][:, 0:NJ - 1, :], whole).then_inc(x_loaded[u], 16)
                        sp.dma_start(x_in[u][0:LAST_IN, NJ - 1, :], rest).then_inc(x_loaded[u], 16)

            @block.gpsimd
            def _(pool):
                with pool.Fori(0, B // 2) as i:
                    for norm in (norm1, norm2):
                        for u in range(2):
                            invert_deviation(pool, moments[u], rstd[u], consts, norm[u], i + 1)

            @block.tensor
            def _(pe):
                pe.wait_ge(weights_in, 16 * 13)
                pe.wait_ge(zeros_set, 2)
                with pe.Fori(0, B // 2) as i:
                    for u in range(2):
                        pe.wait_ge(x_loaded[u], 32 * i + 32)
                        pe.wait_ge(h_ready, 2 * i + u + 1)
                        for j in range(NJ):
                            ins = pe.transpose(tiles_of(0, u)[:, j, :], x_in[u][:, j, :], ident)
                        ins.then_inc(xT_ps, 1)
                    for u in range(2):
                        pe.wait_ge(xT_ready, 2 * i + u + 1)
                        for h in range(2):
                            ins = pe.matmul(banks(1, u)[:, h, 0:HALF_IN], wc[:, :], xT[u][:, h * HALF_IN:(h + 1) * HALF_IN],
                                            start=True, stop=True)
                        ins.then_inc(comp_ps, 1)
                    for u in range(2):
                        pe.wait_ge(taps_ready, 2 * (2 * i + u + 1))
                        for h in range(2):
                            pe.matmul(banks(2, u)[0:BN, h, 0:HALF_IN], wm01[:, :], taps[u][:, h * HALF_IN:(h + 1) * HALF_IN],
                                      start=True, stop=False)
                            ins = pe.matmul(banks(2, u)[0:BN, h, 0:HALF_IN], wm2[:, :],
                                            taps[u][0:BN, h * HALF_IN + 2:(h + 1) * HALF_IN + 2], start=False, stop=True)
                        ins.then_inc(mix_ps, 1)
                    for u in range(2):
                        pe.wait_ge(mixed_ready, 2 * i + u + 1)
                        for j in range(NJ):
                            ins = pe.matmul(tiles_of(3, u)[:, j, :], mixed[u][:, j * P:(j + 1) * P], we[:, :], start=True, stop=True)
                        ins.then_inc(exp_ps, 1)
                    for u in range(2):
                        pe.wait_ge(norm1[u][3], i + 1)
                        for j in range(NJ):
                            ins = pe.transpose(tiles_of(4, u)[:, j, :], yhat[u][:, j, :], ident)
                        ins.then_inc(y1T_ps, 1)
                    for u in range(2):
                        pe.wait_ge(y1T_ready, 2 * i + u + 1)
                        for h in range(2):
                            ins = pe.matmul(banks(5, u)[0:BN, h, 0:TP // 2], wf1[:, :], y1T[u][:, h * TP // 2:(h + 1) * TP // 2],
                                            start=True, stop=True)
                        ins.then_inc(ff_ps, 1)
                    for u in range(2):
                        pe.wait_ge(ff_ready, 2 * i + u + 1)
                        for j in range(NJ):
                            pe.matmul(tiles_of(6, u)[:, j, :], ff[u][:, j * P:(j + 1) * P], wf2[:, :], start=True, stop=False)
                            ins = pe.matmul(tiles_of(6, u)[:, j, :], y1T[u][:, j * P:(j + 1) * P], ident, start=False, stop=True)
                        ins.then_inc(out_ps, 1)
                    for u in range(2):
                        pe.wait_ge(norm2[u][3], i + 1)
                        for j in range(NJ):
                            ins = pe.transpose(tiles_of(7, u)[:, j, :], yhat[u][:, j, :], ident)
                        ins.then_inc(y2T_ps, 1)
                    for u in range(2):
                        pe.wait_ge(pooled_ready, 2 * i + u + 1)
                        for j in range(NJ):
                            ins = pe.transpose(tiles_of(8, u)[:, j, :], pooledT[u][:, j * P:(j + 1) * P], ident)
                        ins.then_inc(h_ps, 1)

            @block.scalar
            def _(act):
                act.wait_ge(weights_in, 16 * 13)
                act.wait_ge(zeros_set, 2)
                with act.Fori(0, B // 2) as i:
                    for u in range(2):
                        act.wait_ge(comp_ps, 2 * i + u + 1)
                        act.activation(taps[u][0:BN, 1:T_IN + 1].rearrange("p (h n) -> p h n", h=2),
                                       banks(1, u)[0:BN, :, 0:HALF_IN], ACT.Silu, bias=bc[0:BN]).then_inc(taps_ready, 1)
                        act.activation(taps[u][BN:P, 0:T_IN].rearrange("p (h n) -> p h n", h=2),
                                       banks(1, u)[BN:P, :, 0:HALF_IN], ACT.Silu, bias=bc[BN:P]).then_inc(taps_ready, 1)
                    for u in range(2):
                        act.wait_ge(mix_ps, 2 * i + u + 1)
                        act.activation(mixed[u][0:BN, 0:T_IN].rearrange("p (h n) -> p h n", h=2),
                                       banks(2, u)[0:BN, :, 0:HALF_IN], ACT.Silu, bias=bm[0:BN]).then_inc(mixed_ready, 1)
                    for u in range(2):
                        act.wait_ge(ff_ps, 2 * i + u + 1)
                        act.activation(ff[u][0:BN, :].rearrange("p (h n) -> p h n", h=2),
                                       banks(5, u)[0:BN, :, 0:TP // 2], ACT.Gelu, bias=bf1[0:BN]).then_inc(ff_ready, 1)
                    for u in range(2):
                        act.wait_ge(h_ps, 2 * i + u + 1)
                        act.activation(hidden[:, bass.ds((2 * i + u) * NJ, NJ), :], tiles_of(8, u), ACT.Copy).then_inc(h_ready, 1)

            @block.vector
            def _(dve):
                for u in range(2):
                    dve.memset(x_in[u][96:P, NJ - 1, :], 0.0)
                    dve.memset(taps[u][:, :], 0.0)
                    dve.memset(mixed[u][:, :], 0.0)
                    dve.memset(pooledT[u][:, :], 0.0)
                    dve.memset(ff[u][BN:BN + 1, :], 1.0)
                    dve.memset(pool_a[u][:, :], 0.0)
                dve.memset(y2T[0][:, :], 0.0).then_inc(zeros_set, 1)
                dve.memset(y2T[1][:, :], 0.0).then_inc(h_ready, 2)
                dve.wait_ge(zeros_set, 1)
                for u in range(2):
                    ins = dve.memset(mixed[u][BN:BN + 1, :], 1.0)
                ins.then_inc(zeros_set, 1)
                dve.wait_ge(weights_in, 16 * 13)
                with dve.Fori(0, B // 2) as i:
                    for u in range(2):
                        dve.wait_ge(xT_ps, 2 * i + u + 1)
                        dve.tensor_copy(xT[u][:, :].rearrange("p (j n) -> p j n", n=P), tiles_of(0, u)).then_inc(xT_ready, 1)
                    for u in range(2):
                        dve.wait_ge(exp_ps, 2 * i + u + 1)
                        dve.tensor_tensor(y0[u][:, :, :], tiles_of(3, u), x_in[u][:, :, :], ALU.add).then_inc(y0_ready, 1)
                        dve.wait_ge(y0_ready, 2 * i + u + 1)
                        find_moments(dve, consts.carrier[:, u:u + 1], y0[u], stats[u], moments[u], norm1[u], i + 1)
                    for u in range(2):
                        scale_tokens(dve, y0[u], yhat[u], moments[u], rstd[u], norm1[u], i + 1)
                    for u in range(2):
                        dve.wait_ge(y1T_ps, 2 * i + u + 1)
                        dve.tensor_scalar(y1T[u][:, :].rearrange("p (j n) -> p j n", n=P), tiles_of(4, u), g_conv, b_conv,
                                          ALU.mult, ALU.add).then_inc(y1T_ready, 1)
                    for u in range(2):
                        dve.wait_ge(out_ps, 2 * i + u + 1)
                        find_moments(dve, consts.carrier[:, 2 + u:3 + u], tiles_of(6, u), stats[u], moments[u], norm2[u], i + 1)
                    for u in range(2):
                        scale_tokens(dve, tiles_of(6, u), yhat[u], moments[u], rstd[u], norm2[u], i + 1)
                    for u in range(2):
                        dve.wait_ge(y2T_ps, 2 * i + u + 1)
                        dve.tensor_scalar(y2T[u][:, :].rearrange("p (j n) -> p j n", n=P), tiles_of(7, u), g_ff, b_ff,
                                          ALU.mult, ALU.add).then_inc(y2T_ready, 1)
                    for u in range(2):
                        n = 2 * i + u + 1
                        dve.wait_ge(y2T_ready, n)
                        dve.tensor_tensor(pool_a[u][:, 0:T], y2T[u][:, 0:T], y2T[u][:, 1:T + 1], ALU.max).then_inc(pool_half, 1)
                        dve.wait_ge(pool_half, n)
                        dve.tensor_tensor(pooledT[u][:, 0:T], pool_a[u][:, 0:T], y2T[u][:, 2:T + 2], ALU.max).then_inc(pooled_ready, 1)



def rope_attention(nc, w, hidden, ident, consts, psum):
    UNITS = [(j, g, p) for j in range(NJ) for g in range(GROUPS) for p in range(2)]
    NU, PAIRS = len(UNITS), len(UNITS) // 2
    PREP = 8
    AFTER_UNIT = (6, 9, 11, 13, 15, 17, 19, 21)
    STATS_AT, APPLY_AT = 1, 4
    SLOTS, AT_SLOT = [], []
    for n in range(NU):
        AT_SLOT.append(len(SLOTS))
        SLOTS.append(("unit", n))
        SLOTS += [("prepare", x) for x in range(PREP) if AFTER_UNIT[x] == n]
    NS = len(SLOTS)
    with ExitStack() as ctx:
        def sb(name, shape, n=1):
            t = [ctx.enter_context(nc.sbuf_tensor(f"{name}{u}", shape, F32)) for u in range(n)]
            return t if n > 1 else t[0]

        def sem(name):
            return ctx.enter_context(nc.semaphore(name))

        hn = sb("ra_hn", [P, NJ, P])
        hnT = sb("ra_hnT", [P, TP])
        stats, moments, rstd = sb("ra_stats", [P, NJ, 6]), sb("ra_moments", [P, NJ, 2]), sb("ra_rstd", [P, NJ])
        cos, sin = sb("ra_cos", [P, 3, TP]), sb("ra_sin", [P, 3, TP])
        wqk = sb("ra_wqk", [P, 3, 2, P])
        wv = sb("ra_wv", [P, P])
        mask = sb("ra_mask", [P, TP])
        by_cos, by_sin = sb("ra_by_cos", [P, 3, TP]), sb("ra_by_sin", [P, 3, TP])
        v_next = sb("ra_v_next", [P, NJ, P])
        qk = sb("ra_qk", [P, 3, TP])
        v = sb("ra_v", [P, NJ, P])
        scaled = sb("ra_scaled", [P, TP], 3)
        least = sb("ra_least", [P, 3])
        prob = sb("ra_prob", [P, TP], 2)
        probT = sb("ra_probT", [P, NJ, 2, P], 2)
        sums = sb("ra_sums", [P, NU])
        recip = sb("ra_recip", [P, NU])
        outT = sb("ra_outT", [P, 2 * P], 2)
        att = sb("ra_att", [P, NU, HD])
        rows = sb("ra_rows", [P, NJ, P])

        consts_in = sem("ra_consts_in")
        norm = [sem(f"ra_norm_{s}") for s in ("stats", "moments", "rstd", "out")]
        slot_ps, slot_read = sem("ra_slot_ps"), sem("ra_slot_read")
        k_q0_ready, q1_ready, v_ready = sem("ra_k_q0_ready"), sem("ra_q1_ready"), sem("ra_v_ready")
        prob_ready, probT_ps = sem("ra_prob_ready"), sem("ra_probT_ps")
        probT_ready = [sem("ra_probT_ready_by_vector"), sem("ra_probT_ready_by_scalar")]
        pv_done = sem("ra_pv_done")
        outT_ready, out_ps = sem("ra_outT_ready"), sem("ra_out_ps")
        recip_ready, att_ready, att_stored = sem("ra_recip_ready"), sem("ra_att_ready"), sem("ra_att_stored")
        rows_loaded, h_ready = sem("ra_rows_loaded"), sem("ra_h_ready")
        by_head = nc.dram_tensor("att_by_head", (B, HEADS, T, HD), F32, kind="Internal").ap()
        by_row = by_head.rearrange("b h t c -> b (h t c)").rearrange("b (t d) -> b t d", d=D)

        flat = psum[:, :, :].rearrange("p k n -> p (k n)")
        HALF = TP // 2

        def bank_pair(k):
            return flat[:, k * 512:k * 512 + TP]

        def slots_before(b):
            return PREP + NS * b

        def turned_bank(n):
            return bank_pair(5 if UNITS[n][0] < 4 and n % 2 else 4)

        def slots_of(prepares):
            return [s for s in SLOTS if prepares or s[0] == "unit"]

        def slot_of(n, prepares):
            return AT_SLOT[n] if prepares else n

        with nc.Block() as block:
            @block.sync
            def _(sp):
                for dst, src in ((cos[:, :, :], w["cos"]), (sin[:, :, :], w["sin"]), (wqk[:, :, :, :], w["wqk"]),
                                 (wv[:, :], w["wv0"]), (mask[:, :], w["mask"])):
                    sp.dma_start(dst, src).then_inc(consts_in, 16)

                def store(b):
                    for j in range(NJ):
                        sp.wait_ge(att_ready, NJ * b + j + 3)
                        n = min(P, T - j * P)
                        sp.dma_start(by_head[b][:, j * P:j * P + n, :].rearrange("h t c -> t h c"),
                                     att[0:n, j * HEADS:(j + 1) * HEADS, :]).then_inc(att_stored, 16)

                def load_rows(b):
                    whole, rest = batch_rows(by_row, b)
                    sp.dma_start(rows[:, 0:NJ - 1, :], whole).then_inc(rows_loaded, 16)
                    sp.dma_start(rows[0:LAST, NJ - 1, :], rest).then_inc(rows_loaded, 16)

                store(0)
                with sp.Fori(0, B - 1) as b:
                    sp.wait_ge(att_stored, 16 * NJ * (b + 2))
                    sp.wait_ge(h_ready, 2 * b + 2)
                    load_rows(b)
                    store(b + 1)
                sp.wait_ge(att_stored, 16 * NJ * (B + 1))
                sp.wait_ge(h_ready, 2 * B)
                load_rows(B - 1)

            @block.tensor
            def _(pe):
                def prepare(x, slot, batch):
                    k = 2 * (slot % 2)
                    if x == 0:
                        pe.wait_ge(norm[3], batch + 1)
                        for j in range(NJ):
                            ins = pe.transpose(bank_pair(k)[:, j * P:(j + 1) * P], hn[:, j, :], ident)
                    elif x == 1:
                        for j in range(NJ):
                            ins = pe.matmul(bank_pair(k)[:, j * P:(j + 1) * P], hnT[:, j * P:(j + 1) * P], wv[:, :], start=True, stop=True)
                    else:
                        s, h = (x - 2) // 2, x % 2
                        for side in range(2):
                            ins = pe.matmul(psum[:, k + side, 0:HALF], wqk[:, s, side, :], hnT[:, h * HALF:(h + 1) * HALF],
                                            start=True, stop=True)
                    ins.then_inc(slot_ps, 1)

                def attend(b, first=False, last=False):
                    prepares = not last
                    base, slots = slots_before(b), slots_of(prepares)

                    def fill(slot):
                        kind, n = slots[slot]
                        pe.wait_ge(slot_read, base + slot - 1)
                        if kind == "prepare":
                            if n == 1:
                                pe.wait_ge(slot_read, base + slots.index(("prepare", 0)) + 1)
                            prepare(n, slot, b + 1)
                            return
                        j, g, p = UNITS[n]
                        for lo in range(0, (j + 1) * P, 512):
                            hi = min(lo + 512, (j + 1) * P)
                            ins = pe.matmul(bank_pair(2 * (slot % 2))[:, lo:hi], qk[32 * g:32 * g + 32, p, j * P:(j + 1) * P],
                                            qk[32 * g:32 * g + 32, 2, lo:hi], start=True, stop=True)
                        ins.then_inc(slot_ps, 1)

                    def turn(n):
                        j = UNITS[n][0]
                        pe.wait_ge(prob_ready, NU * b + n + 1)
                        if (n >= 2 or not first) and (j < 4 or n == 4 * HEADS):
                            pe.wait_ge(probT_ready[n % 2], PAIRS * b + n // 2)
                        if n == 0 and not first:
                            pe.wait_ge(probT_ready[1], PAIRS * b)
                        if j >= 4:
                            pe.wait_ge(probT_ready[(n - 1) % 2], PAIRS * b + (n - 1) // 2 + 1)
                        for k in range(j + 1):
                            ins = pe.transpose(turned_bank(n)[:, k * P:(k + 1) * P], prob[n % 2][:, k * P:(k + 1) * P], ident)
                        ins.then_inc(probT_ps, 1)

                    def values(m):
                        j, g, _ = UNITS[2 * m]
                        pe.wait_ge(probT_ready[0], PAIRS * b + m + 1)
                        pe.wait_ge(probT_ready[1], PAIRS * b + m + 1)
                        if g == 0:
                            pe.wait_ge(att_ready, NJ * b + j + 1)
                        for k in range(j + 1):
                            ins = pe.matmul(psum[32 * g:32 * g + 32, 6 + j % 2, 0:2 * P],
                                            v[:, k, 32 * g:32 * g + 32], probT[m % 2][:, k, :, :].rearrange("q p n -> q (p n)"),
                                            start=(k == 0), stop=(k == j))
                        ins.then_inc(pv_done, 1)

                    def turn_back(j):
                        pe.wait_ge(outT_ready, NJ * b + j + 1)
                        for p in range(2):
                            ins = pe.transpose(psum[:, 6 + j % 2, (2 + p) * P:(3 + p) * P], outT[j % 2][:, p * P:(p + 1) * P], ident)
                        ins.then_inc(out_ps, 1)

                    pe.wait_ge(k_q0_ready, 2 * b + 2)
                    filled = 0
                    for n in range(-2, NU):
                        until = slot_of(min(n + 2, NU - 1), prepares) + 1
                        for slot in range(filled, until):
                            if slot == 1:
                                pe.wait_ge(q1_ready, b + 1)
                            fill(slot)
                        filled = until
                        if n >= 0:
                            turn(n)
                        if n == 2:
                            pe.wait_ge(v_ready, b + 1)
                        if n % 2 == 0 and (n >= 2 or n == 0 and not first):
                            values(n // 2 - 1)
                        if n % 8 == 4 and (n >= 12 or not first):
                            turn_back(n // 8 - 1)
                    if last:
                        values(PAIRS - 1)
                        turn_back(NJ - 1)

                pe.wait_ge(consts_in, 80)
                for x in range(PREP):
                    if x >= 2 or x == 1:
                        pe.wait_ge(slot_read, max(x - 1, 1))
                    prepare(x, x, 0)
                attend(0, first=True)
                with pe.Fori(1, B - 1) as b:
                    attend(b)
                attend(B - 1, last=True)

            @block.scalar
            def _(act):
                def attend(b, first=False, last=False):
                    prepares = not last

                    def turned(n):
                        width = UNITS[n][0] + 1
                        act.wait_ge(probT_ps, NU * b + n + 1)
                        if n >= 4 or not first:
                            act.wait_ge(pv_done, PAIRS * b + n // 2 - 1)
                        act.activation(probT[n // 2 % 2][:, 0:width, n % 2, :],
                                       turned_bank(n)[:, 0:width * P].rearrange("q (k n) -> q k n", n=P), ACT.Copy).then_inc(probT_ready[1], 1)

                    def out_of_tile(j):
                        act.wait_ge(pv_done, PAIRS * b + GROUPS * (j + 1))
                        act.activation(outT[j % 2][:, :], psum[:, 6 + j % 2, 0:2 * P], ACT.Copy).then_inc(outT_ready, 1)

                    for n in range(NU):
                        j, g, p = UNITS[n]
                        width = (j + 1) * P
                        act.wait_ge(slot_read, slots_before(b) + slot_of(n, prepares) + 1)
                        if n >= 2 or not first:
                            act.wait_ge(probT_ps, NU * b + n - 1)
                        at = j * HEADS + GROUPS * p + g
                        act.activation(prob[n % 2][:, 0:width], scaled[n % 3][:, 0:width], ACT.Exp, bias=least[:, n % 3:n % 3 + 1],
                                       scale=-1.0, accum_out=sums[:, at:at + 1]).then_inc(prob_ready, 1)
                        if n >= 2 and n % 2 == 0:
                            turned(n - 1)
                        if n % 8 == 2 and (n >= 10 or not first):
                            out_of_tile(n // 8 - 1)
                        if n == 1:
                            act.wait_ge(slot_read, slots_before(b))
                            if not first:
                                act.wait_ge(pv_done, PAIRS * b)
                            act.activation(v[:, :, :], v_next[:, :, :], ACT.Copy).then_inc(v_ready, 1)
                    turned(NU - 1)
                    if last:
                        out_of_tile(NJ - 1)

                attend(0, first=True)
                with act.Fori(1, B - 1) as b:
                    attend(b)
                attend(B - 1, last=True)

            @block.vector
            def _(dve):
                def statistics(batch):
                    for j in range(NJ):
                        ins = dve.bn_stats(stats[:, j, :], hidden[:, bass.ds(batch * NJ + j, 1), :].rearrange("p o n -> p (o n)"))
                    ins.then_inc(norm[0], 1)
                    dve.wait_ge(norm[0], batch + 1)
                    dve.memset(consts.carrier[:, 0:1], 0.0)
                    for j in range(NJ):
                        ins = dve.bn_aggr(moments[:, j, :], stats[:, j, :])
                    ins.then_inc(norm[1], 1)

                def apply(batch):
                    dve.wait_ge(norm[2], batch + 1)
                    for j in range(NJ):
                        ins = dve.tensor_scalar(hn[:, j, :], hidden[:, bass.ds(batch * NJ + j, 1), :].rearrange("p o n -> p (o n)"),
                                                moments[:, j, 0:1], rstd[:, j:j + 1], ALU.subtract, ALU.mult)
                    ins.then_inc(norm[3], 1)

                def stage(x, slot, batch, first=False):
                    k = 2 * (slot % 2)
                    if x == 0:
                        ins = dve.tensor_copy(hnT[:, :], bank_pair(k))
                    elif x == 1:
                        if not first:
                            dve.wait_ge(v_ready, batch)
                        ins = dve.tensor_copy(v_next[:, :, :].rearrange("p j n -> p (j n)"), bank_pair(k))
                    else:
                        s, h = (x - 2) // 2, x % 2
                        if x == 4 and not first:
                            dve.wait_ge(q1_ready, batch)
                        for side, table, out in ((0, cos, by_cos), (1, sin, by_sin)):
                            ins = dve.tensor_tensor(out[:, s, h * HALF:(h + 1) * HALF], psum[:, k + side, 0:HALF],
                                                    table[:, s, h * HALF:(h + 1) * HALF], ALU.mult)
                    ins.then_inc(slot_read, 1)

                def take_staged(b):
                    dve.wait_ge(slot_read, slots_before(b))
                    dve.tensor_tensor(qk[:, 2, :], by_cos[:, 2, :], by_sin[:, 2, :], ALU.add).then_inc(k_q0_ready, 1)
                    dve.tensor_tensor(qk[:, 0, :], by_cos[:, 0, :], by_sin[:, 0, :], ALU.add).then_inc(k_q0_ready, 1)

                def attend(b, first=False, last=False):
                    prepares = not last
                    base = slots_before(b)

                    def turned(n):
                        width = UNITS[n][0] + 1
                        dve.wait_ge(probT_ps, NU * b + n + 1)
                        if n >= 4 or not first:
                            dve.wait_ge(pv_done, PAIRS * b + n // 2 - 1)
                        dve.tensor_copy(probT[n // 2 % 2][:, 0:width, n % 2, :],
                                        turned_bank(n)[:, 0:width * P].rearrange("q (k n) -> q k n", n=P)).then_inc(probT_ready[0], 1)

                    def normalised_output(j):
                        dve.wait_ge(prob_ready, NU * b + HEADS * (j + 1))
                        here = slice(j % NJ * HEADS, (j % NJ + 1) * HEADS)
                        dve.reciprocal(recip[:, here], sums[:, here]).then_inc(recip_ready, 1)
                        if j == 0:
                            dve.wait_ge(att_stored, 16 * NJ * (b + 1))
                        dve.wait_ge(out_ps, NJ * b + j + 1)
                        dve.wait_ge(recip_ready, NJ * b + j + 1)
                        dve.tensor_tensor(att[:, here, :],
                                          psum[:, 6 + j % 2, 2 * P:4 * P].rearrange("q (n c) -> q n c", c=32)[:, :, 0:HD],
                                          recip[:, here].rearrange("p (n o) -> p n o", o=1).broadcast_to([P, HEADS, HD]),
                                          ALU.mult).then_inc(att_ready, 1)

                    for slot, (kind, n) in enumerate(slots_of(prepares)):
                        if kind == "prepare":
                            dve.wait_ge(slot_ps, base + slot + 1)
                            stage(n, slot, b + 1)
                            continue
                        j, g, p = UNITS[n]
                        width = (j + 1) * P
                        dve.wait_ge(slot_ps, base + slot + 1)
                        if n >= 3 or not first:
                            dve.wait_ge(prob_ready, NU * b + n - 2)
                        dve.memset(consts.carrier[:, 1 + n % 4:2 + n % 4], 0.0)
                        dve.tensor_tensor_reduce(scaled[n % 3][:, 0:width], bank_pair(2 * (slot % 2))[:, 0:width],
                                                 mask[:, TP - width:TP], -ATT_SCALE, -MASKED, ALU.add, ALU.min,
                                                 least[:, n % 3:n % 3 + 1]).then_inc(slot_read, 1)
                        if n >= 2 and n % 2 == 0:
                            turned(n - 2)
                        if n % 8 == 6 and (n >= 14 or not first):
                            normalised_output(n // 8 - 1)
                        if prepares and n == STATS_AT:
                            statistics(b + 1)
                        if prepares and n == APPLY_AT:
                            apply(b + 1)
                    if prepares:
                        take_staged(b + 1)
                    turned(NU - 2)
                    if last:
                        normalised_output(NJ - 1)

                dve.memset(recip[:, :], 0.0).then_inc(att_ready, 2)
                dve.memset(att[:, :, :], 0.0).then_inc(att_stored, 16 * NJ)
                dve.memset(least[:, :], 0.0).then_inc(h_ready, 2)
                dve.wait_ge(consts_in, 80)
                statistics(0)
                apply(0)
                for x in range(PREP):
                    dve.wait_ge(slot_ps, x + 1)
                    stage(x, x, 0, first=True)
                take_staged(0)
                attend(0, first=True)
                with dve.Fori(1, B - 1) as b:
                    attend(b)
                attend(B - 1, last=True)

            @block.gpsimd
            def _(pool):
                def take_second_queries(b):
                    pool.wait_ge(slot_read, slots_before(b))
                    pool.tensor_tensor(qk[:, 1, :], by_cos[:, 1, :], by_sin[:, 1, :], ALU.add).then_inc(q1_ready, 1)

                def add_rows(b):
                    pool.wait_ge(rows_loaded, 32 * (b + 1))
                    first = b * NJ
                    pool.tensor_tensor(hidden[:, bass.ds(first, NJ - 1), :], hidden[:, bass.ds(first, NJ - 1), :],
                                       rows[:, 0:NJ - 1, :], ALU.add).then_inc(h_ready, 1)
                    pool.tensor_tensor(hidden[0:LAST, bass.ds(first + NJ - 1, 1), :], hidden[0:LAST, bass.ds(first + NJ - 1, 1), :],
                                       rows[0:LAST, NJ - 1:NJ, :], ALU.add).then_inc(h_ready, 1)

                invert_deviation(pool, moments, rstd, consts, norm, 1)
                take_second_queries(0)
                invert_deviation(pool, moments, rstd, consts, norm, 2)
                with pool.Fori(0, B - 2) as b:
                    take_second_queries(b + 1)
                    invert_deviation(pool, moments, rstd, consts, norm, b + 3)
                    add_rows(b)
                take_second_queries(B - 1)
                add_rows(B - 2)
                add_rows(B - 1)




def routed_ffn(nc, w, hidden, ident, consts, psum):
    NT = NJ + -(-(N0 - T) // P)
    TC = 3
    VU, NC = NT // TC, F0 // P
    W = TC * P
    with ExitStack() as ctx:
        def sb(name, shape, n=1, dt=F32):
            t = [ctx.enter_context(nc.sbuf_tensor(f"{name}{u}", shape, dt)) for u in range(n)]
            return t if n > 1 else t[0]

        def sem(name):
            return ctx.enter_context(nc.semaphore(name))

        hn, hnT = sb("rf_hn", [P, NT, P]), sb("rf_hnT", [P, NT * P])
        stats, moments, rstd = sb("rf_stats", [P, NT, 6]), sb("rf_moments", [P, NT, 2]), sb("rf_rstd", [P, NT])
        weight, index = sb("rf_weight", [P, NT, TOPK0]), sb("rf_index", [P, NT, TOPK0], dt=I32)
        index_f = sb("rf_index_f", [P, NT, TOPK0])
        chosen = sb("rf_chosen", [P, E0, TOPK0, NT])
        gate = sb("rf_gate", [P, E0, NT])
        gate_now = sb("rf_gate_now", [P, NT], 2)
        w1, w2 = sb("rf_w1", [P, F0], 2), sb("rf_w2", [P, NC, P], 2)
        actT = sb("rf_actT", [P, NC, W], 2)

        norm = [sem(f"rf_norm_{s}") for s in ("stats", "moments", "rstd", "out")]
        w_loaded = [sem("rf_w_loaded0"), sem("rf_w_loaded1")]
        zeroed, routes_in, index_ready, chosen_ready, gate_ready = (
            sem(f"rf_{s}") for s in ("zeroed", "routes_in", "index_ready", "chosen_ready", "gate_ready"))
        hnT_ps, hnT_ready = sem("rf_hnT_ps"), sem("rf_hnT_ready")
        up_ps, act_ready, down_done, added = sem("rf_up_ps"), sem("rf_act_ready"), sem("rf_down_done"), sem("rf_added")
        copied = sem("rf_gate_copied")

        def spans():
            return ((0, (NJ - 1) * P, 0), ((NJ - 1) * P, LAST, NJ - 1),
                    (T, (N0 - T) // P * P, NJ), (T + (N0 - T) // P * P, (N0 - T) % P, NT - 1))

        with nc.Block() as block:
            @block.sync
            def _(sp):
                def load(u, e):
                    sp.dma_start(w1[u][:, :], w["w1"][e]).then_inc(w_loaded[u], 16)
                    sp.dma_start(w2[u][:, :, :], w["w2"][e].rearrange("(k p) d -> p k d", p=P)).then_inc(w_loaded[u], 16)

                sp.wait_ge(zeroed, 1)
                for first, n, tile in spans():
                    for dst, src in ((weight, w["ew0"]), (index, w["ei0"])):
                        if n % P == 0:
                            sp.dma_start(dst[:, tile:tile + n // P, :],
                                         src[first:first + n].rearrange("(j p) k -> p j k", p=P)).then_inc(routes_in, 16)
                        else:
                            sp.dma_start(dst[0:n, tile, :], src[first:first + n]).then_inc(routes_in, 16)
                for u in range(2):
                    load(u, u)
                with sp.Fori(1, E0 // 2) as i:
                    for u in range(2):
                        sp.wait_ge(down_done, VU * (2 * i + u - 1) + 2)
                        load(u, 2 * i + u)

            @block.gpsimd
            def _(pool):
                invert_deviation(pool, moments, rstd, consts, norm, 1)

            @block.vector
            def _(dve):
                dve.memset(weight[:, :, :], 0.0)
                dve.memset(index[:, :, :], 0).then_inc(zeroed, 1)
                dve.memset(index_f[:, :, :], 0.0).then_inc(act_ready, 3)
                dve.memset(gate_now[0][:, :], 0.0).then_inc(down_done, 2)
                dve.memset(gate_now[1][:, :], 0.0).then_inc(added, 2)
                normalise(dve, consts, hidden[:, 0:NT, :], hn, stats, moments, rstd, norm, 1)
                dve.wait_ge(hnT_ps, 1)
                dve.tensor_copy(hnT[:, :], psum[:, :, :].rearrange("p k n -> p (k n)")[:, 0:NT * P]).then_inc(hnT_ready, 1)
                dve.wait_ge(routes_in, 16 * 8)
                dve.tensor_copy(index_f[:, :, :], index[:, :, :]).then_inc(index_ready, 1)
                dve.wait_ge(index_ready, 1)
                for e in range(E0):
                    for k in range(TOPK0):
                        ins = dve.scalar_tensor_tensor(out=chosen[:, e, k, :], in0=index_f[:, :, k], scalar=float(e),
                                                       in1=weight[:, :, k], op0=ALU.is_equal, op1=ALU.mult)
                ins.then_inc(chosen_ready, 1)
                dve.wait_ge(chosen_ready, 1)
                dve.tensor_tensor(gate[:, :, :], chosen[:, :, 0, :], chosen[:, :, 1, :], ALU.add).then_inc(gate_ready, 1)
                dve.wait_ge(gate_ready, 1)
                with dve.Fori(0, E0 // 2) as i:
                    for u in range(2):
                        dve.wait_ge(added, VU * (2 * i + u) + 2)
                        dve.tensor_copy(gate_now[u][:, :].rearrange("p (o n) -> p o n", o=1),
                                        gate[:, bass.ds(2 * i + u, 1), :]).then_inc(copied, 1)
                        dve.wait_ge(copied, 2 * i + u + 1)
                        for c in range(VU):
                            v = VU * u + c
                            V = 2 * VU * i + v
                            dve.wait_ge(down_done, V + 3)
                            dve.wait_ge(added, V + 1)
                            for t in range(TC):
                                tile = TC * c + t
                                ins = dve.scalar_tensor_tensor(
                                    out=hidden[:, tile, :], in0=psum[:, 6 + v % 2, t * P:(t + 1) * P],
                                    scalar=gate_now[u][:, tile:tile + 1], in1=hidden[:, tile, :], op0=ALU.mult, op1=ALU.add)
                            ins.then_inc(added, 1)

            @block.scalar
            def _(act):
                with act.Fori(0, E0 // 2) as i:
                    for v in range(2 * VU):
                        act.wait_ge(down_done, 2 * VU * i + v + 1)
                        for half in range(2):
                            m = 2 * v + half
                            act.wait_ge(up_ps, 4 * VU * i + m + 1)
                            act.activation(actT[v % 2][:, 2 * half:2 * half + 2, :], psum[:, 2 * (m % 3):2 * (m % 3) + 2, 0:W],
                                           ACT.Gelu).then_inc(act_ready, 1)

            @block.tensor
            def _(pe):
                pe.wait_ge(norm[3], 1)
                flat = psum[:, :, :].rearrange("p k n -> p (k n)")
                for j in range(NT):
                    ins = pe.transpose(flat[:, j * P:(j + 1) * P], hn[:, j, :], ident)
                ins.then_inc(hnT_ps, 1)
                pe.wait_ge(hnT_ready, 1)
                pe.wait_ge(added, 2)
                pe.wait_ge(act_ready, 3)
                with pe.Fori(0, E0 // 2) as i:
                    def up(m):
                        u, c, half = m // (2 * VU), m // 2 % VU, m % 2
                        if m % (2 * VU) == 0:
                            pe.wait_ge(w_loaded[u], 32 * i + 32)
                        pe.wait_ge(act_ready, 4 * VU * i + m + 1)
                        for f in range(2):
                            lo = (2 * half + f) * P
                            ins = pe.matmul(psum[:, 2 * (m % 3) + f, 0:W], w1[u][:, lo:lo + P], hnT[:, c * W:(c + 1) * W],
                                            start=True, stop=True)
                        ins.then_inc(up_ps, 1)

                    def down(v):
                        u = v // VU
                        pe.wait_ge(act_ready, 4 * VU * i + 2 * v + 5)
                        pe.wait_ge(added, 2 * VU * i + v + 1)
                        for t in range(TC):
                            for f in range(NC):
                                ins = pe.matmul(psum[:, 6 + v % 2, t * P:(t + 1) * P], actT[v % 2][:, f, t * P:(t + 1) * P],
                                                w2[u][:, f, :], start=(f == 0), stop=(f == NC - 1))
                        ins.then_inc(down_done, 1)

                    up(0)
                    up(1)
                    for v in range(2 * VU):
                        if v + 1 < 2 * VU:
                            up(2 * v + 2)
                            up(2 * v + 3)
                        down(v)


def column_attention(nc, w, hidden, ident, consts, psum):
    HALF = T // 2
    with ExitStack() as ctx:
        def sb(name, shape, n=1, dt=F32):
            t = [ctx.enter_context(nc.sbuf_tensor(f"{name}{u}", shape, dt)) for u in range(n)]
            return t if n > 1 else t[0]

        def sem(name):
            return ctx.enter_context(nc.semaphore(name))

        hn, hnT = sb("ca_hn", [P, NJ, P]), sb("ca_hnT", [P, TP])
        stats, moments, rstd = sb("ca_stats", [P, NJ, 6]), sb("ca_moments", [P, NJ, 2]), sb("ca_rstd", [P, NJ])
        wq, wk, wv = sb("ca_wq", [P, P]), sb("ca_wk", [P, P]), sb("ca_wv", [P, P])
        qT, kT, v = sb("ca_qT", [P, TP]), sb("ca_kT", [P, TP]), sb("ca_v", [P, NJ, P])
        v_scaled = sb("ca_v_scaled", [P, NJ, P])
        prob = sb("ca_prob", [P, NJ, T])
        minus_max, sums, recip = sb("ca_minus_max", [P, NJ]), sb("ca_sums", [P, NJ]), sb("ca_recip", [P, NJ])

        weights_in = sem("ca_weights_in")
        norm = [sem(f"ca_norm_{s}") for s in ("stats", "moments", "rstd", "out")]
        hnT_ps, hnT_ready, proj_ps = sem("ca_hnT_ps"), sem("ca_hnT_ready"), sem("ca_proj_ps")
        q_ready, k_ready, v_ready = sem("ca_q_ready"), sem("ca_k_ready"), sem("ca_v_ready")
        score_ps, max_ready, prob_ready = sem("ca_score_ps"), sem("ca_max_ready"), sem("ca_prob_ready")
        recip_ready, v_scaled_ready = sem("ca_recip_ready"), sem("ca_v_scaled_ready")
        out_ps, h_ready = sem("ca_out_ps"), sem("ca_h_ready")
        flat = psum[:, :, :].rearrange("p k n -> p (k n)")

        def pair(k):
            return flat[:, 2 * k * 512:2 * k * 512 + TP]

        def halves(k, n):
            return psum[:, 2 * k:2 * k + 2, 0:n]

        with nc.Block() as block:
            @block.sync
            def _(sp):
                for dst, src in ((wq, w["wqT"]), (wk, w["wkT"]), (wv, w["wvT"])):
                    sp.dma_start(dst[:, :], src).then_inc(weights_in, 16)

            @block.gpsimd
            def _(pool):
                with pool.Fori(0, B) as b:
                    invert_deviation(pool, moments, rstd, consts, norm, b + 1)

            @block.tensor
            def _(pe):
                def turn(batch):
                    pe.wait_ge(norm[3], batch + 1)
                    for j in range(NJ):
                        ins = pe.transpose(pair(3)[:, j * P:(j + 1) * P], hn[:, j, :], ident)
                    ins.then_inc(hnT_ps, 1)

                def prepare(batch, free):
                    pe.wait_ge(hnT_ready, batch + 1)
                    free(0)
                    for j in range(NJ):
                        ins = pe.matmul(pair(0)[:, j * P:(j + 1) * P], hnT[:, j * P:(j + 1) * P], wv[:, :], start=True, stop=True)
                    ins.then_inc(proj_ps, 1)
                    for r, wt in ((1, wq), (2, wk)):
                        free(r)
                        for h in range(2):
                            ins = pe.matmul(psum[:, 2 * r + h, 0:TP // 2], wt[:, :], hnT[:, h * TP // 2:(h + 1) * TP // 2],
                                            start=True, stop=True)
                        ins.then_inc(proj_ps, 1)

                def attend(b, prepares):
                    pe.wait_ge(q_ready, b + 1)
                    pe.wait_ge(k_ready, b + 1)
                    pe.wait_ge(v_ready, b + 1)
                    for k in range(NJ):
                        if k >= 3:
                            pe.wait_ge(prob_ready, NJ * b + k - 2)
                        for h in range(2):
                            ins = pe.matmul(psum[:, 2 * (k % 3) + h, 0:HALF], kT[:, k * P:(k + 1) * P], qT[:, h * HALF:(h + 1) * HALF],
                                            start=True, stop=True)
                        ins.then_inc(score_ps, 1)
                        if k == 2 and prepares:
                            pe.wait_ge(h_ready, 2 * b + 2)
                            turn(b + 1)
                    if prepares:
                        prepare(b + 1, lambda r: pe.wait_ge(prob_ready, NJ * b + NJ - 2 + r))
                    pe.wait_ge(v_scaled_ready, NJ * b + NJ)
                    pe.wait_ge(h_ready, 2 * b + 2)
                    for j in range(NJ):
                        rows = min(P, T - j * P)
                        for k in range(NJ):
                            ins = pe.matmul(pair(3)[0:rows, j * P:(j + 1) * P], prob[:, k, j * P:j * P + rows], v_scaled[:, k, :],
                                            start=(k == 0), stop=(k == NJ - 1))
                    ins.then_inc(out_ps, 1)

                pe.wait_ge(weights_in, 48)
                turn(0)
                prepare(0, lambda r: None)
                with pe.Fori(0, B - 1) as b:
                    attend(b, True)
                attend(B - 1, False)

            @block.scalar
            def _(act):
                def turned(batch):
                    act.wait_ge(hnT_ps, batch + 1)
                    act.activation(hnT[:, :], pair(3), ACT.Copy).then_inc(hnT_ready, 1)

                def prepare(batch):
                    act.wait_ge(proj_ps, 3 * batch + 2)
                    act.activation(qT[:, :].rearrange("p (h n) -> p h n", h=2), halves(1, TP // 2), ACT.Copy).then_inc(q_ready, 1)

                def attend(b, prepares):
                    act.wait_ge(out_ps, b + 1)
                    for k in range(NJ):
                        act.wait_ge(max_ready, NJ * b + k + 1)
                        act.activation(prob[:, k, :].rearrange("p (h n) -> p h n", h=2), halves(k % 3, HALF),
                                       ACT.Exp, bias=minus_max[:, k:k + 1], accum_out=sums[:, k:k + 1]).then_inc(prob_ready, 1)
                        if k == 3 and prepares:
                            turned(b + 1)
                    if prepares:
                        prepare(b + 1)

                turned(0)
                prepare(0)
                with act.Fori(0, B - 1) as b:
                    attend(b, True)
                attend(B - 1, False)

            @block.vector
            def _(dve):
                def prepare(batch, first=False):
                    dve.wait_ge(proj_ps, 3 * batch + 1)
                    if not first:
                        dve.wait_ge(v_scaled_ready, NJ * batch)
                    dve.tensor_copy(v[:, :, :].rearrange("p j n -> p (j n)"), pair(0)).then_inc(v_ready, 1)
                    dve.wait_ge(proj_ps, 3 * batch + 3)
                    dve.tensor_copy(kT[:, :].rearrange("p (h n) -> p h n", h=2), halves(2, TP // 2)).then_inc(k_ready, 1)

                def normalised(batch):
                    normalise(dve, consts, hidden[:, bass.ds(batch * NJ, NJ), :], hn, stats, moments, rstd, norm, batch + 1)

                def attend(b, prepares, applies):
                    def scale_value(k):
                        dve.wait_ge(prob_ready, NJ * b + k + 1)
                        dve.reciprocal(recip[:, k:k + 1], sums[:, k:k + 1]).then_inc(recip_ready, 1)
                        dve.wait_ge(recip_ready, NJ * b + k + 1)
                        dve.wait_ge(v_ready, b + 1)
                        dve.tensor_scalar(v_scaled[:, k, :], v[:, k, :], recip[:, k:k + 1], None, ALU.mult).then_inc(v_scaled_ready, 1)

                    for k in range(NJ):
                        dve.wait_ge(score_ps, NJ * b + k + 1)
                        dve.tensor_reduce(minus_max[:, k:k + 1], halves(k % 3, HALF), AX.XY, ALU.max,
                                          negate=True).then_inc(max_ready, 1)
                        if k >= 1:
                            scale_value(k - 1)
                    scale_value(NJ - 1)
                    if prepares:
                        prepare(b + 1)
                    if applies:
                        normalised(b + 2)
                    dve.wait_ge(out_ps, b + 2)
                    dve.tensor_tensor(hidden[:, bass.ds(b * NJ, NJ - 1), :], pair(3)[:, 0:(NJ - 1) * P].rearrange("p (j n) -> p j n", n=P),
                                      hidden[:, bass.ds(b * NJ, NJ - 1), :], ALU.add).then_inc(h_ready, 1)
                    dve.tensor_tensor(hidden[0:LAST, bass.ds(b * NJ + NJ - 1, 1), :],
                                      pair(3)[0:LAST, (NJ - 1) * P:TP].rearrange("p (j n) -> p j n", n=P),
                                      hidden[0:LAST, bass.ds(b * NJ + NJ - 1, 1), :], ALU.add).then_inc(h_ready, 1)

                dve.memset(minus_max[:, :], 0.0).then_inc(h_ready, 2)
                dve.memset(recip[:, :], 0.0).then_inc(out_ps, 1)
                normalised(0)
                prepare(0, first=True)
                normalised(1)
                with dve.Fori(0, B - 2) as b:
                    attend(b, True, True)
                attend(B - 2, True, False)
                attend(B - 1, False, False)


def route(nc, w, hidden, ident, consts, psum, hn_all, slot, weight, expert_of, prepare_blocks):
    NT, K = B * NJ, PG1
    SETS = 1 + G1
    N = NT * SETS
    with ExitStack() as ctx:
        def sb(name, shape, n=1, dt=F32):
            t = [ctx.enter_context(nc.sbuf_tensor(f"{name}{u}", shape, dt)) for u in range(n)]
            return t if n > 1 else t[0]

        def sem(name):
            return ctx.enter_context(nc.semaphore(name))

        stats, moments, rstd = sb("ro_stats", [P, NJ, 6], 2), sb("ro_moments", [P, NJ, 2], 2), sb("ro_rstd", [P, NJ], 2)
        hn = sb("ro_hn", [P, NJ, P], 2)
        hnT = sb("ro_hnT", [P, TP], 2)
        wg, bias = sb("ro_wg", [P, SETS * K]), sb("ro_bias", [P, SETS * K])
        prob, first, second, rest = (sb(f"ro_{s}", [P, N, K]) for s in ("prob", "first", "second", "rest"))
        top, total, inv, next_, both, seen, w_first, w_second = (
            sb(f"ro_{s}", [P, N]) for s in ("top", "total", "inv", "next", "both", "seen", "w_first", "w_second"))

        one_hot = sb("ro_one_hot", [P, 4, NT, E1])
        sel, cum = sb("ro_sel", [P, LISTS, NT, E1]), sb("ro_cum", [P, LISTS, NT, E1])
        scan = sb("ro_scan", [P, LISTS, NT, E1], 2)
        within = sb("ro_within", [P, 2, NT, K])
        before, ones = sb("ro_before", [P, P]), sb("ro_ones", [P, P])
        count_i = sb("ro_count_i", [P, LISTS, E1], dt=I32)
        padded, start, ends = sb("ro_padded", [P, LISTS, E1]), sb("ro_start", [P, LISTS, E1], 2), sb("ro_ends", [P, LISTS, E1])
        slot_f = sb("ro_slot_f", [P, 4, NT])
        block_row, expert_f = sb("ro_block_row", [1, LIST_BLOCKS]), sb("ro_expert_f", [1, BLOCKS])

        weights_in = sem("ro_weights_in")
        sel_ready, rank_ps = sem("ro_sel_ready"), sem("ro_rank_ps")
        norm = [[sem(f"ro_norm_{s}{u}") for s in ("stats", "moments", "rstd", "out")] for u in range(2)]
        hnT_ps, hnT_ready, kept = sem("ro_hnT_ps"), sem("ro_hnT_ready"), sem("ro_hn_kept")
        logits_ps, logits_ready, exp_ready, chain = sem("ro_logits_ps"), sem("ro_logits_ready"), sem("ro_exp_ready"), sem("ro_chain")
        shifted = sem("ro_shifted")
        flat = psum[:, :, :].rearrange("p k n -> p (k n)")
        hnT_bank = [flat[:, k * 512:k * 512 + TP] for k in (0, 4)]
        logits_bank = [psum[:, k, 0:NJ * SETS * K] for k in (2, 6)]

        def over(row):
            return row[:, :].rearrange("p (n o) -> p n o", o=1).broadcast_to([P, N, K])

        with nc.Block() as block:
            @block.sync
            def _(sp):
                sp.dma_start(wg[:, :], w["wgate"]).then_inc(weights_in, 16)
                sp.dma_start(bias[:, :], w["bgate"].broadcast_to([P, SETS * K])).then_inc(weights_in, 16)
                sp.dma_start(before[:, :], w["before"]).then_inc(weights_in, 16)
                sp.dma_start(block_row[:, :], w["block_row"]).then_inc(weights_in, 16)
                prepare_blocks(sp)

            @block.gpsimd
            def _(pool):
                with pool.Fori(0, B // 2) as i:
                    for u in range(2):
                        invert_deviation(pool, moments[u], rstd[u], consts, norm[u], i + 1)

            @block.tensor
            def _(pe):
                pe.wait_ge(weights_in, 64)
                with pe.Fori(0, B // 2) as i:
                    for u in range(2):
                        pe.wait_ge(norm[u][3], i + 1)
                        for j in range(NJ):
                            ins = pe.transpose(hnT_bank[u][:, j * P:(j + 1) * P], hn[u][:, j, :], ident)
                        ins.then_inc(hnT_ps, 1)
                    for u in range(2):
                        pe.wait_ge(hnT_ready, 2 * i + u + 1)
                        pe.wait_ge(logits_ready, 2 * i + u + 1)
                        for j in range(NJ):
                            ins = pe.matmul(logits_bank[u][:, j * SETS * K:(j + 1) * SETS * K], hnT[u][:, j * P:(j + 1) * P], wg[:, :],
                                            start=True, stop=True)
                        ins.then_inc(logits_ps, 1)
                pe.wait_ge(sel_ready, 1)
                for k, lhsT in ((0, before), (4, ones)):
                    for a in range(LISTS):
                        sel_cols = sel[:, a, :, :].rearrange("p t e -> p (t e)")
                        for lo in range(0, NT * E1, 512):
                            hi = min(lo + 512, NT * E1)
                            ins = pe.matmul(psum[:, k + 2 * a + lo // 512, 0:hi - lo], lhsT[:, :], sel_cols[:, lo:hi], start=True, stop=True)
                ins.then_inc(rank_ps, 1)

            @block.scalar
            def _(act):
                with act.Fori(0, B // 2) as i:
                    for u in range(2):
                        act.wait_ge(hnT_ps, 2 * i + u + 1)
                        act.activation(hnT[u][:, :], hnT_bank[u], ACT.Copy).then_inc(hnT_ready, 1)
                    for u in range(2):
                        act.activation(hn_all[:, bass.ds((2 * i + u) * NJ, NJ), :], hn[u][:, :, :], ACT.Copy).then_inc(kept, 1)
                act.wait_ge(shifted, 1)
                act.activation(prob[:, :, :], prob[:, :, :], ACT.Exp).then_inc(exp_ready, 1)

            @block.vector
            def _(dve):
                done = 0

                def link(ins):
                    nonlocal done
                    done += 1
                    ins.then_inc(chain, 1)
                    dve.wait_ge(chain, done)

                def choose(values, best, out):
                    link(dve.tensor_tensor(out[:, :, :], values[:, :, :], over(best), ALU.is_equal))
                    link(dve.tensor_tensor(seen[:, :], out[:, :, 0], out[:, :, 1], ALU.max))
                    link(dve.tensor_tensor(out[:, :, 1], out[:, :, 1], out[:, :, 0], ALU.is_gt))
                    link(dve.tensor_tensor(both[:, :], seen[:, :], out[:, :, 2], ALU.max))
                    link(dve.tensor_tensor(out[:, :, 2], out[:, :, 2], seen[:, :], ALU.is_gt))
                    link(dve.tensor_tensor(out[:, :, 3], out[:, :, 3], both[:, :], ALU.is_gt))

                dve.wait_ge(weights_in, 64)
                dve.memset(seen[:, :], 0.0).then_inc(logits_ready, 2)
                dve.memset(both[:, :], 0.0).then_inc(kept, 2)
                with dve.Fori(0, B // 2) as i:
                    here = [hidden[:, bass.ds((2 * i + u) * NJ, NJ), :] for u in range(2)]
                    for u in range(2):
                        find_moments(dve, consts.carrier[:, u:u + 1], here[u], stats[u], moments[u], norm[u], i + 1)
                    for u in range(2):
                        dve.wait_ge(kept, 2 * i + u + 1)
                        scale_tokens(dve, here[u], hn[u], moments[u], rstd[u], norm[u], i + 1)
                    for u in range(2):
                        dve.wait_ge(logits_ps, 2 * i + u + 1)
                        dve.tensor_tensor(prob[:, bass.ds((2 * i + u) * NJ * SETS, NJ * SETS), :].rearrange("p (j s) k -> p j (s k)", s=SETS),
                                          logits_bank[u].rearrange("p (j n) -> p j n", j=NJ),
                                          bias[:, :].rearrange("p (o n) -> p o n", o=1).broadcast_to([P, NJ, SETS * K]),
                                          ALU.add).then_inc(logits_ready, 1)
                dve.wait_ge(logits_ready, B + 2)
                link(dve.tensor_reduce(top[:, :], prob[:, :, :], AX.X, ALU.max))
                dve.tensor_tensor(prob[:, :, :], prob[:, :, :], over(top), ALU.subtract).then_inc(shifted, 1)
                dve.wait_ge(exp_ready, 1)
                link(dve.tensor_reduce(total[:, :], prob[:, :, :], AX.X, ALU.add))
                link(dve.reciprocal(inv[:, :], total[:, :]))
                link(dve.tensor_tensor(prob[:, :, :], prob[:, :, :], over(inv), ALU.mult))
                link(dve.tensor_reduce(top[:, :], prob[:, :, :], AX.X, ALU.max))
                choose(prob, top, first)
                link(dve.scalar_tensor_tensor(out=rest[:, :, :], in0=first[:, :, :], scalar=-2.0, in1=prob[:, :, :],
                                              op0=ALU.mult, op1=ALU.add))
                link(dve.tensor_reduce(next_[:, :], rest[:, :, :], AX.X, ALU.max))
                choose(rest, next_, second)
                link(dve.tensor_tensor(total[:, :], top[:, :], next_[:, :], ALU.add))
                link(dve.scalar_tensor_tensor(out=next_[:, :], in0=total[:, :], scalar=THRESHOLD, in1=next_[:, :],
                                              op0=ALU.is_le, op1=ALU.mult))
                link(dve.tensor_tensor(total[:, :], top[:, :], next_[:, :], ALU.add))
                link(dve.tensor_scalar(total[:, :], total[:, :], 1e-9, None, ALU.add))
                link(dve.reciprocal(inv[:, :], total[:, :]))
                link(dve.tensor_tensor(w_first[:, :], top[:, :], inv[:, :], ALU.mult))
                link(dve.tensor_tensor(w_second[:, :], next_[:, :], inv[:, :], ALU.mult))
                picks = [x[:, :, :].rearrange("p (t s) k -> p t s k", s=SETS) for x in (first, second)]
                shares = [x[:, :].rearrange("p (t s) -> p t s", s=SETS) for x in (w_first, w_second)]
                for a in range(2):
                    for c in range(2):
                        link(dve.tensor_tensor(within[:, c, :, :], picks[a][:, :, 0, :], shares[c][:, :, 1:], ALU.mult))
                        link(dve.tensor_reduce(slot_f[:, 2 * a + c, :], within[:, c, :, :], AX.X, ALU.add))
                        link(dve.scalar_tensor_tensor(out=weight[:, 2 * a + c, :], in0=slot_f[:, 2 * a + c, :], scalar=G1 ** -0.5,
                                                      in1=shares[a][:, :, 0], op0=ALU.mult, op1=ALU.mult))
                        for g in range(G1):
                            ins = dve.tensor_tensor(one_hot[:, 2 * a + c, :, g * K:(g + 1) * K], picks[c][:, :, 1 + g, :],
                                                    picks[a][:, :, 0, g:g + 1].broadcast_to([P, NT, K]), ALU.mult)
                        link(ins)
                dve.memset(ones[:, :], 1.0)
                for a in range(LISTS):
                    ins = dve.tensor_tensor(sel[:, a, :, :], one_hot[:, 2 * a, :, :], one_hot[:, 2 * a + 1, :, :], ALU.add)
                ins.then_inc(sel_ready, 1)
                dve.wait_ge(rank_ps, 1)
                in_tile, of_tile = (psum[:, k:k + 4, :].rearrange("p (a k) n -> p a (k n)", a=LISTS)[:, :, 0:NT * E1]
                                    .rearrange("p a (t e) -> p a t e", e=E1) for k in (0, 4))
                link(dve.tensor_copy(scan[0][:, :, :, :], of_tile))
                step, at = 1, 0
                while step < NT:
                    link(dve.tensor_copy(scan[1 - at][:, :, 0:step, :], scan[at][:, :, 0:step, :]))
                    link(dve.tensor_tensor(scan[1 - at][:, :, step:, :], scan[at][:, :, step:, :], scan[at][:, :, 0:NT - step, :], ALU.add))
                    step, at = 2 * step, 1 - at
                total_of = scan[at][:, :, NT - 1, :]
                link(dve.tensor_tensor(cum[:, :, :, :], scan[at][:, :, :, :], of_tile, ALU.subtract))
                link(dve.tensor_tensor(cum[:, :, :, :], cum[:, :, :, :], in_tile, ALU.add))
                link(dve.tensor_scalar(padded[:, :, :], total_of, float(P - 1), None, ALU.add))
                link(dve.tensor_copy(count_i[:, :, :], padded[:, :, :]))
                link(dve.tensor_scalar(count_i[:, :, :], count_i[:, :, :], -P, None, ALU.bitwise_and))
                link(dve.tensor_copy(padded[:, :, :], count_i[:, :, :]))
                link(dve.tensor_copy(start[0][:, :, :], padded[:, :, :]))
                step, at = 1, 0
                while step < E1:
                    link(dve.tensor_copy(start[1 - at][:, :, 0:step], start[at][:, :, 0:step]))
                    link(dve.tensor_tensor(start[1 - at][:, :, step:], start[at][:, :, step:], start[at][:, :, 0:E1 - step], ALU.add))
                    step, at = 2 * step, 1 - at
                link(dve.tensor_copy(ends[:, :, :], start[at][:, :, :]))
                link(dve.tensor_tensor(start[at][:, :, :], ends[:, :, :], padded[:, :, :], ALU.subtract))
                for a in range(LISTS):
                    ins = dve.scalar_tensor_tensor(out=cum[:, a, :, :], in0=cum[:, a, :, :], scalar=float(a * LIST_BLOCKS * P),
                                                   in1=start[at][:, a:a + 1, :].broadcast_to([P, NT, E1]), op0=ALU.add, op1=ALU.add)
                link(ins)
                for r in range(4):
                    link(dve.tensor_tensor(one_hot[:, r, :, :], one_hot[:, r, :, :], cum[:, r // PER_LIST, :, :], ALU.mult))
                    link(dve.tensor_reduce(slot_f[:, r, :], one_hot[:, r, :, :], AX.X, ALU.add))
                link(dve.tensor_copy(slot[:, :, :], slot_f[:, :, :]))
                link(dve.memset(expert_f[:, :], 0.0))
                for e in range(E1 - 1):
                    for a in range(LISTS):
                        here = expert_f[:, a * LIST_BLOCKS:(a + 1) * LIST_BLOCKS]
                        ins = dve.scalar_tensor_tensor(out=here, in0=block_row[:, :], scalar=ends[0:1, a, e:e + 1],
                                                       in1=here, op0=ALU.is_ge, op1=ALU.add)
                    link(ins)
                link(dve.tensor_copy(expert_of[:, :], expert_f[:, :]))


def grouped_ffn(nc, w, hidden, ident, consts, psum):
    NT, NC = B * NJ, F1 // P
    ZB = 16
    assert BLOCKS % ZB == 0
    with ExitStack() as ctx:
        def sb(name, shape, n=1, dt=F32, stack=ctx):
            t = [stack.enter_context(nc.sbuf_tensor(f"{name}{u}", shape, dt)) for u in range(n)]
            return t if n > 1 else t[0]

        def sem(name):
            return ctx.enter_context(nc.semaphore(name))

        slot, weight = sb("gf_slot", [P, CHOICES, NT], dt=I32), sb("gf_weight", [P, CHOICES, NT])
        expert_of = sb("gf_expert_of", [1, BLOCKS], dt=I32)
        w1, w3 = sb("gf_w1", [P, E1, F1]), sb("gf_w3", [P, E1, F1])
        x_rows = nc.dram_tensor("x_by_slot", (BLOCKS * P, D), F32, kind="Internal").ap()
        y_rows = nc.dram_tensor("y_by_slot", (BLOCKS * P, D), F32, kind="Internal").ap()
        w13_loaded = sem("gf_w13_loaded")
        scattered = [sem(f"gf_scattered{a}") for a in range(LISTS)]
        hn_all = sb("gf_hn_all", [P, NT, P])

        def scatter(pool, a):
            for tile in range(NT):
                for r in range(PER_LIST * a, PER_LIST * (a + 1)):
                    pool.indirect_dma_start(
                        x_rows, bass.IndirectOffsetOnAxis(slot[:, r, tile:tile + 1], 0),
                        hn_all[:, tile, :], None).then_inc(scattered[a], 16)

        with ExitStack() as inner:
            zeros = sb("gf_zeros", [P, ZB * P], stack=inner)
            zero_set, rows_zeroed = sem("gf_zero_set"), sem("gf_rows_zeroed")
            with nc.Block() as block:
                @block.vector
                def _(dve):
                    dve.memset(zeros[:, :], 0.0).then_inc(zero_set, 1)

            def prepare_blocks(sp):
                sp.wait_ge(zero_set, 1)
                for n in range(BLOCKS // ZB):
                    sp.dma_start(x_rows[n * ZB * P:(n + 1) * ZB * P, :].rearrange("(p k) d -> p (k d)", p=P),
                                 zeros[:, :]).then_inc(rows_zeroed, 16)
                sp.dma_start(w1[:, :, :], w["W1"].rearrange("e p f -> p e f")).then_inc(w13_loaded, 16)
                sp.dma_start(w3[:, :, :], w["W3"].rearrange("e p f -> p e f")).then_inc(w13_loaded, 16)

            route(nc, w, hidden, ident, consts, psum, hn_all, slot, weight, expert_of, prepare_blocks)

            with nc.Block() as block:
                @block.gpsimd
                def _(pool):
                    pool.wait_ge(rows_zeroed, 16 * (BLOCKS // ZB))
                    scatter(pool, 0)
                    pool.wait_ge(scattered[0], 16 * PER_LIST * NT)

        with ExitStack() as inner:
            AB = 4
            early, share = sb("gf_early", [P, P], AB, stack=inner), sb("gf_share", [P, P], 2, stack=inner)
            early_in, early_chain = [sem(f"gf_early_in{u}") for u in range(AB)], sem("gf_early_chain")

            def beside_experts(pool, y_stored):
                scatter(pool, 1)
                for stored in y_stored:
                    pool.wait_ge(stored, 16 * (LIST_BLOCKS // len(y_stored) + 1))

                def add(q):
                    tile, r = q // PER_LIST, q % PER_LIST
                    pool.wait_ge(early_in[q % AB], 16 * (q // AB + 1))
                    pool.tensor_tensor(share[q % 2][:, :], early[q % AB][:, :], weight[:, r, tile:tile + 1].broadcast_to([P, P]),
                                       ALU.mult).then_inc(early_chain, 1)
                    pool.wait_ge(early_chain, 2 * q + 1)
                    pool.tensor_tensor(hidden[:, tile, :], hidden[:, tile, :], share[q % 2][:, :], ALU.add).then_inc(early_chain, 1)

                for q in range(PER_LIST * NT):
                    pool.indirect_dma_start(
                        early[q % AB][:, :], None, y_rows[0:LIST_BLOCKS * P, :],
                        bass.IndirectOffsetOnAxis(slot[:, q % PER_LIST, q // PER_LIST:q // PER_LIST + 1], 0)).then_inc(early_in[q % AB], 16)
                    if q >= AB - 1:
                        add(q - AB + 1)
                for q in range(PER_LIST * NT - AB + 1, PER_LIST * NT):
                    add(q)

            expert_blocks(nc, w, ident, psum, expert_of, w1, w3, w13_loaded, x_rows, y_rows, scattered[1],
                          16 * PER_LIST * NT, beside_experts)

        with ExitStack() as inner:
            GB = 4
            rows = sb("gf_rows", [P, PER_LIST, P], GB, stack=inner)
            gathered, added, chain = [sem(f"gf_gathered{u}") for u in range(GB)], sem("gf_added"), sem("gf_chain")
            with nc.Block() as block:
                @block.gpsimd
                def _(pool):
                    for tile in range(NT):
                        if tile >= GB:
                            pool.wait_ge(added, tile - GB + 1)
                        for r in range(PER_LIST):
                            pool.indirect_dma_start(
                                rows[tile % GB][:, r, :], None, y_rows,
                                bass.IndirectOffsetOnAxis(slot[:, PER_LIST + r, tile:tile + 1], 0)).then_inc(gathered[tile % GB], 16)

                @block.vector
                def _(dve):
                    for tile in range(NT):
                        dve.wait_ge(gathered[tile % GB], 16 * PER_LIST * (tile // GB + 1))
                        for r in range(PER_LIST):
                            ins = dve.scalar_tensor_tensor(out=hidden[:, tile, :], in0=rows[tile % GB][:, r, :],
                                                           scalar=weight[:, PER_LIST + r, tile:tile + 1], in1=hidden[:, tile, :],
                                                           op0=ALU.mult, op1=ALU.add)
                            if r < PER_LIST - 1:
                                ins.then_inc(chain, 1)
                                dve.wait_ge(chain, tile * (PER_LIST - 1) + r + 1)
                        ins.then_inc(added, 1)


def expert_blocks(nc, w, ident, psum, expert_of, w1, w3, w13_loaded, x_rows, y_rows, later_rows, later_count,
                  beside_experts):
    NC, LASTB = F1 // P, BLOCKS - 1
    with ExitStack() as ctx:
        def sb(name, shape, n=1, dt=F32):
            t = [ctx.enter_context(nc.sbuf_tensor(f"{name}{u}", shape, dt)) for u in range(n)]
            return t if n > 1 else t[0]

        def sem(name):
            return ctx.enter_context(nc.semaphore(name))

        w2 = sb("eb_w2", [P, E1 * NC, P])
        x_in, xT = sb("eb_x", [P, P], 4), sb("eb_xT", [P, P], 2)
        silu, product, productT = sb("eb_silu", [P, F1], 2), sb("eb_product", [P, F1], 2), sb("eb_productT", [P, F1], 2)
        y = sb("eb_y", [P, P], 4)
        w2_loaded = sem("eb_w2_loaded")
        x_loaded, y_stored = [sem(f"eb_x_loaded{u}") for u in range(4)], [sem(f"eb_y_stored{u}") for u in range(4)]
        xT_ps, xT_ready, up_ps, silu_ready, product_ready, productT_ps, productT_ready, y_ps, y_ready = (
            sem(f"eb_{s}") for s in ("xT_ps", "xT_ready", "up_ps", "silu_ready", "product_ready", "productT_ps",
                                     "productT_ready", "y_ps", "y_ready"))
        x_blocks = x_rows.rearrange("(n p) d -> n p d", p=P)
        y_blocks = y_rows.rearrange("(n p) d -> n p d", p=P)

        def steps(eng, step, before_second=None):
            for n in range(UNROLL):
                step(n, n % 2, 0, n)
            first, second = 1, LIST_BLOCKS // UNROLL - 1
            if before_second:
                with eng.Fori(first, second) as i:
                    for m in range(UNROLL):
                        step(UNROLL * i + m, m % 2, i, m)
                before_second()
                first = second
            with eng.Fori(first, BLOCKS // UNROLL - 1) as i:
                for m in range(UNROLL):
                    step(UNROLL * i + m, m % 2, i, m)
            for n in range(BLOCKS - UNROLL, BLOCKS + 2):
                step(n, n % 2, BLOCKS // UNROLL - 1, n - (BLOCKS - UNROLL))

        def has(n, shift):
            return not isinstance(n, int) or 0 <= n + shift <= LASTB

        with nc.Block() as block:
            @block.sync
            def _(sp):
                for u in range(4):
                    sp.dma_start(x_in[u][:, :], x_blocks[u]).then_inc(x_loaded[u], 16)
                for e in range(E1):
                    sp.dma_start(w2[:, e * NC:(e + 1) * NC, :], w["W2"][e].rearrange("(k p) d -> p k d", p=P)).then_inc(w2_loaded, 16)

                def step(n, u, i, m):
                    if has(n, 4):
                        sp.wait_ge(xT_ps, n + 1)
                        sp.dma_start(x_in[m % 4][:, :], x_blocks[n + 4]).then_inc(x_loaded[m % 4], 16)
                    if has(n, -2):
                        sp.wait_ge(y_ready, n)
                        sp.dma_start(y_blocks[n - 2], y[(m - 2) % 4][:, :]).then_inc(y_stored[(m - 2) % 4], 16)

                steps(sp, step, lambda: sp.wait_ge(later_rows, later_count))
                for stored in y_stored:
                    sp.wait_ge(stored, 16 * (BLOCKS // 4 + 1))

            @block.gpsimd
            def _(pool):
                beside_experts(pool, y_stored)

            @block.tensor
            def _(pe):
                def turn_input(u):
                    ins = pe.transpose(psum[:, 6, 0:P], x_in[u][:, :], ident)
                    ins.then_inc(xT_ps, 1)

                def expert(n):
                    where = slice(n, n + 1) if isinstance(n, int) else bass.ds(n, 1)
                    return pe.value_load(expert_of[0:1, where], min_val=0, max_val=E1 - 1)

                expert_at = {}

                def step(n, u, i, m):
                    if m == 0:
                        for back in range(3):
                            if has(n, -back):
                                expert_at[-back] = expert(n - back)
                    if has(n, 1):
                        pe.wait_ge(x_loaded[(m + 1) % 4], 16 * (UNROLL // 4 * i + (m + 1) // 4 + 1))
                        pe.wait_ge(xT_ready, n + 1)
                        turn_input((m + 1) % 4)
                    if has(n, 0):
                        e = expert_at[m]
                        pe.wait_ge(xT_ready, n + 1)
                        for k, wt in ((u, w1), (2 + u, w3)):
                            ins = pe.matmul(psum[:, k, :], xT[u][:, :], wt[:, bass.ds(e, 1), :], start=True, stop=True)
                        ins.then_inc(up_ps, 1)
                    if has(n, 1) and m + 1 < UNROLL:
                        expert_at[m + 1] = expert(n + 1)
                    if has(n, -1):
                        pe.wait_ge(product_ready, n)
                        for f in range(NC):
                            ins = pe.transpose(psum[:, 4 + (1 - u), f * P:(f + 1) * P], product[1 - u][:, f * P:(f + 1) * P], ident)
                        ins.then_inc(productT_ps, 1)
                    if has(n, -2):
                        if isinstance(n, int) and n == 2:
                            pe.wait_ge(w2_loaded, 16 * E1)
                        e = expert_at[m - 2]
                        pe.wait_ge(productT_ready, n - 1)
                        pe.wait_ge(y_ready, n - 1)
                        for f in range(NC):
                            ins = pe.matmul(psum[:, 7, 0:P], productT[u][:, f * P:(f + 1) * P],
                                            w2[:, bass.ds(e * NC + f, 1), :], start=(f == 0), stop=(f == NC - 1))
                        ins.then_inc(y_ps, 1)

                pe.wait_ge(w13_loaded, 32)
                pe.wait_ge(x_loaded[0], 16)
                turn_input(0)
                steps(pe, step)

            @block.scalar
            def _(act):
                def step(n, u, i, m):
                    if has(n, 0):
                        act.wait_ge(up_ps, n + 1)
                        act.activation(silu[u][:, :], psum[:, u, :], ACT.Silu).then_inc(silu_ready, 1)
                    if has(n, -1):
                        act.wait_ge(productT_ps, n)
                        act.activation(productT[1 - u][:, :], psum[:, 4 + (1 - u), :], ACT.Copy).then_inc(productT_ready, 1)

                steps(act, step)

            @block.vector
            def _(dve):
                for buffer, stored in zip(y, y_stored):
                    dve.memset(buffer[:, :], 0.0).then_inc(stored, 16)
                dve.memset(xT[0][:, 0:1], 0.0).then_inc(y_ready, 1)
                dve.wait_ge(y_ready, 1)
                dve.wait_ge(xT_ps, 1)
                dve.tensor_copy(xT[0][:, :], psum[:, 6, 0:P]).then_inc(xT_ready, 1)

                def step(n, u, i, m):
                    if has(n, 1):
                        dve.wait_ge(xT_ps, n + 2)
                        dve.tensor_copy(xT[1 - u][:, :], psum[:, 6, 0:P]).then_inc(xT_ready, 1)
                    if has(n, 0):
                        dve.wait_ge(silu_ready, n + 1)
                        dve.tensor_tensor(product[u][:, :], silu[u][:, :], psum[:, 2 + u, :], ALU.mult).then_inc(product_ready, 1)
                    if has(n, -2):
                        dve.wait_ge(y_ps, n - 1)
                        dve.wait_ge(y_stored[(m - 2) % 4], 16 * (UNROLL // 4 * i + (m - 2) // 4 + 1))
                        dve.tensor_copy(y[(m - 2) % 4][:, :], psum[:, 7, 0:P]).then_inc(y_ready, 1)

                steps(dve, step)


def store(nc, hidden, out):
    with nc.semaphore("st_stored") as stored, nc.Block() as block:
        @block.sync
        def _(sp):
            for b in range(B):
                whole, rest = batch_rows(out, b)
                sp.dma_start(whole, hidden[:, b * NJ:(b + 1) * NJ - 1, :]).then_inc(stored, 16)
                sp.dma_start(rest, hidden[0:LAST, (b + 1) * NJ - 1, :]).then_inc(stored, 16)
            sp.wait_ge(stored, 32 * B)


class Consts:
    pass


def audio_tower(nc, a, out):
    with ExitStack() as ctx:
        hidden = ctx.enter_context(nc.sbuf_tensor("hidden", [P, B * NJ, P], F32))
        ident_sb = ctx.enter_context(nc.sbuf_tensor("ident", [P, P], F32))
        psum = ctx.enter_context(nc.psum_tensor("psum", [P, 8, 512], F32))
        consts = Consts()
        consts.minus_half = ctx.enter_context(nc.sbuf_tensor("minus_half", [P, 16], F32))
        consts.eps = ctx.enter_context(nc.sbuf_tensor("eps", [P, 16], F32))
        consts.carrier = ctx.enter_context(nc.sbuf_tensor("wait_carrier", [P, 8], F32))
        consts.loaded = ctx.enter_context(nc.semaphore("ident_loaded"))
        ident = ident_sb[:, :]
        with nc.Block() as block:
            @block.sync
            def _(sp):
                sp.dma_start(ident, a["ident"]).then_inc(consts.loaded, 16)
                sp.wait_ge(consts.loaded, 16)

            @block.gpsimd
            def _(pool):
                pool.memset(consts.minus_half[:, :], -0.5)
                pool.memset(consts.eps[:, :], EPS)
        token_mixer(nc, a["x"], a, hidden, ident, consts, psum)
        rope_attention(nc, a, hidden, ident, consts, psum)
        routed_ffn(nc, a, hidden, ident, consts, psum)
        column_attention(nc, a, hidden, ident, consts, psum)
        grouped_ffn(nc, a, hidden, ident, consts, psum)
        store(nc, hidden, out)


def rope_tables():
    cos, sin = np.zeros((P, 3, TP), np.float32), np.zeros((P, 3, TP), np.float32)
    for s in range(3):
        width = D if s < 2 else GROUPS * HD
        i = np.arange(width // 2, dtype=np.float64)
        theta = 10000.0 ** (-(2.0 * (i - 1.0))) / width
        angle = np.arange(T, dtype=np.float64)[:, None] * theta[None, :]
        for g in range(GROUPS):
            for h in range(HD):
                c = (2 * g + s) * HD + h if s < 2 else g * HD + h
                cos[32 * g + h, s, 0:T] = np.cos(angle[:, c // 2]).astype(np.float32)
                sin[32 * g + h, s, 0:T] = np.sin(angle[:, c // 2]).astype(np.float32) * (1 if c % 2 == 0 else -1)
    return cos, sin


def kernel(**inputs):
    import concourse.bacc as bacc
    from concourse.bass_utils import run_bass_kernel_spmd

    g = {k: np.asarray(v) for k, v in inputs.items()}
    t0 = "L0_tok_"
    wqk = np.zeros((P, 3, 2, P), g["L0_attn_Wq"].dtype)
    for s in range(3):
        for grp in range(GROUPS):
            for h in range(HD):
                weight = g["L0_attn_Wq"] if s < 2 else g["L0_attn_Wk"]
                c = (2 * grp + s) * HD + h if s < 2 else grp * HD + h
                wqk[:, s, 0, 32 * grp + h] = weight[:, c]
                wqk[:, s, 1, 32 * grp + h] = weight[:, c ^ 1]
    wv = np.zeros((P, P), g["L0_attn_Wv"].dtype)
    for grp in range(GROUPS):
        wv[:, 32 * grp:32 * grp + HD] = g["L0_attn_Wv"][:, grp * HD:(grp + 1) * HD]
    cos, sin = rope_tables()
    mask = np.zeros((P, TP), np.float32)
    mask[:, TP - P:] = np.where(np.arange(P)[None, :] > np.arange(P)[:, None], MASKED, 0.0)
    arrays = {
        "x": g["x"],
        "ident": np.eye(P, dtype=np.float32),
        "wcT": g[t0 + "w_compress"][:, :, 0].T, "bc": g[t0 + "b_compress"][:, None],
        "wmT": g[t0 + "w_main"].transpose(2, 1, 0), "bm": g[t0 + "b_main"][:, None],
        "weT": np.concatenate([g[t0 + "w_expand"][:, :, 0].T, g[t0 + "b_expand"][None, :]]),
        "wf1T": g[t0 + "w_ff1"].T, "bf1": g[t0 + "b_ff1"][:, None],
        "wf2T": np.concatenate([g[t0 + "w_ff2"].T, g[t0 + "b_ff2"][None, :]]),
        "norms": np.stack([g[t0 + "g_conv_norm"], g[t0 + "b_conv_norm"], g[t0 + "g_ff_norm"], g[t0 + "b_ff_norm"]], axis=1),
        "wqk": wqk, "wv0": wv, "cos": cos, "sin": sin, "mask": mask,
        "ew0": g["L0_ffn_expert_weights"], "ei0": g["L0_ffn_expert_indices"],
        "w1": g["L0_ffn_w1"], "w2": g["L0_ffn_w2"],
        "wqT": g["L1_attn_Wq"].T, "wkT": g["L1_attn_Wk"].T, "wvT": g["L1_attn_Wv"].T,
        "wgate": np.concatenate([g["L1_ffn_Wr"], g["L1_ffn_Wgate"].transpose(1, 0, 2).reshape(D, E1)], axis=1),
        "bgate": np.concatenate([g["L1_ffn_br"], g["L1_ffn_bgate"].reshape(E1)])[None, :],
        "before": np.triu(np.ones((P, P), np.float32), 1), "block_row": np.arange(LIST_BLOCKS, dtype=np.float32)[None, :] * P,
        "W1": g["L1_ffn_W1"], "W3": g["L1_ffn_W3"], "W2": g["L1_ffn_W2"],
    }
    arrays = {k: np.ascontiguousarray(v) for k, v in arrays.items()}
    nc = bacc.Bacc("TRN2", target_bir_lowering=False, num_devices=1)
    aps = {k: nc.dram_tensor(f"in_{k}", v.shape, mybir.dt.from_np(v.dtype), kind="ExternalInput").ap()
           for k, v in arrays.items()}
    out = nc.dram_tensor("out", (B, T, D), F32, kind="ExternalOutput").ap()
    audio_tower(nc, aps, out)
    r = run_bass_kernel_spmd(nc, [{f"in_{k}": v for k, v in arrays.items()}], core_ids=[0])
    return r.results[0]["out"]
```
